# Optimizing a Trainium2 kernel written in Bass

```python
import numpy as np
import jax
import jax.numpy as jnp

def _softmax(x, axis=-1):
    return jax.nn.softmax(x, axis=axis)

def _gelu(x):
    return jax.nn.gelu(x, approximate=True)

def _silu(x):
    return jax.nn.silu(x)

def _sigmoid(x):
    return jax.nn.sigmoid(x)

def _layernorm(x, axis=-1, eps=1e-05):
    m = jnp.mean(x, axis=axis, keepdims=True)
    v = jnp.var(x, axis=axis, keepdims=True)
    return (x - m) / jnp.sqrt(v + eps)

def _scatter_add(tgt, idx, src, axis=0):
    return tgt.at[idx].add(src)

def _segment_sum(src, seg, n):
    return jax.ops.segment_sum(src, seg, n)
kernel_name = 'mk_decoder_postln_d1_seqx_r4_e23420'

def setup_inputs(seed: int=0):
    np.random.seed(seed)
    _w = jnp.asarray

    def _rec_inputs():
        import jax
        import jax.numpy as jnp
        _rk = jax.random.key(seed)
        x = -0.0002928 + 1 * jax.random.normal(jax.random.fold_in(_rk, 1), (4, 1024, 256), jnp.float32)
        _lenS = 1024 - jax.random.randint(jax.random.fold_in(_rk, 7), (4,), 0, max(1, 1024 // 4) + 1, jnp.int32)
        _lenS2 = 154 - jax.random.randint(jax.random.fold_in(_rk, 8), (4,), 0, max(1, 154 // 4) + 1, jnp.int32)
        _ctx_1024P = jax.random.normal(jax.random.fold_in(_rk, 11), (4, 16, 256), jnp.float32)
        _ctx_1024c = jax.random.dirichlet(jax.random.fold_in(_rk, 511), 0.3 * jnp.ones((16,), jnp.float32), (4, 154))
        _ctx_1024t = jnp.einsum('bsk,bkd->bsd', _ctx_1024c, _ctx_1024P)
        _ctx_1024t = _ctx_1024t * jax.lax.rsqrt(jnp.mean(jnp.square(_ctx_1024t)) + 1e-12) * 0.953939
        ctx_1024 = -1.39393e-06 + 0.999914 * (_ctx_1024t + 0.3 * jax.random.normal(jax.random.fold_in(_rk, 611), (4, 154, 256), jnp.float32))
        _validS = jnp.arange(1024)[None, :] < _lenS[:, None]
        _validS2 = jnp.arange(154)[None, :] < _lenS2[:, None]
        _causal = jnp.tril(jnp.ones((1024, 1024), dtype=bool))
        mask_BxSxS2_if1 = jnp.where(jnp.ones((4, 1024, 154), dtype=bool), 1, 0).astype(jnp.int32)
        return (x, ctx_1024, mask_BxSxS2_if1)
    x, ctx_1024, mask_BxSxS2_if1 = _rec_inputs()

    def _L0_attn_setup():
        import jax, jax.numpy as jnp
        import numpy as np
        NUM_HEAD = 16
        D_Q = 128
        D_KV = 128
        ROPE_BASE = 10000.0

        def _cos_sin(seq_len, dim):
            pos = jnp.arange(seq_len, dtype=jnp.float32)[:, None]
            ids = jnp.arange(dim // 2, dtype=jnp.float32)
            theta = ROPE_BASE ** (-2.0 * ids) / (dim // 2)
            r = pos * theta[None, :]
            return (jnp.cos(r), jnp.sin(r))

        def _rope(x, cos, sin):
            b, s, d = x.shape
            xv = x.reshape(b, s, d // 2, 2)
            x0, x1 = (xv[..., 0], xv[..., 1])
            out = jnp.stack([x0 * cos - x1 * sin, x1 * cos + x0 * sin], axis=-1)
            return out.reshape(b, s, d)
        key = jax.random.key(seed)
        ks = jax.random.split(key, 10)
        d_model, d_q, d_kv = (256, D_Q, D_KV)
        b, s = (2, 512)
        w = lambda k, i, o: jax.random.normal(k, (i, o), dtype=jnp.float32) * 0.02
        return {'x': jax.random.normal(ks[0], (b, s, d_model), dtype=jnp.float32), 'Wd_q_w': w(ks[1], d_model, d_q), 'Wd_q_b': jnp.zeros((d_q,), jnp.float32), 'Wu_q_w': w(ks[2], d_q, d_model), 'Wu_q_b': jnp.zeros((d_model,), jnp.float32), 'Wq_r_w': w(ks[3], d_q, d_model), 'Wq_r_b': jnp.zeros((d_model,), jnp.float32), 'Wk_r_w': w(ks[4], d_model, d_model), 'Wk_r_b': jnp.zeros((d_model,), jnp.float32), 'Wd_kv_w': w(ks[5], d_model, d_kv), 'Wd_kv_b': jnp.zeros((d_kv,), jnp.float32), 'Wu_k_w': w(ks[6], d_kv, d_model), 'Wu_k_b': jnp.zeros((d_model,), jnp.float32), 'Wu_v_w': w(ks[7], d_kv, d_model), 'Wu_v_b': jnp.zeros((d_model,), jnp.float32), 'Wo_w': w(ks[8], d_model, d_model), 'Wo_b': jnp.zeros((d_model,), jnp.float32)}
    _L0_attn_all = _L0_attn_setup()
    _L0_attn_in = {k: v for k, v in _L0_attn_all.items() if k in ('Wd_q_w', 'Wd_q_b', 'Wu_q_w', 'Wu_q_b', 'Wq_r_w', 'Wq_r_b', 'Wk_r_w', 'Wk_r_b', 'Wd_kv_w', 'Wd_kv_b', 'Wu_k_w', 'Wu_k_b', 'Wu_v_w', 'Wu_v_b', 'Wo_w', 'Wo_b')}
    del _L0_attn_all

    def _L0_xattn_setup():
        import jax, jax.numpy as jnp
        import numpy as np
        HEAD_NUM = 16
        D_MODEL = 256
        NEG = -1000000000.0
        key = jax.random.key(seed)
        ks = jax.random.split(key, 12)
        B, S, D = (2, 512, D_MODEL)
        inp = {'query': jax.random.normal(ks[0], (B, S, D), jnp.float32), 'key': jax.random.normal(ks[1], (B, S, D), jnp.float32), 'value': jax.random.normal(ks[2], (B, S, D), jnp.float32), 'mask': jnp.ones((B, S, S), jnp.int32)}
        scale = 1.0 / np.sqrt(D)
        for i in range(4):
            inp[f'W{i}'] = jax.random.normal(ks[3 + i], (D, D), jnp.float32) * scale
            inp[f'b{i}'] = jnp.zeros((D,), jnp.float32)
        return inp
    _L0_xattn_all = _L0_xattn_setup()
    _L0_xattn_in = {k: v for k, v in _L0_xattn_all.items() if k in ('W0', 'b0', 'W1', 'b1', 'W2', 'b2', 'W3', 'b3')}
    del _L0_xattn_all

    def _L0_ffn_setup():
        import jax, jax.numpy as jnp
        import numpy as np
        N_EXPERT_CAPACITY = 2
        key = jax.random.key(seed)
        k1, k2, k3, k4 = jax.random.split(key, 4)
        B, S, D, E, F = (8, 256, 256, 8, 512)
        x = jax.random.normal(k1, (B, S, D), dtype=jnp.float32)
        choice_w = jax.random.uniform(k2, (E, D), dtype=jnp.float32, minval=-1.0, maxval=1.0) * (1.0 / np.sqrt(D))
        w1 = jax.random.uniform(k3, (E, D, F), dtype=jnp.float32, minval=-1.0, maxval=1.0) * (1.0 / np.sqrt(D))
        w2 = jax.random.uniform(k4, (E, F, D), dtype=jnp.float32, minval=-1.0, maxval=1.0) * (1.0 / np.sqrt(F))
        return {'x': x, 'choice_w': choice_w, 'w1': w1, 'w2': w2}
    _L0_ffn_all = _L0_ffn_setup()
    _L0_ffn_in = {k: v for k, v in _L0_ffn_all.items() if k in ('choice_w', 'w1', 'w2')}
    del _L0_ffn_all
    return {'x': x, 'ctx_1024': ctx_1024, 'mask_BxSxS2_if1': mask_BxSxS2_if1, 'L0_attn_Wd_q_w': _L0_attn_in['Wd_q_w'], 'L0_attn_Wd_q_b': _L0_attn_in['Wd_q_b'], 'L0_attn_Wu_q_w': _L0_attn_in['Wu_q_w'], 'L0_attn_Wu_q_b': _L0_attn_in['Wu_q_b'], 'L0_attn_Wq_r_w': _L0_attn_in['Wq_r_w'], 'L0_attn_Wq_r_b': _L0_attn_in['Wq_r_b'], 'L0_attn_Wk_r_w': _L0_attn_in['Wk_r_w'], 'L0_attn_Wk_r_b': _L0_attn_in['Wk_r_b'], 'L0_attn_Wd_kv_w': _L0_attn_in['Wd_kv_w'], 'L0_attn_Wd_kv_b': _L0_attn_in['Wd_kv_b'], 'L0_attn_Wu_k_w': _L0_attn_in['Wu_k_w'], 'L0_attn_Wu_k_b': _L0_attn_in['Wu_k_b'], 'L0_attn_Wu_v_w': _L0_attn_in['Wu_v_w'], 'L0_attn_Wu_v_b': _L0_attn_in['Wu_v_b'], 'L0_attn_Wo_w': _L0_attn_in['Wo_w'], 'L0_attn_Wo_b': _L0_attn_in['Wo_b'], 'L0_xattn_W0': _L0_xattn_in['W0'], 'L0_xattn_b0': _L0_xattn_in['b0'], 'L0_xattn_W1': _L0_xattn_in['W1'], 'L0_xattn_b1': _L0_xattn_in['b1'], 'L0_xattn_W2': _L0_xattn_in['W2'], 'L0_xattn_b2': _L0_xattn_in['b2'], 'L0_xattn_W3': _L0_xattn_in['W3'], 'L0_xattn_b3': _L0_xattn_in['b3'], 'L0_ffn_choice_w': _L0_ffn_in['choice_w'], 'L0_ffn_w1': _L0_ffn_in['w1'], 'L0_ffn_w2': _L0_ffn_in['w2']}

def reference(x, ctx_1024, mask_BxSxS2_if1, L0_attn_Wd_q_w, L0_attn_Wd_q_b, L0_attn_Wu_q_w, L0_attn_Wu_q_b, L0_attn_Wq_r_w, L0_attn_Wq_r_b, L0_attn_Wk_r_w, L0_attn_Wk_r_b, L0_attn_Wd_kv_w, L0_attn_Wd_kv_b, L0_attn_Wu_k_w, L0_attn_Wu_k_b, L0_attn_Wu_v_w, L0_attn_Wu_v_b, L0_attn_Wo_w, L0_attn_Wo_b, L0_xattn_W0, L0_xattn_b0, L0_xattn_W1, L0_xattn_b1, L0_xattn_W2, L0_xattn_b2, L0_xattn_W3, L0_xattn_b3, L0_ffn_choice_w, L0_ffn_w1, L0_ffn_w2):
    import jax
    import jax.numpy as jnp

    def _L0_attn_ref(x, Wd_q_w, Wd_q_b, Wu_q_w, Wu_q_b, Wq_r_w, Wq_r_b, Wk_r_w, Wk_r_b, Wd_kv_w, Wd_kv_b, Wu_k_w, Wu_k_b, Wu_v_w, Wu_v_b, Wo_w, Wo_b):
        import jax, jax.numpy as jnp
        import numpy as np
        NUM_HEAD = 16
        D_Q = 128
        D_KV = 128
        ROPE_BASE = 10000.0

        def _cos_sin(seq_len, dim):
            pos = jnp.arange(seq_len, dtype=jnp.float32)[:, None]
            ids = jnp.arange(dim // 2, dtype=jnp.float32)
            theta = ROPE_BASE ** (-2.0 * ids) / (dim // 2)
            r = pos * theta[None, :]
            return (jnp.cos(r), jnp.sin(r))

        def _rope(x, cos, sin):
            b, s, d = x.shape
            xv = x.reshape(b, s, d // 2, 2)
            x0, x1 = (xv[..., 0], xv[..., 1])
            out = jnp.stack([x0 * cos - x1 * sin, x1 * cos + x0 * sin], axis=-1)
            return out.reshape(b, s, d)
        b, s, d_model = x.shape
        h = NUM_HEAD
        hd = d_model // h
        scale = jnp.sqrt(jnp.float32(h + D_KV + D_Q))

        def heads(t):
            return t.reshape(b, s, h, hd).transpose(0, 2, 1, 3)
        cos, sin = _cos_sin(s, d_model)
        ct_q = x @ Wd_q_w + Wd_q_b
        qt_c = heads(ct_q @ Wu_q_w + Wu_q_b)
        qt_r = heads(_rope(ct_q @ Wq_r_w + Wq_r_b, cos, sin))
        query = qt_c + qt_r
        ct_kv = x @ Wd_kv_w + Wd_kv_b
        kt_c = heads(ct_kv @ Wu_k_w + Wu_k_b)
        kt_r = heads(_rope(x @ Wk_r_w + Wk_r_b, cos, sin))
        key = kt_c + kt_r
        value = heads(ct_kv @ Wu_v_w + Wu_v_b)
        attn = jnp.einsum('bhqd,bhkd->bhqk', query, key) / scale
        attn = jax.nn.softmax(attn, axis=-1)
        out = jnp.einsum('bhqk,bhkd->bhqd', attn, value)
        out = out.transpose(0, 2, 1, 3).reshape(b, s, d_model)
        return out @ Wo_w + Wo_b

    def _L0_xattn_ref(query, key, value, mask, W0, b0, W1, b1, W2, b2, W3, b3):
        import jax, jax.numpy as jnp
        import numpy as np
        HEAD_NUM = 16
        D_MODEL = 256
        NEG = -1000000000.0
        B, Sq, D = query.shape
        Sk = key.shape[1]
        H, dk = (HEAD_NUM, D // HEAD_NUM)
        q = (query @ W0.T + b0).reshape(B, Sq, H, dk).transpose(0, 2, 1, 3)
        k = (key @ W1.T + b1).reshape(B, Sk, H, dk).transpose(0, 2, 1, 3)
        v = (value @ W2.T + b2).reshape(B, Sk, H, dk).transpose(0, 2, 1, 3)
        scores = jnp.einsum('bhqd,bhkd->bhqk', q, k) / jnp.sqrt(jnp.float32(dk))
        scores = jnp.where(mask[:, None, :, :] == 0, NEG, scores)
        p_attn = jax.nn.softmax(scores, axis=-1)
        x = jnp.einsum('bhqk,bhkd->bhqd', p_attn, v)
        x = x.transpose(0, 2, 1, 3).reshape(B, Sq, D)
        return x @ W3.T + b3

    def _L0_ffn_ref(x, choice_w, w1, w2):
        import jax, jax.numpy as jnp
        import numpy as np
        N_EXPERT_CAPACITY = 2
        B, S, D = x.shape
        E = choice_w.shape[0]
        k = S * N_EXPERT_CAPACITY // E
        probs = jax.nn.softmax(jnp.einsum('bsd,ed->bse', x, choice_w), axis=-1)
        G, I = jax.lax.top_k(jnp.swapaxes(probs, -1, -2), k)
        x_in = jnp.take_along_axis(x[:, None, :, :], I[..., None], axis=2)
        h = jax.nn.silu(jnp.einsum('bekd,edf->bekf', x_in, w1))
        x_mlp = jnp.einsum('bekf,efd->bekd', h, w2)
        b_idx = jnp.arange(B)[:, None, None]
        out = jnp.zeros_like(x).at[b_idx, I].add(G[..., None] * x_mlp)
        return out
    x = _layernorm(x + _L0_attn_ref(x, L0_attn_Wd_q_w, L0_attn_Wd_q_b, L0_attn_Wu_q_w, L0_attn_Wu_q_b, L0_attn_Wq_r_w, L0_attn_Wq_r_b, L0_attn_Wk_r_w, L0_attn_Wk_r_b, L0_attn_Wd_kv_w, L0_attn_Wd_kv_b, L0_attn_Wu_k_w, L0_attn_Wu_k_b, L0_attn_Wu_v_w, L0_attn_Wu_v_b, L0_attn_Wo_w, L0_attn_Wo_b), axis=-1)
    x = _layernorm(x + _L0_xattn_ref(x, ctx_1024, ctx_1024, mask_BxSxS2_if1, L0_xattn_W0, L0_xattn_b0, L0_xattn_W1, L0_xattn_b1, L0_xattn_W2, L0_xattn_b2, L0_xattn_W3, L0_xattn_b3), axis=-1)
    x = _layernorm(x + _L0_ffn_ref(x, L0_ffn_choice_w, L0_ffn_w1, L0_ffn_w2), axis=-1)
    return x

_drawn_inputs = setup_inputs


def setup_inputs(seed=0):
    import zlib

    import numpy as np

    out = dict(_drawn_inputs(seed))
    spreads = {'L0_attn_Wd_q_b': (0.0, 0.8),
     'L0_attn_Wu_q_b': (0.0, 0.8),
     'L0_attn_Wq_r_b': (0.0, 0.8),
     'L0_attn_Wk_r_b': (0.0, 2.0),
     'L0_attn_Wd_kv_b': (0.0, 0.8),
     'L0_attn_Wu_k_b': (0.0, 2.0),
     'L0_attn_Wu_v_b': (0.0, 0.281),
     'L0_attn_Wo_b': (0.0, 0.1),
     'L0_xattn_b0': (0.0, 0.381),
     'L0_xattn_b1': (0.0, 2.0),
     'L0_xattn_b2': (0.0, 0.1),
     'L0_xattn_b3': (0.0, 0.1)}
    factors = {'L0_attn_Wd_q_w': 8.0,
     'L0_attn_Wu_q_w': 8.0,
     'L0_attn_Wq_r_w': 8.0,
     'L0_attn_Wk_r_w': 8.0,
     'L0_attn_Wd_kv_w': 8.0,
     'L0_attn_Wu_k_w': 8.0,
     'L0_attn_Wu_v_w': 8.0}
    for name, (base, spread) in spreads.items():
        noise = np.random.default_rng([zlib.crc32(name.encode()), seed]).standard_normal(out[name].shape)
        drawn = base * np.exp(spread * noise) if base else spread * noise
        out[name] = jnp.asarray(drawn.astype(out[name].dtype))
    for name, factor in factors.items():
        out[name] = (out[name] * factor).astype(out[name].dtype)
    return out
```

```python
from contextlib import ExitStack

import numpy as np

import concourse.bass as bass
from concourse import mybir

F32 = mybir.dt.float32
BF16 = mybir.dt.bfloat16
I32 = mybir.dt.int32
U32 = mybir.dt.uint32
ALU = mybir.AluOpType
ACT = mybir.ActivationFunctionType
AX = mybir.AxisListType

P = 128
B, S, D = 4, 1024, 256
H = 16
HD = D // H
SK = 154
SKR = SK - P
T = S // P
C = D // P
N = 512
HALVES = S // N
LAT = 128
E, F = 8, 512
CAP = S * 2 // E
EPS = 1e-5
TERMS = [(0, 0), (0, 1), (0, 2), (1, 0), (1, 1), (2, 0)]
KQ = HD * len(TERMS)
KM = KQ + 3
MASKED = -float(2 ** 120)
SCALE_SELF = float(1.0 / np.sqrt(np.float32(H + LAT + LAT)))
SCALE_CROSS = float(1.0 / np.sqrt(np.float32(HD)))
G = 4
NG = H // G
V32 = 32

FRONT = ([("xT", "DA"[n % 2]) for n in range(4)] + [("ctxT", "D")] + [("ctq", "A")] * 2 + [("ctkv", "A")] * 2
         + [("q", "D")] * 12 + [("k", "D")] * 12 + [("v", "D")] * 4 + [("kx", "D"), ("vx", "D"), ("vxr", "D")])
MID = ([("o", "D")] * T + [("oT", "DA"[n % 2]) for n in range(4)] + [("y", "D")] * 4
       + [("x1T", "DA"[n % 2]) for n in range(4)] + [("qx", "D")] * 4)
BACK = ([("ox", "D")] * T + [("oxT", "DA"[n % 2]) for n in range(4)] + [("yx", "D")] * 4
        + [("x2T", "DA"[n % 2]) for n in range(4)] + [("logit", "D")])
ITEMS = FRONT + MID + BACK
STAGE = {**{i: 0 for i in range(len(FRONT))}, **{len(FRONT) + i: len(FRONT) for i in range(len(MID))},
         **{len(FRONT) + len(MID) + i: len(FRONT) + len(MID) for i in range(len(BACK))}}
NI = len(ITEMS)


def first(name):
    return [n for n, _ in ITEMS].index(name)


def taken(engine, upto):
    return sum(e == engine for _, e in ITEMS[:upto])


PIECE = ([first("q") + 3 * i + 2 for i in range(4)] + [first("k") + 3 * i + 2 for i in range(4)] + [first("kx")]
         + [first("qx") + i for i in range(4)])
NA, ND = taken("A", NI), taken("D", NI)
PIECES = 13
PIECES_OF = [7, 6]
SM_SELF, SM_CROSS = H * T * HALVES, H * 3
ST_SELF, ST_CROSS = NG * HALVES * T * G, NG * HALVES * (G + 1)
LAG = 2


def schedule(sm_group, st_group, lead, turn):
    order = []
    total = NG * st_group + sm_group + lead
    for k in range(total + LAG):
        if k < NG * sm_group:
            order.append(("smax", k))
        if k >= sm_group + turn and (k - turn) % sm_group == 0 and (k - turn) // sm_group <= NG:
            order.append(("turn", (k - turn) // sm_group - 1))
        st = k - sm_group - lead
        if 0 <= st < NG * st_group:
            order.append(("st", st))
        if 0 <= st - LAG < NG * st_group:
            order.append(("av", st - LAG))
    return order


TURN_SELF, TURN_CROSS = 6, 4
START = 1
COPIED = 16
BITS = 30
COLS = 5
UNITS = 2 * B
ORDER_SELF = schedule(SM_SELF // NG, ST_SELF // NG, 14, TURN_SELF)
ORDER_CROSS = schedule(SM_CROSS // NG, ST_CROSS // NG, 18, TURN_CROSS)
SM_ALL, ST_ALL = SM_SELF + SM_CROSS, ST_SELF + ST_CROSS


def decoder_block(nc, a, out):
    ctx = ExitStack()
    with ctx:
        def sb(name, shape, dt=F32):
            return ctx.enter_context(nc.sbuf_tensor(name, shape, dt))

        def sem(name):
            return ctx.enter_context(nc.semaphore(name))

        def dram(name, shape, dt):
            return nc.dram_tensor(name, shape, dt, kind="Internal").ap()

        PS = ctx.enter_context(nc.psum_tensor("banks", [P, 8, N], F32))

        q_parts = dram("q_parts", (3, D, S), BF16)
        k_parts = dram("k_parts", (3, D, S), BF16)
        kx_parts = dram("kx_parts", (P, 3, C, SK), BF16)
        x2_rows = dram("x2_rows", (B * S, D), F32)
        acc_rows = dram("acc_rows", (B * S, D), F32)

        ident = sb("ident", [P, P])
        identb = sb("identb", [P, P], BF16)
        tri = sb("tri", [P, P], BF16)
        onesb = sb("onesb", [P, P], BF16)
        iota = sb("iota", [P, CAP], BF16)
        cosT = sb("cosT", [P, C, S])
        sinT = sb("sinT", [P, C, S])
        wdq = sb("wdq", [P, C, LAT])
        wdkv = sb("wdkv", [P, C, LAT])
        wuq = sb("wuq", [P, D])
        wqr = sb("wqr", [P, D])
        wqrs = sb("wqrs", [P, D])
        wuk = sb("wuk", [P, D])
        wuv = sb("wuv", [P, D])
        wkr = sb("wkr", [P, C, D])
        wkrs = sb("wkrs", [P, C, D])
        wo = sb("wo", [P, C, D])
        w0 = sb("w0", [P, C, D])
        w1x = sb("w1x", [P, C, D])
        w2x = sb("w2x", [P, C, D])
        w3 = sb("w3", [P, C, D])
        wch = sb("wch", [P, C, E])
        bcol = sb("bcol", [P, 18])
        brow = sb("brow", [P, 4, D])
        mhalf = sb("mhalf", [P, T])
        oT = sb("oT", [P, NG, S])
        early = oT[:, :, :].rearrange("p g n -> p (g n)")
        x = early[:, 0:T * D].rearrange("p (t d) -> p t d", d=D)
        cx = early[:, T * D:(T + 2) * D].rearrange("p (t d) -> p t d", d=D)
        mask_i = early[:, (T + 2) * D:(T + 2) * D + T * SK].bitcast(I32).rearrange("p (t k) -> p t k", k=SK)
        xT = sb("xT", [P, C, S])
        cxT = sb("cxT", [P, C, SK])
        maskb = sb("maskb", [P, T, 160], BF16)
        pT = sb("pT", [P, 4, N])
        ctq = pT[:, 0:2, :].rearrange("p a n -> p (a n)")
        ctkv = pT[:, 2:4, :].rearrange("p a n -> p (a n)")
        z = sb("z", [P, T, D])
        rotary = z[:, :, :].rearrange("p (a r t) d -> p a r (t d)", a=2, r=2)
        ru, rv = rotary[:, 0], rotary[:, 1]
        iota_f = z[:, 0, :]
        full = sb("full", [P, 2, N])
        rest = sb("rest", [P, 2, N])
        part = sb("part", [P, 2, 3, N], BF16)
        qst = sb("qst", [P, H, S], BF16)
        kst = sb("kst", [P, H, S], BF16)
        kxst = sb("kxst", [P, H, 160], BF16)
        V = sb("V", [P, T, H, V32])
        Vx = sb("Vx", [P, H, V32])
        Vr = sb("Vr", [P, NG, V32])
        mh = sb("mh", [P, 2, T, G, HALVES])
        nmf = sb("nmf", [P, T, G])
        nmr = sb("nmr", [P, T, G])
        nmp = sb("nmp", [P, 2, T, 3 * G], BF16)
        nmT = sb("nmT", [3 * G, 2, S], BF16)
        rz = sb("rz", [P, 2, H])
        xb = sb("xb", [P, T, D])
        st6 = sb("st6", [P, T, 6])
        mv = sb("mv", [P, T, 2])
        ve = sb("ve", [P, T])
        rstd = sb("rstd", [P, T])
        lg = sb("lg", [P, T, E])
        lgm = sb("lgm", [P, T])
        lge = sb("lge", [P, T, E])
        lgs = sb("lgs", [P, T])
        prob = sb("prob", [P, T, B * E])

        q_room = qst[:, :, :].rearrange("p h n -> p (h n)").bitcast(F32)
        k_room = kst[:, :, :].rearrange("p h n -> p (h n)").bitcast(F32)
        v_room = V[:, :, :, :].rearrange("p t h n -> p (t h n)")
        we1 = [q_room[:, 2048 * i:2048 * i + 1024].rearrange("p (c f) -> p c f", c=C) for i in range(2)]
        we2 = [q_room[:, 2048 * i + 1024:2048 * i + 2048].rearrange("p (c d) -> p c d", d=D) for i in range(2)]
        used = [0]

        def room(words):
            used[0] += words
            return k_room[:, used[0] - words:used[0]]

        xg = [room(2 * D).rearrange("p (j d) -> p j d", d=D) for _ in range(2)]
        xgT = [room(C * CAP).rearrange("p (c j) -> p c j", j=CAP) for _ in range(2)]
        hT = [room(F // P * CAP).rearrange("p (f j) -> p f j", j=CAP) for _ in range(2)]
        yg = [room(2 * D).rearrange("p (j d) -> p j d", d=D) for _ in range(2)]
        vused = [0]

        def vroom(words):
            vused[0] += words
            return v_room[:, vused[0] - words:vused[0]]

        BE = B * E
        by_tile = lambda ap: ap.rearrange("p (t n) -> p t n", n=BE)
        onehot = [vroom(T * CAP // 2).bitcast(BF16).rearrange("p (t j) -> p t j", j=CAP) for _ in range(2)]
        picks = vroom(T * BE * 6 // 2).bitcast(BF16).rearrange("p (t n k) -> p t n k", n=BE, k=6)
        pos = by_tile(vroom(T * BE))
        above = by_tile(vroom(T * BE // 2).bitcast(BF16))
        equal = by_tile(vroom(T * BE // 2).bitcast(BF16))
        chosen = by_tile(vroom(T * BE // 2).bitcast(BF16))
        idgate = sb("idgate", [P, BE, 2, COLS])
        thr = vroom(BE)
        cand = vroom(BE)
        bit = vroom(BE)
        hit = vroom(BE)
        tokf = vroom(BE * 2)
        tok = sb("tok", [P, B, E, 2], U32)
        gate = sb("gate", [P, B, E, 2])
        tok_g = sb("tok_g", [P, B, 2, 2], U32)
        tok_s = sb("tok_s", [P, B, 2, 2], U32)
        gate_e = sb("gate_e", [P, B, 2, 2])
        lane = sb("lane", [P, 1])

        s_r = sem("routing_step")
        s_cn = sem("count_ready")
        s_in = sem("indicator_ready")
        s_oh = sem("onehot_ready")
        s_pk = sem("picked")
        s_pe2 = sem("picked_taken")
        s_tk = sem("gather_tokens_ready")
        s_ts = sem("scatter_tokens_ready")
        s_g = [sem(f"gathered{i}") for i in range(2)]
        s_gt = sem("gathered_turned")
        s_te = sem("gathered_turned_taken")
        s_h = sem("hidden_ready")
        s_si = sem("silu_ready")
        s_y = sem("expert_output_ready")
        s_ye = sem("expert_output_gated")
        s_sc = [sem(f"scattered{i}") for i in range(2)]
        s_we = [sem(f"expert_weights{i}") for i in range(2)]
        s_al = [sem(f"sum_loaded{i}") for i in range(2)]
        s_fz = sem("final_stats")
        s_fr = sem("final_rstd")
        s_fl = sem("final_layernorm")
        s_out = [sem(f"out_stored{i}") for i in range(2)]
        fin = [z, xb]

        s_w = sem("weights_loaded")
        s_x = sem("x_loaded")
        s_id = sem("identities_ready")
        s_pool = sem("pool_chain")
        s_dve = sem("dve_chain")
        s_act = sem("act_chain")
        s_item = sem("product_ready")
        s_evd = sem("product_taken_by_dve")
        s_eva = sem("product_taken_by_act")
        s_mask = sem("mask_ready")
        s_xb = sem("residual_ready")
        s_p1 = sem("part1_ready")
        s_p2 = sem("rest_ready")
        s_p3 = sem("part2_ready")
        s_p4 = sem("parts_ready")
        s_pw = [sem(f"parts_stored{i}") for i in range(2)]
        s_ql = [sem(f"q_stack_loaded{i}") for i in range(2)]
        s_kl = [sem(f"k_stack_loaded{i}") for i in range(2)]
        s_kx = sem("kx_stack_loaded")
        s_sm = sem("max_scores_ready")
        s_smu = sem("max_scores_used")
        s_nm = sem("minus_max_ready")
        s_nt = sem("minus_max_turned")
        s_ne = sem("minus_max_rows_ready")
        s_nl = [sem(f"minus_max_loaded{i}") for i in range(2)]
        s_st = sem("scores_ready")
        s_ex = sem("exp_ready")
        s_pu = sem("exp_used")
        s_ave = sem("values_taken")
        s_z = sem("stats_ready")
        s_rs = sem("rstd_ready")
        s_ln = sem("layernorm_ready")
        s_le = sem("logits_exp")
        s_x2 = sem("x2_stored")

        blk = ctx.enter_context(nc.Block())
        bank = lambda idx: (idx - STAGE[idx]) % 8

        ROWS_P = lambda ap: ap.rearrange("(t p) d -> p t d", p=P)
        NW = 19

        def wait(eng, semaphore, value):
            eng.wait_ge(semaphore, value)

        def wait_apart(eng, *waits):
            values = [eng.to_reg(waits[k]) for k in range(1, len(waits), 2)]
            eng.wait_ge(s_id, 1)
            for semaphore, value in zip(waits[0::2], values):
                eng.wait_ge(semaphore, value)

        from_one = [s_xb, s_item, s_mask, s_p2, s_evd, s_eva, s_x2, s_nt, s_ne, s_gt, s_y, s_si, s_te, s_ye,
                    s_pk, s_pe2] + s_pw + s_nl + s_out

        @blk.sync
        def _(sp):
            for semaphore in from_one:
                sp.sem_inc(semaphore, START)
            for dst, src in [
                (bcol[:, :], a["bias_columns"]), (wdq[:, :, :], a["Wd_q"].rearrange("(c p) n -> p c n", p=P)),
                (wdkv[:, :, :], a["Wd_kv"].rearrange("(c p) n -> p c n", p=P)), (wuq[:, :], a["Wu_q"]),
                (wqr[:, :], a["Wq_r"]), (wqrs[:, :], a["Wq_r_swapped"]), (cosT[:, :, :], a["cos"]),
                (sinT[:, :, :], a["sin"]), (wuk[:, :], a["Wu_k"]), (wuv[:, :], a["Wu_v"]),
                (wkr[:, :, :], a["Wk_r"].rearrange("(c p) n -> p c n", p=P)),
                (wkrs[:, :, :], a["Wk_r_swapped"].rearrange("(c p) n -> p c n", p=P)),
                (brow[:, :, :], a["bias_rows"].rearrange("a r d -> a (r d)").to_broadcast([P, 4 * D])
                 .rearrange("p (r d) -> p r d", r=4)),
                (w1x[:, :, :], a["W1T"].rearrange("(c p) n -> p c n", p=P)),
                (w2x[:, :, :], a["W2T"].rearrange("(c p) n -> p c n", p=P)),
                (wo[:, :, :], a["Wo"].rearrange("(c p) n -> p c n", p=P)),
                (w0[:, :, :], a["W0T"].rearrange("(c p) n -> p c n", p=P)),
                (w3[:, :, :], a["W3T"].rearrange("(c p) n -> p c n", p=P)),
                (wch[:, :, :], a["choiceT"].rearrange("(c p) n -> p c n", p=P)),
            ]:
                sp.dma_start(dst, src).then_inc(s_w, 16)

            def store_piece(b, i, dst, cols):
                sp.wait_ge(s_p4, b * PIECES + i + 1)
                src = part[:, i % 2, :, 0:cols]
                sp.dma_start(dst, src).then_inc(s_pw[i % 2], 16)

            def stored(b, i):
                wait_apart(sp, s_pw[0], 16 * (b * PIECES_OF[0] + (i + 2) // 2) + START,
                           s_pw[1], 16 * (b * PIECES_OF[1] + (i + 1) // 2) + START)

            def load_stack(dst, parts, mc, which, s):
                for t, term in enumerate(TERMS):
                    src = parts[term[which], mc * P:(mc + 1) * P, :].rearrange("(h d) n -> d h n", d=HD)
                    sp.dma_start(dst[t * HD:(t + 1) * HD, mc * 8:(mc + 1) * 8, :], src).then_inc(s, 16)

            def load_minus_max(b, n, g):
                sp.wait_ge(s_ne, b * 2 * NG + n + 1 + START)
                for p in range(3):
                    sp.dma_start(qst[KQ + p:KQ + p + 1, g * G:(g + 1) * G, :],
                                 nmT[p * G:(p + 1) * G, n % 2, :]).then_inc(s_nl[n % 2], 16)

            with sp.Fori(0, B) as b:
                wait_apart(sp, s_xb, b * 2 + START, s_item, b * NI + START)
                sp.dma_start(x[:, :, :], ROWS_P(a["x"][bass.ds(b * S, S), :])).then_inc(s_x, 16)
                sp.dma_start(cx[:, 0, :], a["ctx"][bass.ds(b * SK, P), :]).then_inc(s_x, 16)
                sp.dma_start(cx[0:SKR, 1, :], a["ctx"][bass.ds(b * SK + P, SKR), :]).then_inc(s_x, 16)
                sp.wait_ge(s_mask, b + START)
                sp.dma_start(mask_i[:, :, :],
                             a["mask"][bass.ds(b * S, S), :].rearrange("(t p) d -> p t d", p=P)).then_inc(s_x, 16)
                for i in range(8):
                    parts = q_parts if i < 4 else k_parts
                    mc, half = (i % 4) // 2, i % 2
                    store_piece(b, i, parts[:, mc * P:(mc + 1) * P, half * N:(half + 1) * N]
                                .rearrange("k p n -> p k n"), N)
                    if i % 2:
                        stored(b, i)
                        if i < 4:
                            load_stack(qst, q_parts, mc, 0, s_ql[mc])
                        else:
                            load_stack(kst, k_parts, mc, 1, s_kl[mc])
                store_piece(b, 8, kx_parts.rearrange("p k c n -> p k (c n)"), C * SK)
                stored(b, 8)
                for c in range(C):
                    for t, term in enumerate(TERMS):
                        src = kx_parts[:, term[1], c, :].rearrange("(h d) n -> d h n", d=HD)
                        sp.dma_start(kxst[t * HD:(t + 1) * HD, c * 8:(c + 1) * 8, 0:SK], src).then_inc(s_kx, 16)
                for g in range(NG):
                    load_minus_max(b, g, g)
                for i in range(9, 13):
                    mc, half = (i - 9) // 2, (i - 9) % 2
                    if i == 9:
                        wait_apart(sp, s_ql[0], b * 192 + 96, s_ql[1], b * 192 + 96)
                    store_piece(b, i, q_parts[:, mc * P:(mc + 1) * P, half * N:(half + 1) * N]
                                .rearrange("k p n -> p k n"), N)
                    if i % 2 == 0:
                        stored(b, i)
                        load_stack(qst, q_parts, mc, 0, s_ql[mc])
                for g in range(NG):
                    load_minus_max(b, NG + g, g)
                wait_apart(sp, s_ln, (b * 2 + 2) * T)
                sp.dma_start(ROWS_P(x2_rows[bass.ds(b * S, S), :]), z[:, :, :]).then_inc(s_x2, 16)
                wait_apart(sp, s_ql[0], b * 192 + 192, s_ql[1], b * 192 + 192, s_kl[0], b * 96 + 96,
                           s_kl[1], b * 96 + 96, s_kx, b * 192 + 192)
            sp.wait_ge(s_pu, B * ST_ALL)

            def load_expert(e, i):
                sp.dma_start(we1[i], a["w1"][bass.ds(e, 1), :, :].rearrange("a (c p) f -> p (a c) f", p=P)
                             ).then_inc(s_we[i], 16)
                sp.dma_start(we2[i], a["w2"][bass.ds(e, 1), :, :].rearrange("a (c p) d -> p (a c) d", p=P)
                             ).then_inc(s_we[i], 16)

            load_expert(0, 0)
            load_expert(1, 1)
            with sp.Fori(0, E // 2 - 1) as i:
                for half in range(2):
                    wait_apart(sp, s_y, i * UNITS + B * (half + 1) + START)
                    load_expert(i * 2 + 2 + half, half)
            for s in s_sc:
                sp.wait_ge(s, E // 2 * UNITS * 16 + COPIED)
            with sp.Fori(0, B // 2) as i:
                for k in range(2):
                    wait_apart(sp, s_out[k], i * 16 + START)
                    sp.dma_start(fin[k][:, :, :], ROWS_P(acc_rows[bass.ds((i * 2 + k) * S, S), :])
                                 ).then_inc(s_al[k], 16)
                for k in range(2):
                    wait_apart(sp, s_fl, (i * 2 + k + 1) * T)
                    sp.dma_start(ROWS_P(out[bass.ds((i * 2 + k) * S, S), :]), fin[k][:, :, :]).then_inc(s_out[k], 16)
            for k in range(2):
                sp.wait_ge(s_out[k], B // 2 * 16 + START)
            sp.wait_ge(s_x2, B * 16 + START)

        @blk.gpsimd
        def _(pool):
            steps = [0]

            def link(ins):
                steps[0] += 1
                ins.then_inc(s_pool, 1)
                pool.wait_ge(s_pool, steps[0])

            link(pool.memset(ident[:, :], 0.0))
            link(pool.affine_select(out=ident[:, :], in_=ident[:, :], compare_op=ALU.not_equal, fill=1.0,
                                    base=0, pattern=[[-1, P]], channel_multiplier=1))
            link(pool.memset(tri[:, :], 0.0))
            link(pool.affine_select(out=tri[:, :], in_=tri[:, :], compare_op=ALU.is_ge, fill=1.0,
                                    base=0, pattern=[[-1, P]], channel_multiplier=1))
            link(pool.iota(iota_f, pattern=[[1, CAP]], base=0, channel_multiplier=0,
                           allow_small_or_imprecise_dtypes=True))
            link(pool.tensor_copy(iota[:, :], iota_f))
            link(pool.tensor_copy(identb[:, :], ident[:, :]))
            link(pool.memset(onesb[:, :], 1.0))
            link(pool.memset(mhalf[:, :], -0.5))
            link(pool.memset(kst[:, :, :], 1.0))
            link(pool.memset(qst[:, :, :], 0.0))
            link(pool.memset(kxst[:, :, :], 1.0))
            link(pool.memset(kxst[0:KQ, :, SK:160], 0.0))
            link(pool.memset(maskb[:, :, :], MASKED))
            for tile in (V[:, :, :, :], Vx[:, :, :], Vr[:, :, :]):
                link(pool.memset(tile, 0.0))
            link(pool.memset(V[:, :, :, HD:HD + 1], 1.0))
            link(pool.memset(Vx[:, :, HD:HD + 1], 1.0))
            link(pool.iota(lane[:, :], pattern=[[0, 1]], base=0, channel_multiplier=1,
                           allow_small_or_imprecise_dtypes=True))
            pool.memset(Vr[:, :, HD:HD + 1], 1.0).then_inc(s_id, 1)
            pool.wait_ge(s_w, 16 * NW)

            def split(b, i, cols):
                p = i % 2
                pool.wait_ge(s_p1, b * PIECES + i + 1)
                pool.tensor_tensor(rest[:, p, 0:cols], full[:, p, 0:cols], part[:, p, 0, 0:cols],
                                   ALU.subtract).then_inc(s_p2, 1)
                pool.wait_ge(s_p3, b * PIECES + i + 1)
                pool.tensor_tensor(part[:, p, 2, 0:cols], rest[:, p, 0:cols], part[:, p, 1, 0:cols],
                                   ALU.subtract).then_inc(s_p4, 1)

            def rsqrt(b, n):
                pool.wait_ge(s_z, b * 2 + n + 1)
                pool.tensor_tensor(rstd[:, :], ve[:, :], mhalf[:, :], ALU.pow).then_inc(s_rs, 1)

            with pool.Fori(0, B) as b:
                pool.wait_ge(s_x, (b + 1) * 64)
                pool.wait_ge(s_evd, b * ND + START)
                pool.tensor_tensor(xb[:, :, :], x[:, :, :], brow[:, 1:2, :].to_broadcast([P, T, D]),
                                   ALU.add).then_inc(s_xb, 1)
                pool.tensor_scalar(maskb[:, :, 0:SK], mask_i[:, :, :], 0.0, MASKED, ALU.is_equal,
                                   ALU.mult).then_inc(s_mask, 1)
                for i in range(9):
                    split(b, i, C * SK if i == 8 else N)
                rsqrt(b, 0)
                pool.wait_ge(s_ln, b * 2 * T + T)
                pool.tensor_tensor(xb[:, :, :], z[:, :, :], brow[:, 3:4, :].to_broadcast([P, T, D]),
                                   ALU.add).then_inc(s_xb, 1)
                for i in range(9, 13):
                    split(b, i, N)
                rsqrt(b, 1)

            pool.wait_ge(s_x2, B * 16 + START)

            for k in range(2):
                rows = slice(k * B // 2 * S, (k + 1) * B // 2 * S)
                pool.dma_start(acc_rows[rows, :], x2_rows[rows, :]).then_inc(s_sc[k], COPIED)
            for k in range(2):
                pool.wait_ge(s_sc[k], COPIED)

            def gather(i, u):
                k, eh, bb = u % 2, u // B, u % B
                wait_apart(pool, s_gt, i * UNITS + max(0, u - 1) + START)
                for j in range(2):
                    pool.indirect_dma_start(xg[k][:, j, :], None, x2_rows,
                                            bass.IndirectOffsetOnAxis(tok_g[:, bb, eh, j:j + 1], 0)
                                            ).then_inc(s_g[k], 16)

            def scatter(i, u):
                k, eh, bb = u % 2, u // B, u % B
                wait_apart(pool, s_ye, i * UNITS + u + 1 + START, s_sc[k], i * UNITS * 16 + 32 * max(0, u // 2 - 1) + COPIED)
                for j in range(2):
                    pool.indirect_dma_start(acc_rows, bass.IndirectOffsetOnAxis(tok_s[:, bb, eh, j:j + 1], 0),
                                            yg[k][:, j, :], None, compute_op=ALU.add).then_inc(s_sc[k], 16)

            with pool.Fori(0, E // 2) as i:
                pool.wait_ge(s_tk, i + 1)
                gather(i, 0)
                gather(i, 1)
                pool.wait_ge(s_ts, i * 2 + 2)
                for u in range(UNITS):
                    if u + 2 < UNITS:
                        gather(i, u + 2)
                    scatter(i, u)
            with pool.Fori(0, B) as b:
                pool.wait_ge(s_fz, b + 1)
                pool.tensor_tensor(rstd[:, :], ve[:, :], mhalf[:, :], ALU.pow).then_inc(s_fr, 1)

        @blk.scalar
        def _(act):
            def taken_before(b, idx):
                act.wait_ge(s_item, b * NI + idx + 1 + START)

            def copy_item(b, idx, dst, cols=N):
                taken_before(b, idx)
                act.activation(dst, PS[:, bank(idx), 0:cols], ACT.Copy).then_inc(s_eva, 1)

            def part1(b, i, cols):
                p = i % 2
                act.wait_ge(s_evd, b * ND + taken("D", PIECE[i] + 1) + START)
                act.wait_ge(s_pw[p], 16 * (b * PIECES_OF[p] + (i // 2)) + START)
                act.activation(part[:, p, 0, 0:cols], full[:, p, 0:cols], ACT.Copy).then_inc(s_p1, 1)

            def part2(b, i, cols):
                p = i % 2
                act.wait_ge(s_p2, b * PIECES + i + 1 + START)
                act.activation(part[:, p, 1, 0:cols], rest[:, p, 0:cols], ACT.Copy).then_inc(s_p3, 1)

            def attention(b, n0, units, group, scale):
                per = group // HALVES
                for n in range(units + LAG):
                    if n < units:
                        act.wait_ge(s_st, b * ST_ALL + n0 + n + 1)
                        if n0 + n >= 4:
                            act.wait_ge(s_pu, b * ST_ALL + n0 + n - 3)
                        act.activation(pT[:, n % 4, :], PS[:, 3 + n % 2, :], ACT.Exp,
                                       scale=scale).then_inc(s_ex, 1)
                    m = n - LAG
                    if m >= 0 and m % per == per - 1:
                        k = m // per
                        act.wait_ge(s_pu, b * ST_ALL + n0 + m + 1)
                        if n0 == 0 and k == 0:
                            act.wait_ge(s_mask, b + 1 + START)
                            act.wait_ge(s_xb, b * 2 + 1 + START)
                        act.activation(oT[:, k // 2, (k % 2) * N:(k % 2 + 1) * N], PS[:, 5 + k % 2, :],
                                       ACT.Copy).then_inc(s_ave, 1)

            act.wait_ge(s_w, 16 * NW)
            with act.Fori(0, B) as b:
                f = first("xT")
                for n in (1, 3):
                    copy_item(b, f + n, xT[:, n // 2, (n % 2) * N:(n % 2 + 1) * N])
                for name, dst, col in (("ctq", ctq, 0), ("ctkv", ctkv, 1)):
                    for half in range(HALVES):
                        idx = first(name) + half
                        taken_before(b, idx)
                        act.activation(dst[:, half * N:(half + 1) * N], PS[:, bank(idx), :], ACT.Identity,
                                       bias=bcol[:, col:col + 1]).then_inc(s_eva, 1)
                for i in range(10):
                    if i < 9:
                        part1(b, i, C * SK if i == 8 else N)
                    if i >= 1:
                        part2(b, i - 1, C * SK if i == 9 else N)
                attention(b, 0, ST_SELF, ST_SELF // NG, SCALE_SELF)
                for n in (1, 3):
                    copy_item(b, first("oT") + n, xT[:, n // 2, (n % 2) * N:(n % 2 + 1) * N])
                for n in (1, 3):
                    copy_item(b, first("x1T") + n, xT[:, n // 2, (n % 2) * N:(n % 2 + 1) * N])
                for i in range(9, 14):
                    if i < 13:
                        part1(b, i, N)
                    if i >= 10:
                        part2(b, i - 1, N)
                attention(b, ST_SELF, ST_CROSS, ST_CROSS // NG, SCALE_CROSS)
                for n in (1, 3):
                    copy_item(b, first("oxT") + n, xT[:, n // 2, (n % 2) * N:(n % 2 + 1) * N])
                for n in (1, 3):
                    copy_item(b, first("x2T") + n, xT[:, n // 2, (n % 2) * N:(n % 2 + 1) * N])
                act.wait_ge(s_evd, b * ND + ND + START)
                act.activation(lge[:, :, :], lg[:, :, :], ACT.Exp).then_inc(s_le, 1)
            with act.Fori(0, E // 2) as i:
                for u in range(UNITS):
                    k = u % 2
                    act.wait_ge(s_y, i * UNITS + max(0, u - 1) + START)
                    for fh in range(2):
                        act.wait_ge(s_h, i * UNITS * 2 + 2 * u + fh + 1)
                        act.activation(hT[k][:, 2 * fh:2 * fh + 2, :].rearrange("p f j -> p (f j)"),
                                       PS[:, 2 + 2 * k + fh, :], ACT.Silu).then_inc(s_si, 1)

        DVE_STEPS = 8 + NG * (4 + 3) + 2 * (T + 2) + 4

        @blk.vector
        def _(dve):
            steps = [0]

            def link(b, ins, how=wait):
                steps[0] += 1
                ins.then_inc(s_dve, 1)
                how(dve, s_dve, b * DVE_STEPS + steps[0])

            def ready(b, idx):
                dve.wait_ge(s_item, b * NI + idx + 1 + START)

            def copy_item(b, idx, dst, cols=N):
                ready(b, idx)
                dve.tensor_copy(dst, PS[:, bank(idx), 0:cols]).then_inc(s_evd, 1)

            def full_free(b, i):
                dve.wait_ge(s_p2, b * PIECES + max(0, i - 1) + START)

            def roped(b, i, idx, c0):
                p, mc, half = i % 2, (i % 4) // 2, i % 2
                cols = slice(half * N, (half + 1) * N)
                c0 += mc
                ready(b, idx)
                dve.scalar_tensor_tensor(out=ru[:, p, :], in0=PS[:, bank(idx), :], scalar=bcol[:, c0 + 2:c0 + 3],
                                         in1=cosT[:, mc, cols], op0=ALU.add, op1=ALU.mult).then_inc(s_evd, 1)
                ready(b, idx + 1)
                dve.scalar_tensor_tensor(out=rv[:, p, :], in0=PS[:, bank(idx + 1), :],
                                         scalar=bcol[:, c0 + 4:c0 + 5], in1=sinT[:, mc, cols],
                                         op0=ALU.add, op1=ALU.mult).then_inc(s_evd, 1)
                dve.wait_ge(s_evd, b * ND + taken("D", idx + 2) + START)
                link(b, dve.tensor_tensor(ru[:, p, :], ru[:, p, :], rv[:, p, :], ALU.add))
                full_free(b, i)
                ready(b, idx + 2)
                dve.scalar_tensor_tensor(out=full[:, p, :], in0=PS[:, bank(idx + 2), :],
                                         scalar=bcol[:, c0:c0 + 1], in1=ru[:, p, :],
                                         op0=ALU.add, op1=ALU.add).then_inc(s_evd, 1)

            def attention(b, n0, g0, order, cross):
                sm_group = (SM_CROSS if cross else SM_SELF) // NG
                for what, n in order:
                    if what == "smax":
                        dve.wait_ge(s_sm, b * SM_ALL + n0 + n + 1)
                        g, k = divmod(n, sm_group)
                        if cross:
                            j, t0, nt = k // 3, 3 * (k % 3), min(3, T - 3 * (k % 3))
                            dve.tensor_reduce(nmf[:, t0:t0 + nt, j:j + 1],
                                              PS[:, n % 3, 0:nt * SK].rearrange("p (t k) -> p t k", k=SK),
                                              AX.X, ALU.max, negate=True).then_inc(s_smu, 1)
                        else:
                            j, t, half = k // (T * HALVES), k // HALVES % T, k % HALVES
                            dve.tensor_reduce(mh[:, 0, t, j, half:half + 1], PS[:, n % 3, :],
                                              AX.X, ALU.max).then_inc(s_smu, 1)
                        if k == sm_group - 1:
                            p = (g0 + g) % 2
                            dve.wait_ge(s_smu, b * SM_ALL + n0 + n + 1)
                            if not cross:
                                link(b, dve.tensor_reduce(nmf[:, :, :], mh[:, 0, :, :, :], AX.X, ALU.max,
                                                          negate=True))
                            dve.wait_ge(s_nt, b * 2 * NG + max(0, g0 + g - 1) + START)
                            link(b, dve.tensor_copy(nmp[:, p, :, 0:G], nmf[:, :, :]))
                            link(b, dve.tensor_tensor(nmr[:, :, :], nmf[:, :, :], nmp[:, p, :, 0:G],
                                                      ALU.subtract))
                            link(b, dve.tensor_copy(nmp[:, p, :, G:2 * G], nmr[:, :, :]))
                            dve.tensor_tensor(nmp[:, p, :, 2 * G:3 * G], nmr[:, :, :], nmp[:, p, :, G:2 * G],
                                              ALU.subtract).then_inc(s_nm, 1)
                    elif what == "turn":
                        dve.wait_ge(s_nt, b * 2 * NG + g0 + n + 1 + START)
                        m = g0 + n
                        dve.wait_ge(s_nl[m % 2], 48 * (b * NG + m // 2) + START)
                        dve.tensor_copy(nmT[:, m % 2, :], PS[0:3 * G, 7, :].bitcast(BF16)).then_inc(s_ne, 1)

            def heads_out(b, name):
                if name == "ox":
                    dve.wait_ge(s_xb, b * 2 + 2 + START)
                for t in range(T):
                    idx = first(name) + t
                    ready(b, idx)
                    heads = PS[:, bank(idx), :].rearrange("p (h k) -> p h k", k=V32)
                    link(b, dve.reciprocal(rz[:, t % 2, :], heads[:, :, HD]))
                    dve.tensor_tensor(z[:, t, :].rearrange("p (h k) -> p h k", k=HD), heads[:, :, 0:HD],
                                      rz[:, t % 2, :].rearrange("p (h k) -> p h k", k=1).to_broadcast([P, H, HD]),
                                      ALU.mult).then_inc(s_evd, 1)

            def layernorm(b, name, n):
                for k in range(4):
                    idx = first(name) + k
                    ready(b, idx)
                    dve.tensor_tensor(z[:, 2 * k:2 * k + 2, :],
                                      PS[:, bank(idx), :].rearrange("p (t d) -> p t d", t=2),
                                      xb[:, 2 * k:2 * k + 2, :], ALU.add).then_inc(s_evd, 1)
                    dve.wait_ge(s_evd, b * ND + taken("D", idx + 1) + START)
                    for t in (2 * k, 2 * k + 1):
                        ins = dve.bn_stats(st6[:, t, :], z[:, t, :])
                link(b, ins, wait_apart)
                for t in range(T):
                    ins = dve.bn_aggr(mv[:, t, :], st6[:, t, :])
                link(b, ins)
                dve.tensor_scalar(ve[:, :], mv[:, :, 1], EPS, None, ALU.add).then_inc(s_z, 1)
                dve.wait_ge(s_rs, b * 2 + n + 1)
                for t in range(T):
                    dve.tensor_scalar(z[:, t, :], z[:, t, :], mv[:, t, 0:1], rstd[:, t:t + 1],
                                      ALU.subtract, ALU.mult).then_inc(s_ln, 1)

            dve.wait_ge(s_w, 16 * NW)
            dve.wait_ge(s_id, 1)
            with dve.Fori(0, B) as b:
                for n in (0, 2):
                    copy_item(b, first("xT") + n, xT[:, n // 2, (n % 2) * N:(n % 2 + 1) * N])
                copy_item(b, first("ctxT"), cxT[:, :, :].rearrange("p c n -> p (c n)"), C * SK)
                dve.wait_ge(s_x2, b * 16 + START)
                for i in range(4):
                    roped(b, i, first("q") + 3 * i, 2)
                for i in range(4):
                    roped(b, 4 + i, first("k") + 3 * i, 8)
                for k in range(4):
                    idx = first("v") + k
                    ready(b, idx)
                    for t in range(2):
                        ins = dve.tensor_tensor(
                            V[:, 2 * k + t, :, 0:HD],
                            PS[:, bank(idx), t * D:(t + 1) * D].rearrange("p (h d) -> p h d", d=HD),
                            brow[:, 0, :].rearrange("p (h d) -> p h d", d=HD), ALU.add)
                    ins.then_inc(s_evd, 1)
                idx = first("kx")
                ready(b, idx)
                full_free(b, 8)
                for c in range(C):
                    ins = dve.tensor_scalar(full[:, 0, c * SK:(c + 1) * SK], PS[:, bank(idx), c * SK:(c + 1) * SK],
                                            bcol[:, 14 + c:15 + c], None, ALU.add)
                ins.then_inc(s_evd, 1)
                idx = first("vx")
                ready(b, idx)
                dve.tensor_tensor(Vx[:, :, 0:HD], PS[:, bank(idx), 0:D].rearrange("p (h d) -> p h d", d=HD),
                                  brow[:, 2, :].rearrange("p (h d) -> p h d", d=HD), ALU.add).then_inc(s_evd, 1)
                idx = first("vxr")
                ready(b, idx)
                for j in range(G):
                    rows = slice(V32 * j, V32 * j + SKR)
                    ins = dve.tensor_tensor(
                        Vr[rows, :, 0:HD],
                        PS[rows, bank(idx), 0:D].rearrange("p (g j d) -> p g j d", j=G, d=HD)[:, :, j, :],
                        brow[rows, 2, :].rearrange("p (g j d) -> p g j d", j=G, d=HD)[:, :, j, :], ALU.add)
                ins.then_inc(s_evd, 1)
                attention(b, 0, 0, ORDER_SELF, False)
                heads_out(b, "o")
                for n in (0, 2):
                    copy_item(b, first("oT") + n, xT[:, n // 2, (n % 2) * N:(n % 2 + 1) * N])
                layernorm(b, "y", 0)
                for n in (0, 2):
                    copy_item(b, first("x1T") + n, xT[:, n // 2, (n % 2) * N:(n % 2 + 1) * N])
                for i in range(9, 13):
                    idx = first("qx") + i - 9
                    ready(b, idx)
                    full_free(b, i)
                    c = (i - 9) // 2
                    dve.tensor_scalar(full[:, i % 2, :], PS[:, bank(idx), :], bcol[:, 16 + c:17 + c], None,
                                      ALU.add).then_inc(s_evd, 1)
                attention(b, SM_SELF, NG, ORDER_CROSS, True)
                heads_out(b, "ox")
                for n in (0, 2):
                    copy_item(b, first("oxT") + n, xT[:, n // 2, (n % 2) * N:(n % 2 + 1) * N])
                layernorm(b, "yx", 1)
                for n in (0, 2):
                    copy_item(b, first("x2T") + n, xT[:, n // 2, (n % 2) * N:(n % 2 + 1) * N])
                idx = first("logit")
                ready(b, idx)
                lgp = PS[:, bank(idx), 0:T * E].rearrange("p (t e) -> p t e", e=E)
                link(b, dve.tensor_reduce(lgm[:, :], lgp, AX.X, ALU.max))
                dve.tensor_tensor(lg[:, :, :], lgp,
                                  lgm[:, :].rearrange("p (t e) -> p t e", e=1).to_broadcast([P, T, E]),
                                  ALU.subtract).then_inc(s_evd, 1)
                dve.wait_ge(s_le, b + 1)
                link(b, dve.tensor_reduce(lgs[:, :], lge[:, :, :], AX.X, ALU.add))
                link(b, dve.reciprocal(lgm[:, :], lgs[:, :]))
                link(b, dve.tensor_tensor(prob[:, :, bass.ds(b * E, E)], lge[:, :, :],
                                          lgm[:, :].rearrange("p (t e) -> p t e", e=1).to_broadcast([P, T, E]),
                                          ALU.mult))
            assert steps[0] == DVE_STEPS

            made = [0]

            def link_r(ins):
                made[0] += 1
                ins.then_inc(s_r, 1)
                dve.wait_ge(s_r, made[0])

            def over_tiles(ap):
                return ap.rearrange("p (t n) -> p t n", t=1).to_broadcast([P, T, BE])

            def per_expert(ap):
                return PS[:, ap, 0:BE]

            dve.wait_ge(s_pu, B * ST_ALL)
            link_r(dve.memset(thr.bitcast(I32), 0))
            link_r(dve.memset(bit.bitcast(I32), 1 << (BITS - 1)))
            before = made[0]
            with dve.Fori(0, BITS) as n:
                dve.tensor_tensor(cand.bitcast(I32), thr.bitcast(I32), bit.bitcast(I32),
                                  ALU.bitwise_or).then_inc(s_r, 1)
                dve.wait_ge(s_r, n * 3 + before + 1)
                dve.tensor_tensor(above[:, :, :], prob[:, :, :], over_tiles(cand), ALU.is_ge).then_inc(s_in, 1)
                dve.tensor_scalar(bit.bitcast(I32), bit.bitcast(I32), 1, None,
                                  ALU.logical_shift_right)
                dve.wait_ge(s_cn, n + 1)
                dve.scalar_tensor_tensor(out=hit, in0=PS[:, 0, 0:BE], scalar=float(CAP), in1=cand,
                                         op0=ALU.is_ge, op1=ALU.mult).then_inc(s_r, 1)
                dve.wait_ge(s_r, n * 3 + before + 2)
                dve.tensor_tensor(thr, thr, hit, ALU.max).then_inc(s_r, 1)
                dve.wait_ge(s_r, n * 3 + before + 3)
            made[0] = before + 3 * BITS
            link_r(dve.tensor_tensor(above[:, :, :], prob[:, :, :], over_tiles(thr), ALU.is_gt))
            dve.tensor_tensor(equal[:, :, :], prob[:, :, :], over_tiles(thr), ALU.is_equal).then_inc(s_in, 1)
            dve.wait_ge(s_cn, BITS + 1)
            link_r(dve.tensor_scalar(hit, PS[:, 0, 0:BE], -1.0, float(CAP), ALU.mult, ALU.add))
            ranks = PS[:, 1, 0:T * BE].rearrange("p (t n) -> p t n", n=BE)
            link_r(dve.tensor_tensor(pos[:, :, :], ranks, over_tiles(hit), ALU.is_lt))
            link_r(dve.tensor_tensor(pos[:, :, :], pos[:, :, :], equal[:, :, :], ALU.mult))
            dve.tensor_tensor(chosen[:, :, :], pos[:, :, :], above[:, :, :], ALU.add).then_inc(s_in, 1)
            dve.wait_ge(s_in, BITS + 2)
            for t in range(T):
                dve.tensor_scalar(picks[:, t, :, 1], prob[:, t, :], 0.0, float(t), ALU.mult, ALU.add)
            dve.tensor_scalar(picks[:, :, :, 0], prob[:, :, :], 0.0, lane[:, 0:1], ALU.mult, ALU.add)
            link_r(dve.tensor_copy(picks[:, :, :, 2], prob[:, :, :]))
            link_r(dve.tensor_tensor(pos[:, :, :], prob[:, :, :], picks[:, :, :, 2], ALU.subtract))
            link_r(dve.tensor_copy(picks[:, :, :, 3], pos[:, :, :]))
            link_r(dve.tensor_tensor(picks[:, :, :, 4], pos[:, :, :], picks[:, :, :, 3], ALU.subtract))
            dve.wait_ge(s_cn, BITS + 2)
            link_r(dve.scalar_tensor_tensor(out=pos[:, :, :], in0=ranks, scalar=1.0, in1=chosen[:, :, :],
                                            op0=ALU.add, op1=ALU.mult))
            link_r(dve.tensor_scalar(pos[:, :, :], pos[:, :, :], 1.0, None, ALU.subtract))
            with dve.Fori(0, BE // 2) as i:
                for k in range(2):
                    dve.wait_ge(s_pk, i * 2 + START)
                    for t in range(T):
                        ins = dve.tensor_scalar(onehot[k][:, t, :], iota[:, :],
                                                pos[:, t, bass.ds(i * 2 + k, 1)], None, ALU.is_equal)
                    ins.then_inc(s_oh, 1)
                for k in range(2):
                    wait_apart(dve, s_pk, i * 2 + k + 1 + START)
                    dve.tensor_copy(idgate[:, bass.ds(i * 2 + k, 1), :, :].rearrange("p a j c -> p (a j c)"),
                                    PS[:, 2 + k, 0:2 * COLS]).then_inc(s_pe2, 1)
            dve.wait_ge(s_pe2, BE + START)
            col = lambda c: idgate[:, :, :, c]
            tokf3 = tokf.rearrange("p (n j) -> p n j", j=2)
            gate3 = gate[:, :, :, :].rearrange("p b e j -> p (b e) j")
            link_r(dve.scalar_tensor_tensor(out=tokf3, in0=col(1), scalar=float(P), in1=col(0),
                                            op0=ALU.mult, op1=ALU.add))
            link_r(dve.tensor_tensor(gate3, col(2), col(3), ALU.add))
            link_r(dve.tensor_tensor(gate3, gate3, col(4), ALU.add))
            for b in range(B):
                link_r(dve.tensor_scalar(tok[:, b, :, :], tokf3[:, b * E:(b + 1) * E, :], float(b * S), None,
                                         ALU.add))

            def turned(i, u):
                dve.wait_ge(s_gt, i * UNITS + u + 1 + START)
                dve.tensor_copy(xgT[u % 2].rearrange("p c j -> p (c j)"), PS[:, u % 2, :]).then_inc(s_te, 1)

            def gated(i, u):
                k, eh, bb = u % 2, u // B, u % B
                dve.wait_ge(s_y, i * UNITS + u + 1 + START)
                dve.wait_ge(s_sc[k], i * UNITS * 16 + 32 * (u // 2) + COPIED)
                for j in range(2):
                    ins = dve.tensor_scalar(yg[k][:, j, :], PS[:, 6 + k, j * D:(j + 1) * D],
                                            gate_e[:, bb, eh, j:j + 1], None, ALU.mult)
                ins.then_inc(s_ye, 1)

            with dve.Fori(0, E // 2) as i:
                wait_apart(dve, s_gt, i * UNITS + START)
                dve.tensor_copy(tok_g[:, :, :, :], tok[:, :, bass.ds(i * 2, 2), :]).then_inc(s_tk, 1)
                wait_apart(dve, s_sc[0], i * UNITS * 16 + COPIED, s_sc[1], i * UNITS * 16 + COPIED)
                dve.tensor_copy(tok_s[:, :, :, :], tok[:, :, bass.ds(i * 2, 2), :]).then_inc(s_ts, 1)
                dve.tensor_copy(gate_e[:, :, :, :], gate[:, :, bass.ds(i * 2, 2), :]).then_inc(s_ts, 1)
                turned(i, 0)
                turned(i, 1)
                dve.wait_ge(s_ts, i * 2 + 2)
                for u in range(UNITS):
                    if u + 2 < UNITS:
                        turned(i, u + 2)
                    gated(i, u)

            per = 2 * T
            base = made[0]
            with dve.Fori(0, B // 2) as i:
                for k in range(2):
                    n = 0
                    dve.wait_ge(s_al[k], i * 16 + 16)
                    for t in range(T):
                        dve.bn_stats(st6[:, t, :], fin[k][:, t, :]).then_inc(s_r, 1)
                    wait_apart(dve, s_r, (i * 2 + k) * per + base + T)
                    for t in range(T):
                        dve.bn_aggr(mv[:, t, :], st6[:, t, :]).then_inc(s_r, 1)
                    dve.wait_ge(s_r, (i * 2 + k) * per + base + 2 * T)
                    dve.tensor_scalar(ve[:, :], mv[:, :, 1], EPS, None, ALU.add).then_inc(s_fz, 1)
                    dve.wait_ge(s_fr, i * 2 + k + 1)
                    for t in range(T):
                        dve.tensor_scalar(fin[k][:, t, :], fin[k][:, t, :], mv[:, t, 0:1], rstd[:, t:t + 1],
                                          ALU.subtract, ALU.mult).then_inc(s_fl, 1)

        @blk.tensor
        def _(pe):
            def item(b, idx):
                old = idx - 8
                if old >= STAGE[idx]:
                    if ITEMS[old][1] == "A":
                        pe.wait_ge(s_eva, b * NA + taken("A", old + 1) + START)
                    else:
                        pe.wait_ge(s_evd, b * ND + taken("D", old + 1) + START)
                return PS[:, bank(idx), :]

            def taken_upto(b, idx):
                pe.wait_ge(s_eva, b * NA + taken("A", idx) + START)
                pe.wait_ge(s_evd, b * ND + taken("D", idx) + START)

            def turn_tokens(b, name, src, per_tile=None):
                for n in range(4):
                    idx = first(name) + n
                    ps = item(b, idx)
                    for k in range(4):
                        t = 4 * (n % 2) + k
                        if per_tile is not None and n < 2:
                            per_tile(t)
                        ins = pe.transpose(ps[:, k * P:(k + 1) * P], src[:, t, (n // 2) * P:(n // 2 + 1) * P],
                                           ident[:, :])
                    ins.then_inc(s_item, 1)

            def project(b, idx, w, rhs, half, m, cols=N):
                ps = item(b, idx)
                for c in range(C):
                    ins = pe.matmul(ps[:, 0:cols], w[:, c, m * P:(m + 1) * P], rhs[:, c, half * N:half * N + cols],
                                    start=(c == 0), stop=(c == C - 1))
                ins.then_inc(s_item, 1)

            def attention(b, n0, u0, g0, order, cross):
                sm_group = (SM_CROSS if cross else SM_SELF) // NG
                per = (ST_CROSS if cross else ST_SELF) // NG // HALVES
                keys = kxst if cross else kst
                for what, n in order:
                    if what == "smax":
                        g, k = divmod(n, sm_group)
                        if k == 0 and g % 2 == 0:
                            if cross:
                                pe.wait_ge(s_ql[g // 2], b * 192 + 192)
                                pe.wait_ge(s_kx, b * 192 + 192)
                            else:
                                pe.wait_ge(s_ql[g // 2], b * 192 + 96)
                                pe.wait_ge(s_kl[g // 2], b * 96 + 96)
                        if n >= 3:
                            pe.wait_ge(s_smu, b * SM_ALL + n0 + n - 2)
                        ps = PS[:, n % 3, :]
                        if cross:
                            h, t0 = g * G + k // 3, 3 * (k % 3)
                            nt = min(3, T - t0)
                            pe.matmul(ps[:, 0:nt * SK], identb[:, :], maskb[:, t0:t0 + nt, 0:SK],
                                      start=True, stop=False, skip_group_check=True)
                            for t in range(t0, t0 + nt):
                                ins = pe.matmul(ps[:, (t - t0) * SK:(t - t0 + 1) * SK],
                                                qst[0:KQ, h, t * P:(t + 1) * P], kxst[0:KQ, h, 0:SK],
                                                start=False, stop=(t == t0 + nt - 1), skip_group_check=True)
                        else:
                            h, t, half = g * G + k // (T * HALVES), k // HALVES % T, k % HALVES
                            ins = pe.matmul(ps, qst[0:KQ, h, t * P:(t + 1) * P],
                                            kst[0:KQ, h, half * N:(half + 1) * N], start=True, stop=True)
                        ins.then_inc(s_sm, 1)
                    elif what == "turn":
                        m = g0 + n
                        pe.wait_ge(s_nm, b * 2 * NG + m + 1)
                        pe.wait_ge(s_ne, b * 2 * NG + m + START)
                        rows = PS[0:3 * G, 7, :].bitcast(BF16)
                        for t in range(T):
                            ins = pe.transpose(rows[:, t * P:(t + 1) * P], nmp[:, m % 2, t, :], identb[:, :])
                        ins.then_inc(s_nt, 1)
                    elif what == "st":
                        gh, k = divmod(n, per)
                        g, half = divmod(gh, HALVES)
                        cols = slice(half * N, (half + 1) * N)
                        if k == 0 and half == 0:
                            m = g0 + g
                            pe.wait_ge(s_nl[m % 2], 48 * (b * NG + m // 2 + 1) + START)
                        if n >= 2:
                            pe.wait_ge(s_ex, b * ST_ALL + u0 + n - 1)
                        ps = PS[:, 3 + n % 2, :]
                        if not cross:
                            kc, j = divmod(k, G)
                            ins = pe.matmul(ps, kst[0:KM, g * G + j, kc * P:(kc + 1) * P],
                                            qst[0:KM, g * G + j, cols], start=True, stop=True)
                        elif k < G:
                            for t in range(4):
                                pe.matmul(ps[:, t * P:(t + 1) * P], maskb[:, 4 * half + t, 0:P], identb[:, :],
                                          start=(t == 0), stop=False, skip_group_check=True)
                            ins = pe.matmul(ps, kxst[0:KM, g * G + k, 0:P], qst[0:KM, g * G + k, cols],
                                            start=False, stop=True, skip_group_check=True)
                        else:
                            for j in range(G):
                                rows = PS[V32 * j:V32 * (j + 1), 3 + n % 2, :]
                                for t in range(4):
                                    pe.matmul(rows[:, t * P:(t + 1) * P], maskb[:, 4 * half + t, P:P + V32],
                                              identb[:, :], start=(t == 0), stop=False, skip_group_check=True,
                                              tile_position=(0, V32 * j))
                                ins = pe.matmul(rows, kxst[0:KM, g * G + j, P:P + V32], qst[0:KM, g * G + j, cols],
                                                start=False, stop=True, skip_group_check=True,
                                                tile_position=(0, V32 * j))
                        ins.then_inc(s_st, 1)
                    else:
                        gh, k = divmod(n, per)
                        g, half = divmod(gh, HALVES)
                        (wait_apart if cross and k == G else wait)(pe, s_ex, b * ST_ALL + u0 + n + 1)
                        if k == 0 and gh >= 2:
                            pe.wait_ge(s_ave, b * 4 * NG + (2 * NG if cross else 0) + gh - 1)
                        av = PS[:, 5 + gh % 2, :]
                        if not cross:
                            kc, j = divmod(k, G)
                            ins = pe.matmul(av[V32 * j:V32 * (j + 1), :], V[:, kc, g * G + j, :], pT[:, n % 4, :],
                                            start=(kc == 0), stop=(kc == T - 1), tile_position=(0, V32 * j),
                                            skip_group_check=True)
                        elif k < G:
                            ins = pe.matmul(av[V32 * k:V32 * (k + 1), :], Vx[:, g * G + k, :], pT[:, n % 4, :],
                                            start=True, stop=False, tile_position=(0, V32 * k),
                                            skip_group_check=True)
                        else:
                            for j in range(G):
                                rows = slice(V32 * j, V32 * j + SKR)
                                ins = pe.matmul(av[V32 * j:V32 * (j + 1), :], Vr[rows, g, :], pT[rows, n % 4, :],
                                                start=False, stop=True, skip_group_check=True,
                                                tile_position=(V32 * j, V32 * j))
                        ins.then_inc(s_pu, 1)

            def close_stage(b, cross):
                pe.wait_ge(s_smu, b * SM_ALL + (SM_ALL if cross else SM_SELF))
                pe.wait_ge(s_ex, b * ST_ALL + (ST_ALL if cross else ST_SELF))
                pe.wait_ge(s_ave, b * 4 * NG + (4 if cross else 2) * NG)
                pe.wait_ge(s_ne, b * 2 * NG + (2 if cross else 1) * NG + START)

            def output(b, o_name, t_name, y_name, w):
                for t in range(T):
                    idx = first(o_name) + t
                    ps = item(b, idx)
                    for g in range(NG):
                        ins = pe.transpose(ps[:, g * P:(g + 1) * P], oT[:, g, t * P:(t + 1) * P], ident[:, :])
                    ins.then_inc(s_item, 1)
                turn_tokens(b, t_name, z, lambda t: pe.wait_ge(s_evd, b * ND + taken("D", first(o_name) + t + 1) + START))
                taken_upto(b, first(t_name) + 4)
                for k in range(4):
                    idx = first(y_name) + k
                    ps = item(b, idx)
                    for t in (2 * k, 2 * k + 1):
                        for c in range(C):
                            ins = pe.matmul(ps[:, (t % 2) * D:(t % 2 + 1) * D], xT[:, c, t * P:(t + 1) * P],
                                            w[:, c, :], start=(c == 0), stop=(c == C - 1))
                    ins.then_inc(s_item, 1)

            pe.wait_ge(s_id, 1)
            pe.wait_ge(s_w, 16 * NW)
            with pe.Fori(0, B) as b:
                pe.wait_ge(s_x, (b + 1) * 64)
                pe.wait_ge(s_eva, b * NA + START)
                pe.wait_ge(s_evd, b * ND + START)
                turn_tokens(b, "xT", x)
                idx = first("ctxT")
                ps = item(b, idx)
                for c in range(C):
                    pe.transpose(ps[:, c * SK:c * SK + P], cx[:, 0, c * P:(c + 1) * P], ident[:, :])
                    ins = pe.transpose(ps[:, c * SK + P:(c + 1) * SK], cx[0:SKR, 1, c * P:(c + 1) * P],
                                       ident[0:SKR, 0:SKR])
                ins.then_inc(s_item, 1)
                taken_upto(b, first("xT") + 4)
                for name, w in (("ctq", wdq), ("ctkv", wdkv)):
                    for half in range(HALVES):
                        project(b, first(name) + half, w, xT, half, 0)
                taken_upto(b, first("ctkv") + 2)
                for i in range(4):
                    m, half = i // 2, i % 2
                    for k, w in enumerate((wqr, wqrs, wuq)):
                        idx = first("q") + 3 * i + k
                        ps = item(b, idx)
                        pe.matmul(ps, w[:, m * P:(m + 1) * P], ctq[:, half * N:(half + 1) * N],
                                  start=True, stop=True).then_inc(s_item, 1)
                for i in range(4):
                    m, half = i // 2, i % 2
                    project(b, first("k") + 3 * i, wkr, xT, half, m)
                    project(b, first("k") + 3 * i + 1, wkrs, xT, half, m)
                    ps = item(b, first("k") + 3 * i + 2)
                    pe.matmul(ps, wuk[:, m * P:(m + 1) * P], ctkv[:, half * N:(half + 1) * N],
                              start=True, stop=True).then_inc(s_item, 1)
                for k in range(4):
                    ps = item(b, first("v") + k)
                    for t in (2 * k, 2 * k + 1):
                        ins = pe.matmul(ps[:, (t % 2) * D:(t % 2 + 1) * D], ctkv[:, t * P:(t + 1) * P], wuv[:, :],
                                        start=True, stop=True)
                    ins.then_inc(s_item, 1)
                ps = item(b, first("kx"))
                for m in range(C):
                    for c in range(C):
                        ins = pe.matmul(ps[:, m * SK:(m + 1) * SK], w1x[:, c, m * P:(m + 1) * P], cxT[:, c, :],
                                        start=(c == 0), stop=(c == C - 1))
                ins.then_inc(s_item, 1)
                ps = item(b, first("vx"))
                for c in range(C):
                    ins = pe.matmul(ps[:, 0:D], cxT[:, c, 0:P], w2x[:, c, :], start=(c == 0), stop=(c == C - 1))
                ins.then_inc(s_item, 1)
                ps = item(b, first("vxr"))
                for j in range(G):
                    for c in range(C):
                        ins = pe.matmul(ps[V32 * j:V32 * j + SKR, 0:D], cxT[:, c, P:SK], w2x[:, c, :],
                                        start=(c == 0), stop=(c == C - 1), tile_position=(0, V32 * j),
                                        skip_group_check=True)
                ins.then_inc(s_item, 1)
                taken_upto(b, len(FRONT))
                attention(b, 0, 0, 0, ORDER_SELF, False)
                close_stage(b, False)
                output(b, "o", "oT", "y", wo)
                pe.wait_ge(s_ln, b * 2 * T + T)
                turn_tokens(b, "x1T", z)
                taken_upto(b, first("x1T") + 4)
                for i in range(4):
                    project(b, first("qx") + i, w0, xT, i % 2, i // 2)
                taken_upto(b, first("qx") + 4)
                pe.wait_ge(s_mask, b + 1 + START)
                attention(b, SM_SELF, ST_SELF, NG, ORDER_CROSS, True)
                close_stage(b, True)
                output(b, "ox", "oxT", "yx", w3)
                pe.wait_ge(s_ln, b * 2 * T + 2 * T)
                turn_tokens(b, "x2T", z)
                taken_upto(b, first("x2T") + 4)
                ps = item(b, first("logit"))
                for t in range(T):
                    for c in range(C):
                        ins = pe.matmul(ps[:, t * E:(t + 1) * E], xT[:, c, t * P:(t + 1) * P], wch[:, c, :],
                                        start=(c == 0), stop=(c == C - 1))
                ins.then_inc(s_item, 1)
            def count(ps, src):
                for t in range(T):
                    ins = pe.matmul(ps, onesb[:, :], src[:, t, :], start=(t == 0), stop=(t == T - 1))
                return ins

            def prefix(src):
                for t in range(T):
                    ps = PS[:, 1, t * BE:(t + 1) * BE]
                    for k in range(t):
                        pe.matmul(ps, onesb[:, :], src[:, k, :], start=(k == 0), stop=False)
                    ins = pe.matmul(ps, tri[:, :], src[:, t, :], start=(t == 0), stop=True)
                return ins

            pe.wait_ge(s_evd, B * ND + START)
            with pe.Fori(0, BITS) as n:
                pe.wait_ge(s_in, n + 1)
                count(PS[:, 0, 0:BE], above).then_inc(s_cn, 1)
            pe.wait_ge(s_in, BITS + 1)
            count(PS[:, 0, 0:BE], above)
            prefix(equal).then_inc(s_cn, 1)
            pe.wait_ge(s_in, BITS + 2)
            prefix(chosen).then_inc(s_cn, 1)
            with pe.Fori(0, BE // 2) as i:
                for k in range(2):
                    pe.wait_ge(s_oh, i * 2 + k + 1)
                    pe.wait_ge(s_pe2, i * 2 + START)
                    for j in range(2):
                        for t in range(T):
                            ins = pe.matmul(PS[:, 2 + k, j * COLS:(j + 1) * COLS],
                                            onehot[k][:, t, j * P:(j + 1) * P],
                                            picks[:, t, bass.ds(i * 2 + k, 1), 0:COLS].rearrange(
                                                "p a c -> p (a c)"),
                                            start=(t == 0), stop=(t == T - 1))
                    ins.then_inc(s_pk, 1)

            def turn_rows(i, u):
                k = u % 2
                pe.wait_ge(s_g[k], i * UNITS * 16 + 32 * (u // 2 + 1))
                pe.wait_ge(s_te, i * UNITS + max(0, u - 1) + START)
                for c in range(C):
                    for j in range(2):
                        ins = pe.transpose(PS[:, k, c * CAP + j * P:c * CAP + (j + 1) * P],
                                           xg[k][:, j, c * P:(c + 1) * P], ident[:, :])
                ins.then_inc(s_gt, 1)

            def hidden(i, u):
                k, eh = u % 2, u // B
                if u % B == 0:
                    pe.wait_ge(s_we[eh], i * 32 + 32)
                pe.wait_ge(s_te, i * UNITS + u + 1 + START)
                pe.wait_ge(s_si, i * UNITS * 2 + 2 * max(0, u - 1) + START)
                for f in range(F // P):
                    for c in range(C):
                        ins = pe.matmul(PS[:, 2 + 2 * k + f // 2, (f % 2) * CAP:(f % 2 + 1) * CAP],
                                        we1[eh][:, c, f * P:(f + 1) * P], xgT[k][:, c, :],
                                        start=(c == 0), stop=(c == C - 1))
                    if f % 2:
                        ins.then_inc(s_h, 1)

            def expert_out(i, u):
                k, eh = u % 2, u // B
                pe.wait_ge(s_si, i * UNITS * 2 + 2 * u + 2 + START)
                pe.wait_ge(s_ye, i * UNITS + max(0, u - 1) + START)
                for j in range(2):
                    for f in range(F // P):
                        ins = pe.matmul(PS[:, 6 + k, j * D:(j + 1) * D], hT[k][:, f, j * P:(j + 1) * P],
                                        we2[eh][:, f, :], start=(f == 0), stop=(f == F // P - 1))
                ins.then_inc(s_y, 1)

            pe.wait_ge(s_pe2, BE + START)
            with pe.Fori(0, E // 2) as i:
                turn_rows(i, 0)
                for u in range(UNITS):
                    if u + 1 < UNITS:
                        turn_rows(i, u + 1)
                    hidden(i, u)
                    if u >= 1:
                        expert_out(i, u - 1)
                expert_out(i, UNITS - 1)


def host_arrays(i):
    pair = np.arange(D) ^ 1
    pos = np.arange(S, dtype=np.float32)[:, None]
    theta = (np.float32(10000.0) ** (np.float32(-2.0) * np.arange(D // 2, dtype=np.float32))
             / np.float32(D // 2)).astype(np.float32)
    r = pos * theta[None, :]
    cos = np.repeat(np.cos(r).T, 2, axis=0)
    sin = np.repeat(np.sin(r).T, 2, axis=0)
    sin[0::2] = -sin[0::2]
    lay = lambda t: np.ascontiguousarray(t.reshape(C, P, S).transpose(1, 0, 2).astype(np.float32))
    col = lambda v: np.asarray(v).reshape(-1, P).T
    g = {k: np.asarray(v) for k, v in i.items()}
    at = lambda n: g["L0_attn_" + n]
    xa = lambda n: g["L0_xattn_" + n]
    bias_columns = np.concatenate([col(at("Wd_q_b")), col(at("Wd_kv_b")),
                                   col(at("Wu_q_b")), col(at("Wq_r_b")), col(at("Wq_r_b")[pair]),
                                   col(at("Wu_k_b")), col(at("Wk_r_b")), col(at("Wk_r_b")[pair]),
                                   col(xa("b1")), col(xa("b0"))], axis=1)
    out = {
        "x": g["x"].reshape(B * S, D), "ctx": g["ctx_1024"].reshape(B * SK, D),
        "mask": g["mask_BxSxS2_if1"].reshape(B * S, SK),
        "bias_columns": bias_columns,
        "bias_rows": np.stack([at("Wu_v_b"), at("Wo_b"), xa("b2"), xa("b3")])[None],
        "cos": lay(cos), "sin": lay(sin),
        "Wd_q": at("Wd_q_w"), "Wd_kv": at("Wd_kv_w"), "Wu_q": at("Wu_q_w"), "Wq_r": at("Wq_r_w"),
        "Wq_r_swapped": at("Wq_r_w")[:, pair], "Wu_k": at("Wu_k_w"), "Wu_v": at("Wu_v_w"),
        "Wk_r": at("Wk_r_w"), "Wk_r_swapped": at("Wk_r_w")[:, pair], "Wo": at("Wo_w"),
        "W0T": xa("W0").T, "W1T": xa("W1").T, "W2T": xa("W2").T, "W3T": xa("W3").T,
        "choiceT": g["L0_ffn_choice_w"].T,
        "w1": g["L0_ffn_w1"], "w2": g["L0_ffn_w2"],
    }
    return {k: np.ascontiguousarray(v) for k, v in out.items()}


def kernel(**inputs):
    import concourse.bacc as _bacc
    from concourse.bass_utils import run_bass_kernel_spmd as _run

    arrays = host_arrays(inputs)
    nc = _bacc.Bacc("TRN2", target_bir_lowering=False, num_devices=1)
    args = {n: nc.dram_tensor(f"in_{n}", v.shape, mybir.dt.from_np(v.dtype), kind="ExternalInput").ap()
            for n, v in arrays.items()}
    out = nc.dram_tensor("out", (B * S, D), F32, kind="ExternalOutput").ap()
    decoder_block(nc, args, out)
    r = _run(nc, [{f"in_{n}": v for n, v in arrays.items()}], core_ids=[0])
    return r.results[0]["out"].reshape(B, S, D)
```

```python
from contextlib import ExitStack

import numpy as np

import concourse.bass as bass
from concourse import mybir

F32 = mybir.dt.float32
BF16 = mybir.dt.bfloat16
I32 = mybir.dt.int32
U32 = mybir.dt.uint32
ALU = mybir.AluOpType
ACT = mybir.ActivationFunctionType
AX = mybir.AxisListType

P = 128
B, S, D = 4, 1024, 256
H = 16
HD = D // H
SK = 154
SKR = SK - P
T = S // P
C = D // P
N = 512
HALVES = S // N
LAT = 128
E, F = 8, 512
CAP = S * 2 // E
EPS = 1e-5
TERMS = [(0, 0), (0, 1), (0, 2), (1, 0), (1, 1), (2, 0)]
KQ = HD * len(TERMS)
KM = KQ + 3
MASKED = -float(2 ** 120)
SCALE_SELF = float(1.0 / np.sqrt(np.float32(H + LAT + LAT)))
SCALE_CROSS = float(1.0 / np.sqrt(np.float32(HD)))
G = 4
NG = H // G
V32 = 32

FRONT = ([("xT", "DA"[n % 2]) for n in range(4)] + [("ctxT", "D")] + [("ctq", "A")] * 2 + [("ctkv", "A")] * 2
         + [("q", "D")] * 12 + [("k", "D")] * 12 + [("v", "D")] * 4 + [("kx", "D"), ("vx", "D"), ("vxr", "D")])
MID = ([("o", "D")] * T + [("oT", "DA"[n % 2]) for n in range(4)] + [("y", "D")] * 4
       + [("x1T", "DA"[n % 2]) for n in range(4)] + [("qx", "D")] * 4)
BACK = ([("ox", "D")] * T + [("oxT", "DA"[n % 2]) for n in range(4)] + [("yx", "D")] * 4
        + [("x2T", "DA"[n % 2]) for n in range(4)] + [("logit", "D")])
ITEMS = FRONT + MID + BACK
STAGE = {**{i: 0 for i in range(len(FRONT))}, **{len(FRONT) + i: len(FRONT) for i in range(len(MID))},
         **{len(FRONT) + len(MID) + i: len(FRONT) + len(MID) for i in range(len(BACK))}}
NI = len(ITEMS)


def first(name):
    return [n for n, _ in ITEMS].index(name)


def taken(engine, upto):
    return sum(e == engine for _, e in ITEMS[:upto])


PIECE = ([first("q") + 3 * i + 2 for i in range(4)] + [first("k") + 3 * i + 2 for i in range(4)] + [first("kx")]
         + [first("qx") + i for i in range(4)])
NA, ND = taken("A", NI), taken("D", NI)
PIECES = 13
PIECES_OF = [7, 6]
SM_SELF, SM_CROSS = H * T * HALVES, H * 3
ST_SELF, ST_CROSS = NG * HALVES * T * G, NG * HALVES * (G + 1)
LAG = 2


def schedule(sm_group, st_group, lead, turn):
    order = []
    total = NG * st_group + sm_group + lead
    for k in range(total + LAG):
        if k < NG * sm_group:
            order.append(("smax", k))
        if k >= sm_group + turn and (k - turn) % sm_group == 0 and (k - turn) // sm_group <= NG:
            order.append(("turn", (k - turn) // sm_group - 1))
        st = k - sm_group - lead
        if 0 <= st < NG * st_group:
            order.append(("st", st))
        if 0 <= st - LAG < NG * st_group:
            order.append(("av", st - LAG))
    return order


TURN_SELF, TURN_CROSS = 6, 4
START = 2
COPIED = 16
BITS = 30
COLS = 5
UNITS = 2 * B
ORDER_SELF = schedule(SM_SELF // NG, ST_SELF // NG, 14, TURN_SELF)
ORDER_CROSS = schedule(SM_CROSS // NG, ST_CROSS // NG, 18, TURN_CROSS)
SM_ALL, ST_ALL = SM_SELF + SM_CROSS, ST_SELF + ST_CROSS


def decoder_block(nc, a, out):
    ctx = ExitStack()
    with ctx:
        def sb(name, shape, dt=F32):
            return ctx.enter_context(nc.sbuf_tensor(name, shape, dt))

        def sem(name):
            return ctx.enter_context(nc.semaphore(name))

        def dram(name, shape, dt):
            return nc.dram_tensor(name, shape, dt, kind="Internal").ap()

        PS = ctx.enter_context(nc.psum_tensor("banks", [P, 8, N], F32))

        q_parts = dram("q_parts", (3, D, S), BF16)
        k_parts = dram("k_parts", (3, D, S), BF16)
        kx_parts = dram("kx_parts", (P, 3, C, SK), BF16)
        x2_rows = dram("x2_rows", (B * S, D), F32)
        acc_rows = dram("acc_rows", (B * S, D), F32)

        ident = sb("ident", [P, P])
        identb = sb("identb", [P, P], BF16)
        tri = sb("tri", [P, P], BF16)
        onesb = sb("onesb", [P, P], BF16)
        iota = sb("iota", [P, CAP], BF16)
        cosT = sb("cosT", [P, C, S])
        sinT = sb("sinT", [P, C, S])
        wdq = sb("wdq", [P, C, LAT])
        wdkv = sb("wdkv", [P, C, LAT])
        wuq = sb("wuq", [P, D])
        wqr = sb("wqr", [P, D])
        wqrs = sb("wqrs", [P, D])
        wuk = sb("wuk", [P, D])
        wuv = sb("wuv", [P, D])
        wkr = sb("wkr", [P, C, D])
        wkrs = sb("wkrs", [P, C, D])
        wo = sb("wo", [P, C, D])
        w0 = sb("w0", [P, C, D])
        w1x = sb("w1x", [P, C, D])
        w2x = sb("w2x", [P, C, D])
        w3 = sb("w3", [P, C, D])
        wch = sb("wch", [P, C, E])
        bcol = sb("bcol", [P, 18])
        brow = sb("brow", [P, 4, D])
        mhalf = sb("mhalf", [P, T])
        oT = sb("oT", [P, NG, S])
        early = oT[:, :, :].rearrange("p g n -> p (g n)")
        x = early[:, 0:T * D].rearrange("p (t d) -> p t d", d=D)
        cx = early[:, T * D:(T + 2) * D].rearrange("p (t d) -> p t d", d=D)
        mask_i = early[:, (T + 2) * D:(T + 2) * D + T * SK].bitcast(I32).rearrange("p (t k) -> p t k", k=SK)
        xT = sb("xT", [P, C, S])
        cxT = sb("cxT", [P, C, SK])
        maskb = sb("maskb", [P, T, 160], BF16)
        pT = sb("pT", [P, 4, N])
        ctq = pT[:, 0:2, :].rearrange("p a n -> p (a n)")
        ctkv = pT[:, 2:4, :].rearrange("p a n -> p (a n)")
        z = sb("z", [P, T, D])
        rotary = z[:, :, :].rearrange("p (a r t) d -> p a r (t d)", a=2, r=2)
        ru, rv = rotary[:, 0], rotary[:, 1]
        iota_f = z[:, 0, :]
        full = sb("full", [P, 2, N])
        rest = sb("rest", [P, 2, N])
        part = sb("part", [P, 2, 3, N], BF16)
        qst = sb("qst", [P, H, S], BF16)
        kst = sb("kst", [P, H, S], BF16)
        kxst = sb("kxst", [P, H, 160], BF16)
        V = sb("V", [P, T, H, V32])
        Vx = sb("Vx", [P, H, V32])
        Vr = sb("Vr", [P, NG, V32])
        mh = sb("mh", [P, 2, T, G, HALVES])
        nmf = sb("nmf", [P, T, G])
        nmr = sb("nmr", [P, T, G])
        nmp = sb("nmp", [P, 2, T, 3 * G], BF16)
        nmT = sb("nmT", [3 * G, 2, S], BF16)
        rz = sb("rz", [P, 2, H])
        xb = sb("xb", [P, T, D])
        st6 = sb("st6", [P, T, 6])
        mv = sb("mv", [P, T, 2])
        ve = sb("ve", [P, T])
        rstd = sb("rstd", [P, T])
        lg = sb("lg", [P, T, E])
        lgm = sb("lgm", [P, T])
        lge = sb("lge", [P, T, E])
        lgs = sb("lgs", [P, T])
        prob = sb("prob", [P, T, B * E])

        q_room = qst[:, :, :].rearrange("p h n -> p (h n)").bitcast(F32)
        k_room = kst[:, :, :].rearrange("p h n -> p (h n)").bitcast(F32)
        v_room = V[:, :, :, :].rearrange("p t h n -> p (t h n)")
        we1 = [q_room[:, 2048 * i:2048 * i + 1024].rearrange("p (c f) -> p c f", c=C) for i in range(2)]
        we2 = [q_room[:, 2048 * i + 1024:2048 * i + 2048].rearrange("p (c d) -> p c d", d=D) for i in range(2)]
        used = [0]

        def room(words):
            used[0] += words
            return k_room[:, used[0] - words:used[0]]

        xg = [room(2 * D).rearrange("p (j d) -> p j d", d=D) for _ in range(B)]
        xgT = [room(C * CAP).rearrange("p (c j) -> p c j", j=CAP) for _ in range(2)]
        hT = [room(F // P * CAP).rearrange("p (f j) -> p f j", j=CAP) for _ in range(2)]
        yg = [room(2 * D).rearrange("p (j d) -> p j d", d=D) for _ in range(B)]
        vused = [0]

        def vroom(words):
            vused[0] += words
            return v_room[:, vused[0] - words:vused[0]]

        BE = B * E
        by_tile = lambda ap: ap.rearrange("p (t n) -> p t n", n=BE)
        onehot = [vroom(T * CAP // 2).bitcast(BF16).rearrange("p (t j) -> p t j", j=CAP) for _ in range(2)]
        picks = vroom(T * BE * 6 // 2).bitcast(BF16).rearrange("p (t n k) -> p t n k", n=BE, k=6)
        pos = by_tile(vroom(T * BE))
        above = by_tile(vroom(T * BE // 2).bitcast(BF16))
        equal = by_tile(vroom(T * BE // 2).bitcast(BF16))
        chosen = by_tile(vroom(T * BE // 2).bitcast(BF16))
        picked = sb("picked", [P, B, 2, COLS])
        thr = vroom(BE)
        cand = vroom(BE)
        bit = vroom(BE)
        hit = vroom(BE)
        tokf = vroom(B * 2)
        tok_g = [sb(f"tok_g{i}", [P, B, 2], U32) for i in range(2)]
        tok_s = [sb(f"tok_s{i}", [P, B, 2], U32) for i in range(2)]
        gate = [sb(f"gate{i}", [P, B, 2]) for i in range(2)]
        lane = sb("lane", [P, 1])

        s_r = sem("routing_step")
        s_cn = sem("count_ready")
        s_in = sem("indicator_ready")
        s_oh = sem("onehot_ready")
        s_pk = sem("picked")
        s_pe2 = sem("picked_taken")
        s_tk = sem("gather_tokens_ready")
        s_g = [sem(f"gathered{i}") for i in range(B)]
        s_gt = sem("gathered_turned")
        s_te = sem("gathered_turned_taken")
        s_h = sem("hidden_ready")
        s_si = sem("silu_ready")
        s_y = sem("expert_output_ready")
        s_ye = sem("expert_output_gated")
        s_sc = [sem(f"scattered{i}") for i in range(B)]
        s_we = [sem(f"expert_weights{i}") for i in range(2)]
        s_al = [sem(f"sum_loaded{i}") for i in range(B)]
        s_fz = sem("final_stats")
        s_fr = sem("final_rstd")
        s_fb = sem("final_shift")
        s_fl = sem("final_layernorm")
        s_out = sem("out_stored")
        late = early.rearrange("p (b t d) -> p b t d", b=2, d=D)
        fin = [z, xb, late[:, 0], late[:, 1]]
        fmv = sb("fmv", [P, B, T, 2])
        frstd = sb("frstd", [P, B, T])
        fshift = sb("fshift", [P, B, T])

        s_w = sem("weights_loaded")
        s_x = sem("x_loaded")
        s_id = sem("identities_ready")
        s_pool = sem("pool_chain")
        s_dve = sem("dve_chain")
        s_act = sem("act_chain")
        s_item = sem("product_ready")
        s_evd = sem("product_taken_by_dve")
        s_eva = sem("product_taken_by_act")
        s_mask = sem("mask_ready")
        s_xb = sem("residual_ready")
        s_p1 = sem("part1_ready")
        s_p2 = sem("rest_ready")
        s_p3 = sem("part2_ready")
        s_p4 = sem("parts_ready")
        s_pw = [sem(f"parts_stored{i}") for i in range(2)]
        s_ql = [sem(f"q_stack_loaded{i}") for i in range(2)]
        s_kl = [sem(f"k_stack_loaded{i}") for i in range(2)]
        s_kx = sem("kx_stack_loaded")
        s_sm = sem("max_scores_ready")
        s_smu = sem("max_scores_used")
        s_nm = sem("minus_max_ready")
        s_nt = sem("minus_max_turned")
        s_ne = sem("minus_max_rows_ready")
        s_nl = [sem(f"minus_max_loaded{i}") for i in range(2)]
        s_st = sem("scores_ready")
        s_ex = sem("exp_ready")
        s_pu = sem("exp_used")
        s_ave = sem("values_taken")
        s_z = sem("stats_ready")
        s_rs = sem("rstd_ready")
        s_ln = sem("layernorm_ready")
        s_le = sem("logits_exp")
        s_x2 = sem("x2_stored")

        blk = ctx.enter_context(nc.Block())
        bank = lambda idx: (idx - STAGE[idx]) % 8

        ROWS_P = lambda ap: ap.rearrange("(t p) d -> p t d", p=P)
        NW = 19

        def wait(eng, semaphore, value):
            eng.wait_ge(semaphore, value)

        def wait_apart(eng, *waits):
            values = [v if isinstance(v, int) else eng.to_reg(v) for v in waits[1::2]]
            eng.wait_ge(s_id, 1)
            for semaphore, value in zip(waits[0::2], values):
                eng.wait_ge(semaphore, value)

        from_one = [s_xb, s_item, s_mask, s_p2, s_evd, s_eva, s_x2, s_nt, s_ne, s_gt, s_y, s_si, s_te, s_ye,
                    s_pk, s_pe2] + s_pw + s_nl

        @blk.sync
        def _(sp):
            for semaphore in from_one:
                sp.sem_inc(semaphore, START)
            for dst, src in [
                (bcol[:, :], a["bias_columns"]), (wdq[:, :, :], a["Wd_q"].rearrange("(c p) n -> p c n", p=P)),
                (wdkv[:, :, :], a["Wd_kv"].rearrange("(c p) n -> p c n", p=P)), (wuq[:, :], a["Wu_q"]),
                (wqr[:, :], a["Wq_r"]), (wqrs[:, :], a["Wq_r_swapped"]), (cosT[:, :, :], a["cos"]),
                (sinT[:, :, :], a["sin"]), (wuk[:, :], a["Wu_k"]), (wuv[:, :], a["Wu_v"]),
                (wkr[:, :, :], a["Wk_r"].rearrange("(c p) n -> p c n", p=P)),
                (wkrs[:, :, :], a["Wk_r_swapped"].rearrange("(c p) n -> p c n", p=P)),
                (brow[:, :, :], a["bias_rows"].rearrange("a r d -> a (r d)").to_broadcast([P, 4 * D])
                 .rearrange("p (r d) -> p r d", r=4)),
                (w1x[:, :, :], a["W1T"].rearrange("(c p) n -> p c n", p=P)),
                (w2x[:, :, :], a["W2T"].rearrange("(c p) n -> p c n", p=P)),
                (wo[:, :, :], a["Wo"].rearrange("(c p) n -> p c n", p=P)),
                (w0[:, :, :], a["W0T"].rearrange("(c p) n -> p c n", p=P)),
                (w3[:, :, :], a["W3T"].rearrange("(c p) n -> p c n", p=P)),
                (wch[:, :, :], a["choiceT"].rearrange("(c p) n -> p c n", p=P)),
            ]:
                sp.dma_start(dst, src).then_inc(s_w, 16)

            def store_piece(b, i, dst, cols):
                sp.wait_ge(s_p4, b * PIECES + i + 1)
                src = part[:, i % 2, :, 0:cols]
                sp.dma_start(dst, src).then_inc(s_pw[i % 2], 16)

            def stored(b, i):
                wait_apart(sp, s_pw[0], 16 * (b * PIECES_OF[0] + (i + 2) // 2) + START,
                           s_pw[1], 16 * (b * PIECES_OF[1] + (i + 1) // 2) + START)

            def load_stack(dst, parts, mc, which, s):
                for t, term in enumerate(TERMS):
                    src = parts[term[which], mc * P:(mc + 1) * P, :].rearrange("(h d) n -> d h n", d=HD)
                    sp.dma_start(dst[t * HD:(t + 1) * HD, mc * 8:(mc + 1) * 8, :], src).then_inc(s, 16)

            def load_minus_max(b, n, g):
                sp.wait_ge(s_ne, b * 2 * NG + n + 1 + START)
                for p in range(3):
                    sp.dma_start(qst[KQ + p:KQ + p + 1, g * G:(g + 1) * G, :],
                                 nmT[p * G:(p + 1) * G, n % 2, :]).then_inc(s_nl[n % 2], 16)

            with sp.Fori(0, B) as b:
                wait_apart(sp, s_xb, b * 2 + START, s_item, b * NI + START)
                sp.dma_start(x[:, :, :], ROWS_P(a["x"][bass.ds(b * S, S), :])).then_inc(s_x, 16)
                sp.dma_start(cx[:, 0, :], a["ctx"][bass.ds(b * SK, P), :]).then_inc(s_x, 16)
                sp.dma_start(cx[0:SKR, 1, :], a["ctx"][bass.ds(b * SK + P, SKR), :]).then_inc(s_x, 16)
                sp.wait_ge(s_mask, b + START)
                sp.dma_start(mask_i[:, :, :],
                             a["mask"][bass.ds(b * S, S), :].rearrange("(t p) d -> p t d", p=P)).then_inc(s_x, 16)
                for i in range(8):
                    parts = q_parts if i < 4 else k_parts
                    mc, half = (i % 4) // 2, i % 2
                    store_piece(b, i, parts[:, mc * P:(mc + 1) * P, half * N:(half + 1) * N]
                                .rearrange("k p n -> p k n"), N)
                    if i % 2:
                        stored(b, i)
                        if i < 4:
                            load_stack(qst, q_parts, mc, 0, s_ql[mc])
                        else:
                            load_stack(kst, k_parts, mc, 1, s_kl[mc])
                store_piece(b, 8, kx_parts.rearrange("p k c n -> p k (c n)"), C * SK)
                stored(b, 8)
                for c in range(C):
                    for t, term in enumerate(TERMS):
                        src = kx_parts[:, term[1], c, :].rearrange("(h d) n -> d h n", d=HD)
                        sp.dma_start(kxst[t * HD:(t + 1) * HD, c * 8:(c + 1) * 8, 0:SK], src).then_inc(s_kx, 16)
                for g in range(NG):
                    load_minus_max(b, g, g)
                for i in range(9, 13):
                    mc, half = (i - 9) // 2, (i - 9) % 2
                    if i == 9:
                        wait_apart(sp, s_ql[0], b * 192 + 96, s_ql[1], b * 192 + 96)
                    store_piece(b, i, q_parts[:, mc * P:(mc + 1) * P, half * N:(half + 1) * N]
                                .rearrange("k p n -> p k n"), N)
                    if i % 2 == 0:
                        stored(b, i)
                        load_stack(qst, q_parts, mc, 0, s_ql[mc])
                for g in range(NG):
                    load_minus_max(b, NG + g, g)
                wait_apart(sp, s_ln, (b * 2 + 2) * T)
                sp.dma_start(ROWS_P(x2_rows[bass.ds(b * S, S), :]), z[:, :, :]).then_inc(s_x2, 16)
                wait_apart(sp, s_ql[0], b * 192 + 192, s_ql[1], b * 192 + 192, s_kl[0], b * 96 + 96,
                           s_kl[1], b * 96 + 96, s_kx, b * 192 + 192)
            sp.wait_ge(s_pu, B * ST_ALL)

            def load_expert(e, i):
                sp.dma_start(we1[i], a["w1"][bass.ds(e, 1), :, :].rearrange("a (c p) f -> p (a c) f", p=P)
                             ).then_inc(s_we[i], 16)
                sp.dma_start(we2[i], a["w2"][bass.ds(e, 1), :, :].rearrange("a (c p) d -> p (a c) d", p=P)
                             ).then_inc(s_we[i], 16)

            load_expert(0, 0)
            load_expert(1, 1)
            with sp.Fori(0, E // 2 - 1) as i:
                for half in range(2):
                    wait_apart(sp, s_y, i * UNITS + B * (half + 1) + START)
                    load_expert(i * 2 + 2 + half, half)
            for b in range(B):
                sp.wait_ge(s_sc[b], E * 32 + COPIED)
                sp.dma_start(fin[b][:, :, :], ROWS_P(acc_rows[b * S:(b + 1) * S, :])).then_inc(s_al[b], 16)
            for b in range(B):
                sp.wait_ge(s_fl, b + 1)
                sp.dma_start(ROWS_P(out[b * S:(b + 1) * S, :]), fin[b][:, :, :]).then_inc(s_out, 16)
            sp.wait_ge(s_out, B * 16)
            sp.wait_ge(s_x2, B * 16 + START)

        @blk.gpsimd
        def _(pool):
            steps = [0]

            def link(ins):
                steps[0] += 1
                ins.then_inc(s_pool, 1)
                pool.wait_ge(s_pool, steps[0])

            link(pool.memset(ident[:, :], 0.0))
            link(pool.affine_select(out=ident[:, :], in_=ident[:, :], compare_op=ALU.not_equal, fill=1.0,
                                    base=0, pattern=[[-1, P]], channel_multiplier=1))
            link(pool.memset(tri[:, :], 0.0))
            link(pool.affine_select(out=tri[:, :], in_=tri[:, :], compare_op=ALU.is_ge, fill=1.0,
                                    base=0, pattern=[[-1, P]], channel_multiplier=1))
            link(pool.iota(iota_f, pattern=[[1, CAP]], base=0, channel_multiplier=0,
                           allow_small_or_imprecise_dtypes=True))
            link(pool.tensor_copy(iota[:, :], iota_f))
            link(pool.tensor_copy(identb[:, :], ident[:, :]))
            link(pool.memset(onesb[:, :], 1.0))
            link(pool.memset(mhalf[:, :], -0.5))
            link(pool.memset(kst[:, :, :], 1.0))
            link(pool.memset(qst[:, :, :], 0.0))
            link(pool.memset(kxst[:, :, :], 1.0))
            link(pool.memset(kxst[0:KQ, :, SK:160], 0.0))
            link(pool.memset(maskb[:, :, :], MASKED))
            for tile in (V[:, :, :, :], Vx[:, :, :], Vr[:, :, :]):
                link(pool.memset(tile, 0.0))
            link(pool.memset(V[:, :, :, HD:HD + 1], 1.0))
            link(pool.memset(Vx[:, :, HD:HD + 1], 1.0))
            link(pool.iota(lane[:, :], pattern=[[0, 1]], base=0, channel_multiplier=1,
                           allow_small_or_imprecise_dtypes=True))
            pool.memset(Vr[:, :, HD:HD + 1], 1.0).then_inc(s_id, 1)
            pool.wait_ge(s_w, 16 * NW)

            def split(b, i, cols):
                p = i % 2
                pool.wait_ge(s_p1, b * PIECES + i + 1)
                pool.tensor_tensor(rest[:, p, 0:cols], full[:, p, 0:cols], part[:, p, 0, 0:cols],
                                   ALU.subtract).then_inc(s_p2, 1)
                pool.wait_ge(s_p3, b * PIECES + i + 1)
                pool.tensor_tensor(part[:, p, 2, 0:cols], rest[:, p, 0:cols], part[:, p, 1, 0:cols],
                                   ALU.subtract).then_inc(s_p4, 1)

            def rsqrt(b, n):
                pool.wait_ge(s_z, b * 2 + n + 1)
                pool.tensor_tensor(rstd[:, :], ve[:, :], mhalf[:, :], ALU.pow).then_inc(s_rs, 1)

            with pool.Fori(0, B) as b:
                pool.wait_ge(s_x, (b + 1) * 64)
                pool.wait_ge(s_evd, b * ND + START)
                pool.tensor_tensor(xb[:, :, :], x[:, :, :], brow[:, 1:2, :].to_broadcast([P, T, D]),
                                   ALU.add).then_inc(s_xb, 1)
                pool.tensor_scalar(maskb[:, :, 0:SK], mask_i[:, :, :], 0.0, MASKED, ALU.is_equal,
                                   ALU.mult).then_inc(s_mask, 1)
                for i in range(9):
                    split(b, i, C * SK if i == 8 else N)
                rsqrt(b, 0)
                pool.wait_ge(s_ln, b * 2 * T + T)
                pool.tensor_tensor(xb[:, :, :], z[:, :, :], brow[:, 3:4, :].to_broadcast([P, T, D]),
                                   ALU.add).then_inc(s_xb, 1)
                for i in range(9, 13):
                    split(b, i, N)
                rsqrt(b, 1)

            pool.wait_ge(s_x2, B * 16 + START)

            for b in range(B):
                rows = slice(b * S, (b + 1) * S)
                pool.dma_start(acc_rows[rows, :], x2_rows[rows, :]).then_inc(s_sc[b], COPIED)
            for b in range(B):
                pool.wait_ge(s_sc[b], COPIED)

            def gather(b, half):
                for j in range(2):
                    pool.indirect_dma_start(xg[b][:, j, :], None, x2_rows,
                                            bass.IndirectOffsetOnAxis(tok_g[half][:, b, j:j + 1], 0)
                                            ).then_inc(s_g[b], 16)

            def scatter(b, half):
                for j in range(2):
                    pool.indirect_dma_start(acc_rows, bass.IndirectOffsetOnAxis(tok_s[half][:, b, j:j + 1], 0),
                                            yg[b][:, j, :], None, compute_op=ALU.add).then_inc(s_sc[b], 16)

            def experts(i, last):
                for u in range(UNITS):
                    half, b = divmod(u, B)
                    more = not (last and half == 1)
                    if b == 0:
                        wait_apart(pool, s_tk, i * 4 + half * 2 + (3 if more else 2))
                    if more:
                        wait_apart(pool, s_gt, i * UNITS + u + 1 + START)
                        gather(b, 1 - half)
                    wait_apart(pool, s_ye, i * UNITS + u + 1 + START, s_sc[b], (i * 2 + half) * 32 + COPIED)
                    scatter(b, half)

            pool.wait_ge(s_tk, 1)
            for b in range(B):
                gather(b, 0)
            with pool.Fori(0, E // 2 - 1) as i:
                experts(i, False)
            experts(E // 2 - 1, True)
            for b in range(B):
                pool.wait_ge(s_fz, b + 1)
                pool.tensor_tensor(frstd[:, b, :], frstd[:, b, :], mhalf[:, :], ALU.pow).then_inc(s_fr, 1)

        @blk.scalar
        def _(act):
            def taken_before(b, idx):
                act.wait_ge(s_item, b * NI + idx + 1 + START)

            def copy_item(b, idx, dst, cols=N):
                taken_before(b, idx)
                act.activation(dst, PS[:, bank(idx), 0:cols], ACT.Copy).then_inc(s_eva, 1)

            def part1(b, i, cols):
                p = i % 2
                act.wait_ge(s_evd, b * ND + taken("D", PIECE[i] + 1) + START)
                act.wait_ge(s_pw[p], 16 * (b * PIECES_OF[p] + (i // 2)) + START)
                act.activation(part[:, p, 0, 0:cols], full[:, p, 0:cols], ACT.Copy).then_inc(s_p1, 1)

            def part2(b, i, cols):
                p = i % 2
                act.wait_ge(s_p2, b * PIECES + i + 1 + START)
                act.activation(part[:, p, 1, 0:cols], rest[:, p, 0:cols], ACT.Copy).then_inc(s_p3, 1)

            def attention(b, n0, units, group, scale):
                per = group // HALVES
                for n in range(units + LAG):
                    if n < units:
                        act.wait_ge(s_st, b * ST_ALL + n0 + n + 1)
                        if n0 + n >= 4:
                            act.wait_ge(s_pu, b * ST_ALL + n0 + n - 3)
                        act.activation(pT[:, n % 4, :], PS[:, 3 + n % 2, :], ACT.Exp,
                                       scale=scale).then_inc(s_ex, 1)
                    m = n - LAG
                    if m >= 0 and m % per == per - 1:
                        k = m // per
                        act.wait_ge(s_pu, b * ST_ALL + n0 + m + 1)
                        if n0 == 0 and k == 0:
                            act.wait_ge(s_mask, b + 1 + START)
                            act.wait_ge(s_xb, b * 2 + 1 + START)
                        act.activation(oT[:, k // 2, (k % 2) * N:(k % 2 + 1) * N], PS[:, 5 + k % 2, :],
                                       ACT.Copy).then_inc(s_ave, 1)

            act.wait_ge(s_w, 16 * NW)
            with act.Fori(0, B) as b:
                f = first("xT")
                for n in (1, 3):
                    copy_item(b, f + n, xT[:, n // 2, (n % 2) * N:(n % 2 + 1) * N])
                for name, dst, col in (("ctq", ctq, 0), ("ctkv", ctkv, 1)):
                    for half in range(HALVES):
                        idx = first(name) + half
                        taken_before(b, idx)
                        act.activation(dst[:, half * N:(half + 1) * N], PS[:, bank(idx), :], ACT.Identity,
                                       bias=bcol[:, col:col + 1]).then_inc(s_eva, 1)
                for i in range(10):
                    if i < 9:
                        part1(b, i, C * SK if i == 8 else N)
                    if i >= 1:
                        part2(b, i - 1, C * SK if i == 9 else N)
                attention(b, 0, ST_SELF, ST_SELF // NG, SCALE_SELF)
                for n in (1, 3):
                    copy_item(b, first("oT") + n, xT[:, n // 2, (n % 2) * N:(n % 2 + 1) * N])
                for n in (1, 3):
                    copy_item(b, first("x1T") + n, xT[:, n // 2, (n % 2) * N:(n % 2 + 1) * N])
                for i in range(9, 14):
                    if i < 13:
                        part1(b, i, N)
                    if i >= 10:
                        part2(b, i - 1, N)
                attention(b, ST_SELF, ST_CROSS, ST_CROSS // NG, SCALE_CROSS)
                for n in (1, 3):
                    copy_item(b, first("oxT") + n, xT[:, n // 2, (n % 2) * N:(n % 2 + 1) * N])
                for n in (1, 3):
                    copy_item(b, first("x2T") + n, xT[:, n // 2, (n % 2) * N:(n % 2 + 1) * N])
                act.wait_ge(s_evd, b * ND + ND + START)
                act.activation(lge[:, :, :], lg[:, :, :], ACT.Exp).then_inc(s_le, 1)
            with act.Fori(0, E // 2) as i:
                for u in range(UNITS):
                    k = u % 2
                    act.wait_ge(s_y, i * UNITS + u - 1 + START)
                    for fh in range(2):
                        act.wait_ge(s_h, i * UNITS * 2 + 2 * u + fh + 1)
                        act.activation(hT[k][:, 2 * fh:2 * fh + 2, :].rearrange("p f j -> p (f j)"),
                                       PS[:, 2 + 2 * k + fh, :], ACT.Silu).then_inc(s_si, 1)
            for b in range(B):
                act.wait_ge(s_fb, b + 1)
                for t in range(T):
                    ins = act.activation(fin[b][:, t, :], fin[b][:, t, :], ACT.Identity,
                                         bias=fshift[:, b, t:t + 1], scale=frstd[:, b, t:t + 1])
                ins.then_inc(s_fl, 1)

        DVE_STEPS = 8 + NG * (4 + 3) + 2 * (T + 2) + 4

        @blk.vector
        def _(dve):
            steps = [0]

            def link(b, ins, how=wait):
                steps[0] += 1
                ins.then_inc(s_dve, 1)
                how(dve, s_dve, b * DVE_STEPS + steps[0])

            def ready(b, idx):
                dve.wait_ge(s_item, b * NI + idx + 1 + START)

            def copy_item(b, idx, dst, cols=N):
                ready(b, idx)
                dve.tensor_copy(dst, PS[:, bank(idx), 0:cols]).then_inc(s_evd, 1)

            def full_free(b, i):
                dve.wait_ge(s_p2, b * PIECES + max(0, i - 1) + START)

            def roped(b, i, idx, c0):
                p, mc, half = i % 2, (i % 4) // 2, i % 2
                cols = slice(half * N, (half + 1) * N)
                c0 += mc
                ready(b, idx)
                dve.scalar_tensor_tensor(out=ru[:, p, :], in0=PS[:, bank(idx), :], scalar=bcol[:, c0 + 2:c0 + 3],
                                         in1=cosT[:, mc, cols], op0=ALU.add, op1=ALU.mult).then_inc(s_evd, 1)
                ready(b, idx + 1)
                dve.scalar_tensor_tensor(out=rv[:, p, :], in0=PS[:, bank(idx + 1), :],
                                         scalar=bcol[:, c0 + 4:c0 + 5], in1=sinT[:, mc, cols],
                                         op0=ALU.add, op1=ALU.mult).then_inc(s_evd, 1)
                dve.wait_ge(s_evd, b * ND + taken("D", idx + 2) + START)
                link(b, dve.tensor_tensor(ru[:, p, :], ru[:, p, :], rv[:, p, :], ALU.add))
                full_free(b, i)
                ready(b, idx + 2)
                dve.scalar_tensor_tensor(out=full[:, p, :], in0=PS[:, bank(idx + 2), :],
                                         scalar=bcol[:, c0:c0 + 1], in1=ru[:, p, :],
                                         op0=ALU.add, op1=ALU.add).then_inc(s_evd, 1)

            def attention(b, n0, g0, order, cross):
                sm_group = (SM_CROSS if cross else SM_SELF) // NG
                for what, n in order:
                    if what == "smax":
                        dve.wait_ge(s_sm, b * SM_ALL + n0 + n + 1)
                        g, k = divmod(n, sm_group)
                        if cross:
                            j, t0, nt = k // 3, 3 * (k % 3), min(3, T - 3 * (k % 3))
                            dve.tensor_reduce(nmf[:, t0:t0 + nt, j:j + 1],
                                              PS[:, n % 3, 0:nt * SK].rearrange("p (t k) -> p t k", k=SK),
                                              AX.X, ALU.max, negate=True).then_inc(s_smu, 1)
                        else:
                            j, t, half = k // (T * HALVES), k // HALVES % T, k % HALVES
                            dve.tensor_reduce(mh[:, 0, t, j, half:half + 1], PS[:, n % 3, :],
                                              AX.X, ALU.max).then_inc(s_smu, 1)
                        if k == sm_group - 1:
                            p = (g0 + g) % 2
                            dve.wait_ge(s_smu, b * SM_ALL + n0 + n + 1)
                            if not cross:
                                link(b, dve.tensor_reduce(nmf[:, :, :], mh[:, 0, :, :, :], AX.X, ALU.max,
                                                          negate=True))
                            dve.wait_ge(s_nt, b * 2 * NG + max(0, g0 + g - 1) + START)
                            link(b, dve.tensor_copy(nmp[:, p, :, 0:G], nmf[:, :, :]))
                            link(b, dve.tensor_tensor(nmr[:, :, :], nmf[:, :, :], nmp[:, p, :, 0:G],
                                                      ALU.subtract))
                            link(b, dve.tensor_copy(nmp[:, p, :, G:2 * G], nmr[:, :, :]))
                            dve.tensor_tensor(nmp[:, p, :, 2 * G:3 * G], nmr[:, :, :], nmp[:, p, :, G:2 * G],
                                              ALU.subtract).then_inc(s_nm, 1)
                    elif what == "turn":
                        dve.wait_ge(s_nt, b * 2 * NG + g0 + n + 1 + START)
                        m = g0 + n
                        dve.wait_ge(s_nl[m % 2], 48 * (b * NG + m // 2) + START)
                        dve.tensor_copy(nmT[:, m % 2, :], PS[0:3 * G, 7, :].bitcast(BF16)).then_inc(s_ne, 1)

            def heads_out(b, name):
                if name == "ox":
                    dve.wait_ge(s_xb, b * 2 + 2 + START)
                for t in range(T):
                    idx = first(name) + t
                    ready(b, idx)
                    heads = PS[:, bank(idx), :].rearrange("p (h k) -> p h k", k=V32)
                    link(b, dve.reciprocal(rz[:, t % 2, :], heads[:, :, HD]))
                    dve.tensor_tensor(z[:, t, :].rearrange("p (h k) -> p h k", k=HD), heads[:, :, 0:HD],
                                      rz[:, t % 2, :].rearrange("p (h k) -> p h k", k=1).to_broadcast([P, H, HD]),
                                      ALU.mult).then_inc(s_evd, 1)

            def layernorm(b, name, n):
                for k in range(4):
                    idx = first(name) + k
                    ready(b, idx)
                    dve.tensor_tensor(z[:, 2 * k:2 * k + 2, :],
                                      PS[:, bank(idx), :].rearrange("p (t d) -> p t d", t=2),
                                      xb[:, 2 * k:2 * k + 2, :], ALU.add).then_inc(s_evd, 1)
                    dve.wait_ge(s_evd, b * ND + taken("D", idx + 1) + START)
                    for t in (2 * k, 2 * k + 1):
                        ins = dve.bn_stats(st6[:, t, :], z[:, t, :])
                link(b, ins, wait_apart)
                for t in range(T):
                    ins = dve.bn_aggr(mv[:, t, :], st6[:, t, :])
                link(b, ins)
                dve.tensor_scalar(ve[:, :], mv[:, :, 1], EPS, None, ALU.add).then_inc(s_z, 1)
                dve.wait_ge(s_rs, b * 2 + n + 1)
                for t in range(T):
                    dve.tensor_scalar(z[:, t, :], z[:, t, :], mv[:, t, 0:1], rstd[:, t:t + 1],
                                      ALU.subtract, ALU.mult).then_inc(s_ln, 1)

            dve.wait_ge(s_w, 16 * NW)
            dve.wait_ge(s_id, 1)
            with dve.Fori(0, B) as b:
                for n in (0, 2):
                    copy_item(b, first("xT") + n, xT[:, n // 2, (n % 2) * N:(n % 2 + 1) * N])
                copy_item(b, first("ctxT"), cxT[:, :, :].rearrange("p c n -> p (c n)"), C * SK)
                dve.wait_ge(s_x2, b * 16 + START)
                for i in range(4):
                    roped(b, i, first("q") + 3 * i, 2)
                for i in range(4):
                    roped(b, 4 + i, first("k") + 3 * i, 8)
                for k in range(4):
                    idx = first("v") + k
                    ready(b, idx)
                    for t in range(2):
                        ins = dve.tensor_tensor(
                            V[:, 2 * k + t, :, 0:HD],
                            PS[:, bank(idx), t * D:(t + 1) * D].rearrange("p (h d) -> p h d", d=HD),
                            brow[:, 0, :].rearrange("p (h d) -> p h d", d=HD), ALU.add)
                    ins.then_inc(s_evd, 1)
                idx = first("kx")
                ready(b, idx)
                full_free(b, 8)
                for c in range(C):
                    ins = dve.tensor_scalar(full[:, 0, c * SK:(c + 1) * SK], PS[:, bank(idx), c * SK:(c + 1) * SK],
                                            bcol[:, 14 + c:15 + c], None, ALU.add)
                ins.then_inc(s_evd, 1)
                idx = first("vx")
                ready(b, idx)
                dve.tensor_tensor(Vx[:, :, 0:HD], PS[:, bank(idx), 0:D].rearrange("p (h d) -> p h d", d=HD),
                                  brow[:, 2, :].rearrange("p (h d) -> p h d", d=HD), ALU.add).then_inc(s_evd, 1)
                idx = first("vxr")
                ready(b, idx)
                for j in range(G):
                    rows = slice(V32 * j, V32 * j + SKR)
                    ins = dve.tensor_tensor(
                        Vr[rows, :, 0:HD],
                        PS[rows, bank(idx), 0:D].rearrange("p (g j d) -> p g j d", j=G, d=HD)[:, :, j, :],
                        brow[rows, 2, :].rearrange("p (g j d) -> p g j d", j=G, d=HD)[:, :, j, :], ALU.add)
                ins.then_inc(s_evd, 1)
                attention(b, 0, 0, ORDER_SELF, False)
                heads_out(b, "o")
                for n in (0, 2):
                    copy_item(b, first("oT") + n, xT[:, n // 2, (n % 2) * N:(n % 2 + 1) * N])
                layernorm(b, "y", 0)
                for n in (0, 2):
                    copy_item(b, first("x1T") + n, xT[:, n // 2, (n % 2) * N:(n % 2 + 1) * N])
                for i in range(9, 13):
                    idx = first("qx") + i - 9
                    ready(b, idx)
                    full_free(b, i)
                    c = (i - 9) // 2
                    dve.tensor_scalar(full[:, i % 2, :], PS[:, bank(idx), :], bcol[:, 16 + c:17 + c], None,
                                      ALU.add).then_inc(s_evd, 1)
                attention(b, SM_SELF, NG, ORDER_CROSS, True)
                heads_out(b, "ox")
                for n in (0, 2):
                    copy_item(b, first("oxT") + n, xT[:, n // 2, (n % 2) * N:(n % 2 + 1) * N])
                layernorm(b, "yx", 1)
                for n in (0, 2):
                    copy_item(b, first("x2T") + n, xT[:, n // 2, (n % 2) * N:(n % 2 + 1) * N])
                idx = first("logit")
                ready(b, idx)
                lgp = PS[:, bank(idx), 0:T * E].rearrange("p (t e) -> p t e", e=E)
                link(b, dve.tensor_reduce(lgm[:, :], lgp, AX.X, ALU.max))
                dve.tensor_tensor(lg[:, :, :], lgp,
                                  lgm[:, :].rearrange("p (t e) -> p t e", e=1).to_broadcast([P, T, E]),
                                  ALU.subtract).then_inc(s_evd, 1)
                dve.wait_ge(s_le, b + 1)
                link(b, dve.tensor_reduce(lgs[:, :], lge[:, :, :], AX.X, ALU.add))
                link(b, dve.reciprocal(lgm[:, :], lgs[:, :]))
                link(b, dve.tensor_tensor(prob[:, :, bass.ds(b * E, E)], lge[:, :, :],
                                          lgm[:, :].rearrange("p (t e) -> p t e", e=1).to_broadcast([P, T, E]),
                                          ALU.mult))
            assert steps[0] == DVE_STEPS

            made = [0]

            def link_r(ins):
                made[0] += 1
                ins.then_inc(s_r, 1)
                dve.wait_ge(s_r, made[0])

            def over_tiles(ap):
                return ap.rearrange("p (t n) -> p t n", t=1).to_broadcast([P, T, BE])

            def per_expert(ap):
                return PS[:, ap, 0:BE]

            dve.wait_ge(s_pu, B * ST_ALL)
            link_r(dve.memset(thr.bitcast(I32), 0))
            link_r(dve.memset(bit.bitcast(I32), 1 << (BITS - 1)))
            before = made[0]
            with dve.Fori(0, BITS) as n:
                dve.tensor_tensor(cand.bitcast(I32), thr.bitcast(I32), bit.bitcast(I32),
                                  ALU.bitwise_or).then_inc(s_r, 1)
                dve.wait_ge(s_r, n * 3 + before + 1)
                dve.tensor_tensor(above[:, :, :], prob[:, :, :], over_tiles(cand), ALU.is_ge).then_inc(s_in, 1)
                dve.tensor_scalar(bit.bitcast(I32), bit.bitcast(I32), 1, None,
                                  ALU.logical_shift_right)
                dve.wait_ge(s_cn, n + 1)
                dve.scalar_tensor_tensor(out=hit, in0=PS[:, 0, 0:BE], scalar=float(CAP), in1=cand,
                                         op0=ALU.is_ge, op1=ALU.mult).then_inc(s_r, 1)
                dve.wait_ge(s_r, n * 3 + before + 2)
                dve.tensor_tensor(thr, thr, hit, ALU.max).then_inc(s_r, 1)
                dve.wait_ge(s_r, n * 3 + before + 3)
            made[0] = before + 3 * BITS
            link_r(dve.tensor_tensor(above[:, :, :], prob[:, :, :], over_tiles(thr), ALU.is_gt))
            dve.tensor_tensor(equal[:, :, :], prob[:, :, :], over_tiles(thr), ALU.is_equal).then_inc(s_in, 1)
            dve.wait_ge(s_cn, BITS + 1)
            link_r(dve.tensor_scalar(hit, PS[:, 0, 0:BE], -1.0, float(CAP), ALU.mult, ALU.add))
            ranks = PS[:, 1, 0:T * BE].rearrange("p (t n) -> p t n", n=BE)
            link_r(dve.tensor_tensor(pos[:, :, :], ranks, over_tiles(hit), ALU.is_lt))
            link_r(dve.tensor_tensor(pos[:, :, :], pos[:, :, :], equal[:, :, :], ALU.mult))
            dve.tensor_tensor(chosen[:, :, :], pos[:, :, :], above[:, :, :], ALU.add).then_inc(s_in, 1)
            dve.wait_ge(s_in, BITS + 2)
            for t in range(T):
                for b in range(B):
                    dve.memset(picks[:, t, b * E:(b + 1) * E, 1], float(b * T + t))
            dve.tensor_scalar(picks[:, :, :, 0], prob[:, :, :], 0.0, lane[:, 0:1], ALU.mult, ALU.add)
            link_r(dve.tensor_copy(picks[:, :, :, 2], prob[:, :, :]))
            link_r(dve.tensor_tensor(pos[:, :, :], prob[:, :, :], picks[:, :, :, 2], ALU.subtract))
            link_r(dve.tensor_copy(picks[:, :, :, 3], pos[:, :, :]))
            link_r(dve.tensor_tensor(picks[:, :, :, 4], pos[:, :, :], picks[:, :, :, 3], ALU.subtract))
            dve.wait_ge(s_cn, BITS + 2)
            link_r(dve.scalar_tensor_tensor(out=pos[:, :, :], in0=ranks, scalar=1.0, in1=chosen[:, :, :],
                                            op0=ALU.add, op1=ALU.mult))
            link_r(dve.tensor_scalar(pos[:, :, :], pos[:, :, :], 1.0, None, ALU.subtract))

            def choose(n, e, b):
                wait_apart(dve, s_pk, n - 1 + START)
                for t in range(T):
                    ins = dve.tensor_scalar(onehot[b % 2][:, t, :], iota[:, :], pos[:, t, bass.ds(e + b * E, 1)],
                                            None, ALU.is_equal)
                ins.then_inc(s_oh, 1)

            def take_choice(e, half, link):
                wait_apart(dve, s_pk, (e + 1) * B + START)
                dve.tensor_copy(picked[:, :, :, :].rearrange("p b j c -> p (b j c)"),
                                PS[:, 1, 0:B * 2 * COLS]).then_inc(s_pe2, 1)
                dve.wait_ge(s_pe2, e + 1 + START)
                col = lambda c: picked[:, :, :, c]
                tokf3 = tokf.rearrange("p (b j) -> p b j", j=2)
                link(dve.scalar_tensor_tensor(out=tokf3, in0=col(1), scalar=float(P), in1=col(0),
                                              op0=ALU.mult, op1=ALU.add))
                dve.tensor_scalar(tok_g[half][:, :, :], tokf3, 0.0, None, ALU.add).then_inc(s_tk, 1)
                link(dve.tensor_tensor(gate[half][:, :, :], col(2), col(3), ALU.add))
                link(dve.tensor_tensor(gate[half][:, :, :], gate[half][:, :, :], col(4), ALU.add))

            def scatter_tokens(half):
                dve.tensor_copy(tok_s[half][:, :, :], tok_g[half][:, :, :]).then_inc(s_tk, 1)

            def turned(n, k):
                dve.wait_ge(s_gt, n + 1 + START)
                dve.tensor_copy(xgT[k].rearrange("p c j -> p (c j)"), PS[:, 0, :]).then_inc(s_te, 1)

            def gated(n, e, b, half):
                wait_apart(dve, s_y, n + 1 + START, s_sc[b], e * 32 + COPIED)
                for j in range(2):
                    ins = dve.tensor_scalar(yg[b][:, j, :], PS[:, 6 + b % 2, j * D:(j + 1) * D],
                                            gate[half][:, b, j:j + 1], None, ALU.mult)
                ins.then_inc(s_ye, 1)

            for e in range(2):
                for b in range(B):
                    choose(e * B + b, e, b)
                take_choice(e, e, link_r)
                if e == 0:
                    dve.wait_ge(s_tk, 1)
                    scatter_tokens(0)
            turned(0, 0)
            turned(1, 1)
            STEPS = 2 * 3
            before = made[0]

            def experts(i, last):
                linked = [0]

                def link_e(ins):
                    linked[0] += 1
                    ins.then_inc(s_r, 1)
                    dve.wait_ge(s_r, i * STEPS + before + linked[0])

                for u in range(UNITS):
                    half, b = divmod(u, B)
                    n, e = i * UNITS + u, i * 2 + half
                    if not (last and u + 2 >= UNITS):
                        turned(n + 2, u % 2)
                    if not last:
                        choose(n + 2 * B, e + 2, b)
                    gated(n, e, b, half)
                    if b == B - 1 and not (last and half == 1):
                        dve.wait_ge(s_tk, i * 4 + half * 2 + 3)
                        scatter_tokens(1 - half)
                        if not last:
                            take_choice(e + 2, half, link_e)

            with dve.Fori(0, E // 2 - 1) as i:
                experts(i, False)
            experts(E // 2 - 1, True)

            base = before + (E // 2 - 1) * STEPS
            made[0] = base
            for b in range(B):
                dve.wait_ge(s_al[b], 16)
                for t in range(T):
                    ins = dve.bn_stats(st6[:, t, :], fin[b][:, t, :])
                link_r(ins)
                for t in range(T):
                    ins = dve.bn_aggr(fmv[:, b, t, :], st6[:, t, :])
                link_r(ins)
                dve.tensor_scalar(frstd[:, b, :], fmv[:, b, :, 1], EPS, None, ALU.add).then_inc(s_fz, 1)
                dve.wait_ge(s_fr, b + 1)
                dve.scalar_tensor_tensor(out=fshift[:, b, :], in0=fmv[:, b, :, 0], scalar=-1.0,
                                         in1=frstd[:, b, :], op0=ALU.mult, op1=ALU.mult).then_inc(s_fb, 1)

        @blk.tensor
        def _(pe):
            def item(b, idx):
                old = idx - 8
                if old >= STAGE[idx]:
                    if ITEMS[old][1] == "A":
                        pe.wait_ge(s_eva, b * NA + taken("A", old + 1) + START)
                    else:
                        pe.wait_ge(s_evd, b * ND + taken("D", old + 1) + START)
                return PS[:, bank(idx), :]

            def taken_upto(b, idx):
                pe.wait_ge(s_eva, b * NA + taken("A", idx) + START)
                pe.wait_ge(s_evd, b * ND + taken("D", idx) + START)

            def turn_tokens(b, name, src, per_tile=None):
                for n in range(4):
                    idx = first(name) + n
                    ps = item(b, idx)
                    for k in range(4):
                        t = 4 * (n % 2) + k
                        if per_tile is not None and n < 2:
                            per_tile(t)
                        ins = pe.transpose(ps[:, k * P:(k + 1) * P], src[:, t, (n // 2) * P:(n // 2 + 1) * P],
                                           ident[:, :])
                    ins.then_inc(s_item, 1)

            def project(b, idx, w, rhs, half, m, cols=N):
                ps = item(b, idx)
                for c in range(C):
                    ins = pe.matmul(ps[:, 0:cols], w[:, c, m * P:(m + 1) * P], rhs[:, c, half * N:half * N + cols],
                                    start=(c == 0), stop=(c == C - 1))
                ins.then_inc(s_item, 1)

            def attention(b, n0, u0, g0, order, cross):
                sm_group = (SM_CROSS if cross else SM_SELF) // NG
                per = (ST_CROSS if cross else ST_SELF) // NG // HALVES
                keys = kxst if cross else kst
                for what, n in order:
                    if what == "smax":
                        g, k = divmod(n, sm_group)
                        if k == 0 and g % 2 == 0:
                            if cross:
                                pe.wait_ge(s_ql[g // 2], b * 192 + 192)
                                pe.wait_ge(s_kx, b * 192 + 192)
                            else:
                                pe.wait_ge(s_ql[g // 2], b * 192 + 96)
                                pe.wait_ge(s_kl[g // 2], b * 96 + 96)
                        if n >= 3:
                            pe.wait_ge(s_smu, b * SM_ALL + n0 + n - 2)
                        ps = PS[:, n % 3, :]
                        if cross:
                            h, t0 = g * G + k // 3, 3 * (k % 3)
                            nt = min(3, T - t0)
                            pe.matmul(ps[:, 0:nt * SK], identb[:, :], maskb[:, t0:t0 + nt, 0:SK],
                                      start=True, stop=False, skip_group_check=True)
                            for t in range(t0, t0 + nt):
                                ins = pe.matmul(ps[:, (t - t0) * SK:(t - t0 + 1) * SK],
                                                qst[0:KQ, h, t * P:(t + 1) * P], kxst[0:KQ, h, 0:SK],
                                                start=False, stop=(t == t0 + nt - 1), skip_group_check=True)
                        else:
                            h, t, half = g * G + k // (T * HALVES), k // HALVES % T, k % HALVES
                            ins = pe.matmul(ps, qst[0:KQ, h, t * P:(t + 1) * P],
                                            kst[0:KQ, h, half * N:(half + 1) * N], start=True, stop=True)
                        ins.then_inc(s_sm, 1)
                    elif what == "turn":
                        m = g0 + n
                        pe.wait_ge(s_nm, b * 2 * NG + m + 1)
                        pe.wait_ge(s_ne, b * 2 * NG + m + START)
                        rows = PS[0:3 * G, 7, :].bitcast(BF16)
                        for t in range(T):
                            ins = pe.transpose(rows[:, t * P:(t + 1) * P], nmp[:, m % 2, t, :], identb[:, :])
                        ins.then_inc(s_nt, 1)
                    elif what == "st":
                        gh, k = divmod(n, per)
                        g, half = divmod(gh, HALVES)
                        cols = slice(half * N, (half + 1) * N)
                        if k == 0 and half == 0:
                            m = g0 + g
                            pe.wait_ge(s_nl[m % 2], 48 * (b * NG + m // 2 + 1) + START)
                        if n >= 2:
                            pe.wait_ge(s_ex, b * ST_ALL + u0 + n - 1)
                        ps = PS[:, 3 + n % 2, :]
                        if not cross:
                            kc, j = divmod(k, G)
                            ins = pe.matmul(ps, kst[0:KM, g * G + j, kc * P:(kc + 1) * P],
                                            qst[0:KM, g * G + j, cols], start=True, stop=True)
                        elif k < G:
                            for t in range(4):
                                pe.matmul(ps[:, t * P:(t + 1) * P], maskb[:, 4 * half + t, 0:P], identb[:, :],
                                          start=(t == 0), stop=False, skip_group_check=True)
                            ins = pe.matmul(ps, kxst[0:KM, g * G + k, 0:P], qst[0:KM, g * G + k, cols],
                                            start=False, stop=True, skip_group_check=True)
                        else:
                            for j in range(G):
                                rows = PS[V32 * j:V32 * (j + 1), 3 + n % 2, :]
                                for t in range(4):
                                    pe.matmul(rows[:, t * P:(t + 1) * P], maskb[:, 4 * half + t, P:P + V32],
                                              identb[:, :], start=(t == 0), stop=False, skip_group_check=True,
                                              tile_position=(0, V32 * j))
                                ins = pe.matmul(rows, kxst[0:KM, g * G + j, P:P + V32], qst[0:KM, g * G + j, cols],
                                                start=False, stop=True, skip_group_check=True,
                                                tile_position=(0, V32 * j))
                        ins.then_inc(s_st, 1)
                    else:
                        gh, k = divmod(n, per)
                        g, half = divmod(gh, HALVES)
                        (wait_apart if cross and k == G else wait)(pe, s_ex, b * ST_ALL + u0 + n + 1)
                        if k == 0 and gh >= 2:
                            pe.wait_ge(s_ave, b * 4 * NG + (2 * NG if cross else 0) + gh - 1)
                        av = PS[:, 5 + gh % 2, :]
                        if not cross:
                            kc, j = divmod(k, G)
                            ins = pe.matmul(av[V32 * j:V32 * (j + 1), :], V[:, kc, g * G + j, :], pT[:, n % 4, :],
                                            start=(kc == 0), stop=(kc == T - 1), tile_position=(0, V32 * j),
                                            skip_group_check=True)
                        elif k < G:
                            ins = pe.matmul(av[V32 * k:V32 * (k + 1), :], Vx[:, g * G + k, :], pT[:, n % 4, :],
                                            start=True, stop=False, tile_position=(0, V32 * k),
                                            skip_group_check=True)
                        else:
                            for j in range(G):
                                rows = slice(V32 * j, V32 * j + SKR)
                                ins = pe.matmul(av[V32 * j:V32 * (j + 1), :], Vr[rows, g, :], pT[rows, n % 4, :],
                                                start=False, stop=True, skip_group_check=True,
                                                tile_position=(V32 * j, V32 * j))
                        ins.then_inc(s_pu, 1)

            def close_stage(b, cross):
                pe.wait_ge(s_smu, b * SM_ALL + (SM_ALL if cross else SM_SELF))
                pe.wait_ge(s_ex, b * ST_ALL + (ST_ALL if cross else ST_SELF))
                pe.wait_ge(s_ave, b * 4 * NG + (4 if cross else 2) * NG)
                pe.wait_ge(s_ne, b * 2 * NG + (2 if cross else 1) * NG + START)

            def output(b, o_name, t_name, y_name, w):
                for t in range(T):
                    idx = first(o_name) + t
                    ps = item(b, idx)
                    for g in range(NG):
                        ins = pe.transpose(ps[:, g * P:(g + 1) * P], oT[:, g, t * P:(t + 1) * P], ident[:, :])
                    ins.then_inc(s_item, 1)
                turn_tokens(b, t_name, z, lambda t: pe.wait_ge(s_evd, b * ND + taken("D", first(o_name) + t + 1) + START))
                taken_upto(b, first(t_name) + 4)
                for k in range(4):
                    idx = first(y_name) + k
                    ps = item(b, idx)
                    for t in (2 * k, 2 * k + 1):
                        for c in range(C):
                            ins = pe.matmul(ps[:, (t % 2) * D:(t % 2 + 1) * D], xT[:, c, t * P:(t + 1) * P],
                                            w[:, c, :], start=(c == 0), stop=(c == C - 1))
                    ins.then_inc(s_item, 1)

            pe.wait_ge(s_id, 1)
            pe.wait_ge(s_w, 16 * NW)
            with pe.Fori(0, B) as b:
                pe.wait_ge(s_x, (b + 1) * 64)
                pe.wait_ge(s_eva, b * NA + START)
                pe.wait_ge(s_evd, b * ND + START)
                turn_tokens(b, "xT", x)
                idx = first("ctxT")
                ps = item(b, idx)
                for c in range(C):
                    pe.transpose(ps[:, c * SK:c * SK + P], cx[:, 0, c * P:(c + 1) * P], ident[:, :])
                    ins = pe.transpose(ps[:, c * SK + P:(c + 1) * SK], cx[0:SKR, 1, c * P:(c + 1) * P],
                                       ident[0:SKR, 0:SKR])
                ins.then_inc(s_item, 1)
                taken_upto(b, first("xT") + 4)
                for name, w in (("ctq", wdq), ("ctkv", wdkv)):
                    for half in range(HALVES):
                        project(b, first(name) + half, w, xT, half, 0)
                taken_upto(b, first("ctkv") + 2)
                for i in range(4):
                    m, half = i // 2, i % 2
                    for k, w in enumerate((wqr, wqrs, wuq)):
                        idx = first("q") + 3 * i + k
                        ps = item(b, idx)
                        pe.matmul(ps, w[:, m * P:(m + 1) * P], ctq[:, half * N:(half + 1) * N],
                                  start=True, stop=True).then_inc(s_item, 1)
                for i in range(4):
                    m, half = i // 2, i % 2
                    project(b, first("k") + 3 * i, wkr, xT, half, m)
                    project(b, first("k") + 3 * i + 1, wkrs, xT, half, m)
                    ps = item(b, first("k") + 3 * i + 2)
                    pe.matmul(ps, wuk[:, m * P:(m + 1) * P], ctkv[:, half * N:(half + 1) * N],
                              start=True, stop=True).then_inc(s_item, 1)
                for k in range(4):
                    ps = item(b, first("v") + k)
                    for t in (2 * k, 2 * k + 1):
                        ins = pe.matmul(ps[:, (t % 2) * D:(t % 2 + 1) * D], ctkv[:, t * P:(t + 1) * P], wuv[:, :],
                                        start=True, stop=True)
                    ins.then_inc(s_item, 1)
                ps = item(b, first("kx"))
                for m in range(C):
                    for c in range(C):
                        ins = pe.matmul(ps[:, m * SK:(m + 1) * SK], w1x[:, c, m * P:(m + 1) * P], cxT[:, c, :],
                                        start=(c == 0), stop=(c == C - 1))
                ins.then_inc(s_item, 1)
                ps = item(b, first("vx"))
                for c in range(C):
                    ins = pe.matmul(ps[:, 0:D], cxT[:, c, 0:P], w2x[:, c, :], start=(c == 0), stop=(c == C - 1))
                ins.then_inc(s_item, 1)
                ps = item(b, first("vxr"))
                for j in range(G):
                    for c in range(C):
                        ins = pe.matmul(ps[V32 * j:V32 * j + SKR, 0:D], cxT[:, c, P:SK], w2x[:, c, :],
                                        start=(c == 0), stop=(c == C - 1), tile_position=(0, V32 * j),
                                        skip_group_check=True)
                ins.then_inc(s_item, 1)
                taken_upto(b, len(FRONT))
                attention(b, 0, 0, 0, ORDER_SELF, False)
                close_stage(b, False)
                output(b, "o", "oT", "y", wo)
                pe.wait_ge(s_ln, b * 2 * T + T)
                turn_tokens(b, "x1T", z)
                taken_upto(b, first("x1T") + 4)
                for i in range(4):
                    project(b, first("qx") + i, w0, xT, i % 2, i // 2)
                taken_upto(b, first("qx") + 4)
                pe.wait_ge(s_mask, b + 1 + START)
                attention(b, SM_SELF, ST_SELF, NG, ORDER_CROSS, True)
                close_stage(b, True)
                output(b, "ox", "oxT", "yx", w3)
                pe.wait_ge(s_ln, b * 2 * T + 2 * T)
                turn_tokens(b, "x2T", z)
                taken_upto(b, first("x2T") + 4)
                ps = item(b, first("logit"))
                for t in range(T):
                    for c in range(C):
                        ins = pe.matmul(ps[:, t * E:(t + 1) * E], xT[:, c, t * P:(t + 1) * P], wch[:, c, :],
                                        start=(c == 0), stop=(c == C - 1))
                ins.then_inc(s_item, 1)
            def count(ps, src):
                for t in range(T):
                    ins = pe.matmul(ps, onesb[:, :], src[:, t, :], start=(t == 0), stop=(t == T - 1))
                return ins

            def prefix(src):
                for t in range(T):
                    ps = PS[:, 1, t * BE:(t + 1) * BE]
                    for k in range(t):
                        pe.matmul(ps, onesb[:, :], src[:, k, :], start=(k == 0), stop=False)
                    ins = pe.matmul(ps, tri[:, :], src[:, t, :], start=(t == 0), stop=True)
                return ins

            pe.wait_ge(s_evd, B * ND + START)
            with pe.Fori(0, BITS) as n:
                pe.wait_ge(s_in, n + 1)
                count(PS[:, 0, 0:BE], above).then_inc(s_cn, 1)
            pe.wait_ge(s_in, BITS + 1)
            count(PS[:, 0, 0:BE], above)
            prefix(equal).then_inc(s_cn, 1)
            pe.wait_ge(s_in, BITS + 2)
            prefix(chosen).then_inc(s_cn, 1)

            def pick(n, e, b):
                wait_apart(pe, s_oh, n + 1)
                if b == 0:
                    pe.wait_ge(s_pe2, e + START)
                for j in range(2):
                    for t in range(T):
                        ins = pe.matmul(PS[:, 1, (b * 2 + j) * COLS:(b * 2 + j + 1) * COLS],
                                        onehot[b % 2][:, t, j * P:(j + 1) * P],
                                        picks[:, t, bass.ds(e + b * E, 1), 0:COLS].rearrange("p a c -> p (a c)"),
                                        start=(t == 0), stop=(t == T - 1))
                ins.then_inc(s_pk, 1)

            def turn_rows(n, e, b):
                pe.wait_ge(s_g[b], e * 32 + 32)
                pe.wait_ge(s_te, n + START)
                for c in range(C):
                    for j in range(2):
                        ins = pe.transpose(PS[:, 0, c * CAP + j * P:c * CAP + (j + 1) * P],
                                           xg[b][:, j, c * P:(c + 1) * P], ident[:, :])
                ins.then_inc(s_gt, 1)

            def hidden(n, turn, u, first_unit=False):
                k, half = u % 2, u // B
                if u % B == 0:
                    pe.wait_ge(s_we[half], turn * 32 + 32)
                pe.wait_ge(s_te, n + 1 + START)
                if not first_unit:
                    pe.wait_ge(s_si, (n - 1) * 2 + START)
                for f in range(F // P):
                    for c in range(C):
                        ins = pe.matmul(PS[:, 2 + 2 * k + f // 2, (f % 2) * CAP:(f % 2 + 1) * CAP],
                                        we1[half][:, c, f * P:(f + 1) * P], xgT[k][:, c, :],
                                        start=(c == 0), stop=(c == C - 1))
                    if f % 2:
                        ins.then_inc(s_h, 1)

            def expert_out(i, u):
                k, half = u % 2, u // B
                pe.wait_ge(s_si, i * UNITS * 2 + 2 * u + 2 + START)
                pe.wait_ge(s_ye, i * UNITS + u - 1 + START)
                for j in range(2):
                    for f in range(F // P):
                        ins = pe.matmul(PS[:, 6 + k, j * D:(j + 1) * D], hT[k][:, f, j * P:(j + 1) * P],
                                        we2[half][:, f, :], start=(f == 0), stop=(f == F // P - 1))
                ins.then_inc(s_y, 1)

            def experts(i, last):
                for u in range(UNITS):
                    n = i * UNITS + u
                    half, b = divmod(u, B)
                    if not (last and u + 2 >= UNITS):
                        turn_rows(n + 2, i * 2 + (u + 2) // B, (u + 2) % B)
                    if not (last and u + 1 >= UNITS):
                        hidden(n + 1, i + (u + 1) // UNITS, (u + 1) % UNITS)
                    if not last:
                        pick(n + 2 * B, i * 2 + half + 2, b)
                    expert_out(i, u)

            for e in range(2):
                for b in range(B):
                    pick(e * B + b, e, b)
            turn_rows(0, 0, 0)
            turn_rows(1, 0, 1)
            hidden(0, 0, 0, True)
            with pe.Fori(0, E // 2 - 1) as i:
                experts(i, False)
            experts(E // 2 - 1, True)


def host_arrays(i):
    pair = np.arange(D) ^ 1
    pos = np.arange(S, dtype=np.float32)[:, None]
    theta = (np.float32(10000.0) ** (np.float32(-2.0) * np.arange(D // 2, dtype=np.float32))
             / np.float32(D // 2)).astype(np.float32)
    r = pos * theta[None, :]
    cos = np.repeat(np.cos(r).T, 2, axis=0)
    sin = np.repeat(np.sin(r).T, 2, axis=0)
    sin[0::2] = -sin[0::2]
    lay = lambda t: np.ascontiguousarray(t.reshape(C, P, S).transpose(1, 0, 2).astype(np.float32))
    col = lambda v: np.asarray(v).reshape(-1, P).T
    g = {k: np.asarray(v) for k, v in i.items()}
    at = lambda n: g["L0_attn_" + n]
    xa = lambda n: g["L0_xattn_" + n]
    bias_columns = np.concatenate([col(at("Wd_q_b")), col(at("Wd_kv_b")),
                                   col(at("Wu_q_b")), col(at("Wq_r_b")), col(at("Wq_r_b")[pair]),
                                   col(at("Wu_k_b")), col(at("Wk_r_b")), col(at("Wk_r_b")[pair]),
                                   col(xa("b1")), col(xa("b0"))], axis=1)
    out = {
        "x": g["x"].reshape(B * S, D), "ctx": g["ctx_1024"].reshape(B * SK, D),
        "mask": g["mask_BxSxS2_if1"].reshape(B * S, SK),
        "bias_columns": bias_columns,
        "bias_rows": np.stack([at("Wu_v_b"), at("Wo_b"), xa("b2"), xa("b3")])[None],
        "cos": lay(cos), "sin": lay(sin),
        "Wd_q": at("Wd_q_w"), "Wd_kv": at("Wd_kv_w"), "Wu_q": at("Wu_q_w"), "Wq_r": at("Wq_r_w"),
        "Wq_r_swapped": at("Wq_r_w")[:, pair], "Wu_k": at("Wu_k_w"), "Wu_v": at("Wu_v_w"),
        "Wk_r": at("Wk_r_w"), "Wk_r_swapped": at("Wk_r_w")[:, pair], "Wo": at("Wo_w"),
        "W0T": xa("W0").T, "W1T": xa("W1").T, "W2T": xa("W2").T, "W3T": xa("W3").T,
        "choiceT": g["L0_ffn_choice_w"].T,
        "w1": g["L0_ffn_w1"], "w2": g["L0_ffn_w2"],
    }
    return {k: np.ascontiguousarray(v) for k, v in out.items()}


def kernel(**inputs):
    import concourse.bacc as _bacc
    from concourse.bass_utils import run_bass_kernel_spmd as _run

    arrays = host_arrays(inputs)
    nc = _bacc.Bacc("TRN2", target_bir_lowering=False, num_devices=1)
    args = {n: nc.dram_tensor(f"in_{n}", v.shape, mybir.dt.from_np(v.dtype), kind="ExternalInput").ap()
            for n, v in arrays.items()}
    out = nc.dram_tensor("out", (B * S, D), F32, kind="ExternalOutput").ap()
    decoder_block(nc, args, out)
    r = _run(nc, [{f"in_{n}": v for n, v in arrays.items()}], core_ids=[0])
    return r.results[0]["out"].reshape(B, S, D)
```

```python
from contextlib import ExitStack

import numpy as np

import concourse.bass as bass
from concourse import mybir

F32 = mybir.dt.float32
BF16 = mybir.dt.bfloat16
I32 = mybir.dt.int32
U32 = mybir.dt.uint32
ALU = mybir.AluOpType
ACT = mybir.ActivationFunctionType
AX = mybir.AxisListType

P = 128
B, S, D = 4, 1024, 256
H = 16
HD = D // H
SK = 154
SKR = SK - P
T = S // P
C = D // P
N = 512
HALVES = S // N
LAT = 128
E, F = 8, 512
CAP = S * 2 // E
EPS = 1e-5
TERMS = [(0, 0), (0, 1), (0, 2), (1, 0), (1, 1), (2, 0)]
KQ = HD * len(TERMS)
KM = KQ + 3
MASKED = -float(2 ** 120)
SCALE_SELF = float(1.0 / np.sqrt(np.float32(H + LAT + LAT)))
SCALE_CROSS = float(1.0 / np.sqrt(np.float32(HD)))
G = 2
TILES = G * HALVES
NG = H // G
V32 = 32

TURN_IN = [("xT", "D")] * 4
LATENTS = [("ctq", "D")] * 2 + [("ctkv", "D")] * 2
TURN_CTX = [("ctxT", "D")]
VALUES = [("v", "D")] * 4 + [("kx", "D"), ("vx", "D"), ("vxr", "D")]
FRONT = TURN_IN + TURN_CTX + LATENTS + [("q", "D")] * 8 + [("k", "D")] * 8 + VALUES
MID = ([("o", "D")] * T + [("oT", "DA"[n % 2]) for n in range(4)] + [("y", "D")] * 4
       + [("x1T", "DA"[n % 2]) for n in range(4)] + [("qx", "D")] * 4)
OX = [("ox", "D")] * T
OXT = [("oxT", "D")] * 4
YX = [("yx", "D")] * 4
X2T = [("x2T", "D")] * 4
BACK = OX + OXT + YX + X2T
WOVEN = [("q", "D")] * 8 + [("k", "D")] * 4 + OX + [("k", "D")] * 4 + OXT + YX + VALUES + X2T


class Plan:

    def __init__(self, *stages):
        self.items = sum(stages, [])
        self.start = sum(([sum(map(len, stages[:n]))] * len(stage) for n, stage in enumerate(stages)), [])

    def nth(self, name, n=0):
        return [i for i, (item, _) in enumerate(self.items) if item == name][n]

    def taken(self, engine, upto):
        return sum(e == engine for _, e in self.items[:upto])


FIRST, EACH, LAST = Plan(FRONT), Plan(MID + TURN_IN + TURN_CTX + LATENTS, WOVEN), Plan(MID, BACK)


class Place:

    def __init__(self, plan, b=0):
        self.plan, self.b, self.nth, self.waited = plan, b, plan.nth, {}

    def made(self, upto):
        before = 0 if self.plan is FIRST else self.b * len(EACH.items) + len(FRONT)
        return before + (upto + START)

    def taken(self, engine, upto):
        ahead = 10 ** 6
        before = (0 if self.plan is FIRST
                  else self.b * EACH.taken(engine, ahead) + FIRST.taken(engine, ahead))
        return before + (self.plan.taken(engine, upto) + START)

    def bank(self, idx):
        return (idx - self.plan.start[idx]) % 8

    def piece(self, i):
        name, n = (("q", 4 * (i // 2) + 2 + i % 2) if i < 4 else ("k", 4 * (i // 2 - 2) + 2 + i % 2) if i < 8
                   else ("kx", 0) if i == 8 else ("qx", i - 9))
        return self.nth(name, n)


PIECES = 13
RING = 4
PIECES_OF = [len(range(i, PIECES, RING)) for i in range(RING)]
SM_SELF, SM_CROSS = H * T * HALVES, H * 3
ST_SELF, ST_CROSS = NG * HALVES * T * G, NG * (TILES + 1)
LAG = 2


def schedule(sm_group, st_group, lead, turn):
    order, av = [], 0
    total = NG * st_group + sm_group + lead
    for k in range(total):
        if k < NG * sm_group:
            order.append(("smax", k))
        if k >= sm_group + turn and (k - turn) % sm_group == 0 and (k - turn) // sm_group <= NG:
            order.append(("turn", (k - turn) // sm_group - 1))
        st = k - sm_group - lead
        if st >= 0:
            order.append(("st", st))
        if av <= st - LAG - (k >= NG * sm_group):
            order.append(("av", av))
            av += 1
    return order + [("av", n) for n in range(av, NG * st_group)]


def score_banks(order):
    last_max = max(n for n, (what, _) in enumerate(order) if what == "smax")
    banks, before, free = [], [], [3, 4]
    had = {}
    for n, (what, unit) in enumerate(order):
        if what == "st":
            if n > last_max and len(free) == 2:
                free = [0, 1, 2] + free
            banks.append(free.pop(0))
            free.append(banks[-1])
            before.append(had.get(banks[-1]))
            had[banks[-1]] = unit
    return banks, before


TURN_SELF, TURN_CROSS = 3, 4
START = 2
COPIED = 16
BITS = 30
COLS = 5
UNITS = 2 * B
ORDER_SELF = schedule(SM_SELF // NG, ST_SELF // NG, 12, TURN_SELF)
ORDER_NEXT = []
for step in ORDER_SELF:
    ORDER_NEXT.append(step)
    if step[0] == "smax" and step[1] % 3 == 2 and step[1] < 3 * T:
        ORDER_NEXT.append(("logits", step[1] // 3))
ORDER_CROSS = schedule(SM_CROSS // NG, ST_CROSS // NG, 18, TURN_CROSS)
BANKS_SELF, BEFORE_SELF = score_banks(ORDER_SELF)
BANKS_CROSS, BEFORE_CROSS = score_banks(ORDER_CROSS)
SM_ALL, ST_ALL = SM_SELF + SM_CROSS, ST_SELF + ST_CROSS


def decoder_block(nc, a, out):
    ctx = ExitStack()
    with ctx:
        def sb(name, shape, dt=F32):
            return ctx.enter_context(nc.sbuf_tensor(name, shape, dt))

        def sem(name):
            return ctx.enter_context(nc.semaphore(name))

        def dram(name, shape, dt):
            return nc.dram_tensor(name, shape, dt, kind="Internal").ap()

        PS = ctx.enter_context(nc.psum_tensor("banks", [P, 8, N], F32))

        q_parts = dram("q_parts", (3, D, S), BF16)
        k_parts = dram("k_parts", (3, D, S), BF16)
        kx_parts = dram("kx_parts", (P, 3, C, SK), BF16)
        x2_rows = dram("x2_rows", (B * S, D), F32)
        acc_rows = dram("acc_rows", (B * S, D), F32)

        ident = sb("ident", [P, P])
        identb = sb("identb", [P, P], BF16)
        tri = sb("tri", [P, P], BF16)
        onesb = sb("onesb", [P, P], BF16)
        iota = sb("iota", [P, CAP], BF16)
        cosT = sb("cosT", [P, S])
        sinT = sb("sinT", [P, S])
        wdq = sb("wdq", [P, C, LAT])
        wdkv = sb("wdkv", [P, C, LAT])
        wuq = sb("wuq", [P, D])
        wqr = sb("wqr", [P, D])
        wuk = sb("wuk", [P, D])
        wuv = sb("wuv", [P, D])
        wkr = sb("wkr", [P, C, D])
        wo = sb("wo", [P, C, D])
        w0 = sb("w0", [P, C, D])
        w1x = sb("w1x", [P, C, D])
        w2x = sb("w2x", [P, C, D])
        w3 = sb("w3", [P, C, D])
        wch = sb("wch", [P, C, E])
        bcol = sb("bcol", [P, 14])
        brow = sb("brow", [P, 4, D])
        mhalf = sb("mhalf", [P, T])
        oT = sb("oT", [P, NG, N])
        early = oT[:, :, :].rearrange("p g n -> p (g n)")
        mask_i = early[:, 0:T * SK].bitcast(I32).rearrange("p (t k) -> p t k", k=SK)
        xT = sb("xT", [P, C, S])
        cxT = sb("cxT", [P, C, SK])
        maskb = sb("maskb", [P, T, 160], BF16)
        pT = sb("pT", [P, 4, N])
        ctkv = sb("ctkv", [P, S])
        z = sb("z", [P, T, D])
        iota_f = z[:, 0, :]
        full = sb("full", [P, 2, N])
        rest = sb("rest", [P, 2, N])
        part = sb("part", [P, RING, 3, N], BF16)
        qst = sb("qst", [P, H, S], BF16)
        kst = sb("kst", [P, H, S], BF16)
        kxst = sb("kxst", [P, H, 160], BF16)
        V = sb("V", [P, T, H, V32])
        Vx = sb("Vx", [P, H, V32])
        Vr = sb("Vr", [P, NG, V32])
        mh = sb("mh", [P, 2, T, G, HALVES])
        nmf = sb("nmf", [P, T, G])
        nmr = sb("nmr", [P, T, G])
        nmp = sb("nmp", [P, 2, T, 3 * G], BF16)
        nmT = sb("nmT", [3 * G, 2, S], BF16)
        rz = sb("rz", [P, 2, H])
        xb = sb("xb", [P, T, D])
        st6 = sb("st6", [P, T, 6])
        mv = sb("mv", [P, T, 2])
        ve = sb("ve", [P, T])
        rstd = sb("rstd", [P, T])
        lg = sb("lg", [P, T, E])
        lgm = sb("lgm", [P, T])
        lge = sb("lge", [P, T, E])
        lgs = sb("lgs", [P, T])
        prob = sb("prob", [P, T, B * E])

        room_k = kst[:, :, :].rearrange("p h n -> p (h n)").bitcast(F32)
        x = room_k[:, 0:T * D].rearrange("p (t d) -> p t d", d=D)
        xTf = room_k[:, T * D:2 * T * D].rearrange("p (c n) -> p c n", c=C)
        by_cos = room_k[:, 2 * T * D:2 * T * D + C * N].rearrange("p (c n) -> p c n", c=C)
        by_sin = room_k[:, 2 * T * D + C * N:2 * T * D + 2 * C * N].rearrange("p (c n) -> p c n", c=C)
        cx = room_k[:, 3 * T * D:3 * T * D + 2 * D].rearrange("p (t d) -> p t d", d=D)
        ctq = room_k[:, 3 * T * D + 2 * D:3 * T * D + 2 * D + S]

        q_room = qst[:, :, :].rearrange("p h n -> p (h n)").bitcast(F32)
        k_room = kst[:, :, :].rearrange("p h n -> p (h n)").bitcast(F32)
        v_room = V[:, :, :, :].rearrange("p t h n -> p (t h n)")
        we1 = [q_room[:, 2048 * i:2048 * i + 1024].rearrange("p (c f) -> p c f", c=C) for i in range(2)]
        we2 = [q_room[:, 2048 * i + 1024:2048 * i + 2048].rearrange("p (c d) -> p c d", d=D) for i in range(2)]
        used = [0]

        def room(words):
            used[0] += words
            return k_room[:, used[0] - words:used[0]]

        xg = [room(2 * D).rearrange("p (j d) -> p j d", d=D) for _ in range(B)]
        xgT = [room(C * CAP).rearrange("p (c j) -> p c j", j=CAP) for _ in range(2)]
        hT = [room(F // P * CAP).rearrange("p (f j) -> p f j", j=CAP) for _ in range(2)]
        yg = [room(2 * D).rearrange("p (j d) -> p j d", d=D) for _ in range(B)]
        vused = [0]

        def vroom(words):
            vused[0] += words
            return v_room[:, vused[0] - words:vused[0]]

        BE = B * E
        by_tile = lambda ap: ap.rearrange("p (t n) -> p t n", n=BE)
        onehot = [vroom(T * CAP // 2).bitcast(BF16).rearrange("p (t j) -> p t j", j=CAP) for _ in range(2)]
        picks = vroom(T * BE * 6 // 2).bitcast(BF16).rearrange("p (t n k) -> p t n k", n=BE, k=6)
        pos = by_tile(vroom(T * BE))
        above = by_tile(vroom(T * BE // 2).bitcast(BF16))
        equal = by_tile(vroom(T * BE // 2).bitcast(BF16))
        chosen = by_tile(vroom(T * BE // 2).bitcast(BF16))
        picked = sb("picked", [P, B, 2, COLS])
        thr = vroom(BE)
        cand = vroom(BE)
        bit = vroom(BE)
        hit = vroom(BE)
        tokf = vroom(B * 2)
        tok_g = [sb(f"tok_g{i}", [P, B, 2], U32) for i in range(2)]
        tok_s = [sb(f"tok_s{i}", [P, B, 2], U32) for i in range(2)]
        gate = [sb(f"gate{i}", [P, B, 2]) for i in range(2)]
        lane = sb("lane", [P, 1])

        s_r = sem("routing_step")
        s_cn = sem("count_ready")
        s_in = sem("indicator_ready")
        s_oh = sem("onehot_ready")
        s_pk = sem("picked")
        s_pe2 = sem("picked_taken")
        s_tk = sem("gather_tokens_ready")
        s_g = [sem(f"gathered{i}") for i in range(B)]
        s_gt = sem("gathered_turned")
        s_te = sem("gathered_turned_taken")
        s_h = sem("hidden_ready")
        s_si = sem("silu_ready")
        s_y = sem("expert_output_ready")
        s_ye = sem("expert_output_gated")
        s_sc = [sem(f"scattered{i}") for i in range(B)]
        s_we = [sem(f"expert_weights{i}") for i in range(2)]
        s_al = [sem(f"sum_loaded{i}") for i in range(B)]
        s_fz = sem("final_stats")
        s_fr = sem("final_rstd")
        s_fb = sem("final_shift")
        s_fl = sem("final_layernorm")
        s_out = sem("out_stored")
        late = early.rearrange("p (b t d) -> p b t d", b=2, d=D)
        fin = [z, xb, late[:, 0], late[:, 1]]
        fmv = sb("fmv", [P, B, T, 2])
        frstd = sb("frstd", [P, B, T])
        fshift = sb("fshift", [P, B, T])

        s_wa = sem("latent_weights_loaded")
        s_wb = sem("front_weights_loaded")
        s_w = sem("weights_loaded")
        s_ms = sem("memory_set")
        s_mi = sem("mask_loaded")
        s_on = sem("ones_loaded")
        s_x = sem("x_loaded")
        s_xl = sem("residual_loaded")
        s_id = sem("identities_ready")
        s_pool = sem("pool_chain")
        s_dve = sem("dve_chain")
        s_act = sem("act_chain")
        s_item = sem("product_ready")
        s_evd = sem("product_taken_by_dve")
        s_eva = sem("product_taken_by_act")
        s_mask = sem("mask_ready")
        s_xb = sem("residual_ready")
        s_p1 = sem("part1_ready")
        s_p2 = sem("rest_ready")
        s_p3 = sem("part2_ready")
        s_p4 = sem("parts_ready")
        s_pw = [sem(f"parts_stored{i}") for i in range(RING)]
        s_ql = [sem(f"q_stack_loaded{i}") for i in range(2)]
        s_kl = [sem(f"k_stack_loaded{i}") for i in range(2)]
        s_kx = sem("kx_stack_loaded")
        s_sm = sem("max_scores_ready")
        s_smu = sem("max_scores_used")
        s_nm = sem("minus_max_ready")
        s_nt = sem("minus_max_turned")
        s_ne = sem("minus_max_rows_ready")
        s_nl = [sem(f"minus_max_loaded{i}") for i in range(2)]
        s_st = sem("scores_ready")
        s_ex = sem("exp_ready")
        s_pu = sem("exp_used")
        s_ave = sem("values_taken")
        s_z = sem("stats_ready")
        s_rs = sem("rstd_ready")
        s_ln = sem("layernorm_ready")
        s_lo = sem("logits_ready")
        s_ls = sem("logits_shifted")
        s_le = sem("logits_exp")
        s_x2 = sem("x2_stored")

        blk = ctx.enter_context(nc.Block())

        ROWS_P = lambda ap: ap.rearrange("(t p) d -> p t d", p=P)

        def wait(eng, semaphore, value):
            eng.wait_ge(semaphore, value)

        def wait_apart(eng, *waits):
            values = [v if isinstance(v, int) else eng.to_reg(v) for v in waits[1::2]]
            eng.wait_ge(s_id, 1)
            for semaphore, value in zip(waits[0::2], values):
                eng.wait_ge(semaphore, value)

        from_one = [s_xb, s_item, s_mask, s_p2, s_evd, s_eva, s_x2, s_nt, s_ne, s_gt, s_y, s_si, s_te, s_ye,
                    s_pk, s_pe2] + s_pw + s_nl

        @blk.sync
        def _(sp):
            for semaphore in from_one:
                sp.sem_inc(semaphore, START)

            def load_x(b):
                if not isinstance(b, int):
                    wait_apart(sp, s_pu, (b - 1) * ST_ALL + ST_SELF)
                sp.dma_start(x[:, :, :], ROWS_P(a["x"][bass.ds(b * S, S), :])).then_inc(s_x, 16)
                sp.dma_start(cx[:, 0, :], a["ctx"][bass.ds(b * SK, P), :]).then_inc(s_x, 16)
                sp.dma_start(cx[0:SKR, 1, :], a["ctx"][bass.ds(b * SK + P, SKR), :]).then_inc(s_x, 16)

            def load_residual(b):
                sp.dma_start(xb[:, :, :], ROWS_P(a["x"][bass.ds(b * S, S), :])).then_inc(s_xl, 16)

            def load_mask(b):
                sp.dma_start(mask_i[:, :, :], a["mask"][bass.ds(b * S, S), :].rearrange("(t p) d -> p t d", p=P)
                             ).then_inc(s_mi, 16)

            chunks = lambda name: a[name].rearrange("(c p) n -> p c n", p=P)
            load_x(0)
            for semaphore, loads in (
                (s_wa, [(bcol[:, :], a["bias_columns"]), (wdq[:, :, :], chunks("Wd_q")),
                        (wdkv[:, :, :], chunks("Wd_kv"))]),
                (s_wb, [(wqr[:, :], a["Wq_r"]), (wuq[:, :], a["Wu_q"]), (cosT[:, :], a["cos"]),
                        (sinT[:, :], a["sin"]), (wkr[:, :, :], chunks("Wk_r")), (wuk[:, :], a["Wu_k"]),
                        (wuv[:, :], a["Wu_v"]), (w1x[:, :, :], chunks("W1T")), (w2x[:, :, :], chunks("W2T")),
                        (brow[:, :, :], a["bias_rows"].rearrange("a r d -> a (r d)").to_broadcast([P, 4 * D])
                         .rearrange("p (r d) -> p r d", r=4))]),
                (s_w, [(wo[:, :, :], chunks("Wo")), (w0[:, :, :], chunks("W0T")), (w3[:, :, :], chunks("W3T")),
                       (wch[:, :, :], chunks("choiceT"))]),
            ):
                for dst, src in loads:
                    sp.dma_start(dst, src).then_inc(semaphore, 16)
            load_mask(0)
            load_residual(0)

            def store_piece(b, i, dst, cols):
                sp.wait_ge(s_p4, b * PIECES + i + 1)
                for k in range(3):
                    sp.dma_start(dst[k], part[:, i % RING, k, 0:cols]).then_inc(s_pw[i % RING], 16)

            def stored(b, i):
                wait_apart(sp, *[w for r in range(RING) for w in (
                    s_pw[r], 48 * (b * PIECES_OF[r] + len(range(r, i + 1, RING))) + START)])

            def rows_of(parts, c, half):
                rows = parts.rearrange("k (h c d) n -> k c h d n", c=C, d=HD // C)
                return [rows[k, c, :, :, half * N:(half + 1) * N] for k in range(3)]

            def load_stack(dst, parts, mc, which, s):
                for t, term in enumerate(TERMS):
                    src = parts[term[which], mc * P:(mc + 1) * P, :].rearrange("(h d) n -> d h n", d=HD)
                    sp.dma_start(dst[t * HD:(t + 1) * HD, mc * 8:(mc + 1) * 8, :], src).then_inc(s, 16)

            def load_minus_max(b, n, g):
                sp.wait_ge(s_ne, b * 2 * NG + n + 1 + START)
                for p in range(3):
                    sp.dma_start(qst[KQ + p:KQ + p + 1, g * G:(g + 1) * G, :],
                                 nmT[p * G:(p + 1) * G, n % 2, :]).then_inc(s_nl[n % 2], 16)

            def store_front(b, pieces):
                for i in pieces:
                    store_piece(b, i, rows_of(q_parts if i < 4 else k_parts, i % 2, i % 4 // 2), N)

            def load_q(b):
                stored(b, 3)
                load_stack(qst, q_parts, 0, 0, s_ql[0])

            def store_keys(b):
                store_front(b, (6, 7))
                stored(b, 7)
                load_stack(kst, k_parts, 0, 1, s_kl[0])
                load_stack(kst, k_parts, 1, 1, s_kl[1])
                sp.dma_start(kst[KQ:KM, :, :].rearrange("p h (a n) -> p (h a) n", n=P),
                             onesb[0:KM - KQ, :].rearrange("p (a n) -> p a n", a=1).to_broadcast(
                                 [KM - KQ, H * T, P])).then_inc(s_on, 16)
                load_stack(qst, q_parts, 1, 0, s_ql[1])
                store_piece(b, 8, [kx_parts[:, k, :, :].rearrange("p c n -> p (c n)") for k in range(3)], C * SK)
                stored(b, 8)
                for c in range(C):
                    for t, term in enumerate(TERMS):
                        src = kx_parts[:, term[1], c, :].rearrange("(h d) n -> d h n", d=HD)
                        sp.dma_start(kxst[t * HD:(t + 1) * HD, c * 8:(c + 1) * 8, 0:SK], src).then_inc(s_kx, 16)

            def self_attention(b):
                for g in range(NG):
                    load_minus_max(b, g, g)

            def rest_of_batch(b, more):
                if more:
                    load_x(b + 1)
                wait_apart(sp, s_ql[0], b * 192 + 96, s_ql[1], b * 192 + 96)
                for i in range(9, 13):
                    mc, half = (i - 9) // 2, (i - 9) % 2
                    store_piece(b, i, [q_parts[k, mc * P:(mc + 1) * P, half * N:(half + 1) * N]
                                       for k in range(3)], N)
                    if i % 2 == 0:
                        stored(b, i)
                        load_stack(qst, q_parts, mc, 0, s_ql[mc])
                for g in range(NG):
                    load_minus_max(b, NG + g, g)
                if more:
                    at = Place(EACH, b)
                    wait_apart(sp, s_item, at.made(at.nth("ox", T - 1) + 1))
                    load_mask(b + 1)
                    wait_apart(sp, s_ql[0], b * 192 + 192, s_ql[1], b * 192 + 192, s_kl[0], b * 96 + 96,
                               s_kl[1], b * 96 + 96, s_kx, b * 192 + 192)
                    store_front(b + 1, range(6))
                    load_q(b + 1)
                    store_keys(b + 1)
                    wait_apart(sp, s_evd, at.taken("D", at.nth("yx", 3) + 1))
                    load_residual(b + 1)
                wait_apart(sp, s_ln, (b * 2 + 2) * T)
                sp.dma_start(ROWS_P(x2_rows[bass.ds(b * S, S), :]), z[:, :, :]).then_inc(s_x2, 16)
                if more:
                    self_attention(b + 1)

            store_front(0, range(6))
            load_q(0)
            store_keys(0)
            self_attention(0)
            with sp.Fori(0, B - 1) as b:
                rest_of_batch(b, True)
            rest_of_batch(B - 1, False)
            sp.wait_ge(s_pu, B * ST_ALL)

            def load_expert(e, i):
                sp.dma_start(we1[i], a["w1"][bass.ds(e, 1), :, :].rearrange("a (c p) f -> p (a c) f", p=P)
                             ).then_inc(s_we[i], 16)
                sp.dma_start(we2[i], a["w2"][bass.ds(e, 1), :, :].rearrange("a (c p) d -> p (a c) d", p=P)
                             ).then_inc(s_we[i], 16)

            load_expert(0, 0)
            load_expert(1, 1)
            with sp.Fori(0, E // 2 - 1) as i:
                for half in range(2):
                    wait_apart(sp, s_y, i * UNITS + B * (half + 1) + START)
                    load_expert(i * 2 + 2 + half, half)
            for b in range(B):
                sp.wait_ge(s_sc[b], E * 32 + COPIED)
                sp.dma_start(fin[b][:, :, :], ROWS_P(acc_rows[b * S:(b + 1) * S, :])).then_inc(s_al[b], 16)
            for b in range(B):
                sp.wait_ge(s_fl, b + 1)
                sp.dma_start(ROWS_P(out[b * S:(b + 1) * S, :]), fin[b][:, :, :]).then_inc(s_out, 16)
            sp.wait_ge(s_out, B * 16)
            sp.wait_ge(s_x2, B * 16 + START)

        @blk.gpsimd
        def _(pool):
            steps = [0]

            def link(ins):
                steps[0] += 1
                ins.then_inc(s_pool, 1)
                pool.wait_ge(s_pool, steps[0])

            link(pool.memset(ident[:, :], 0.0))
            link(pool.affine_select(out=ident[:, :], in_=ident[:, :], compare_op=ALU.not_equal, fill=1.0,
                                    base=0, pattern=[[-1, P]], channel_multiplier=1))
            link(pool.memset(tri[:, :], 0.0))
            link(pool.affine_select(out=tri[:, :], in_=tri[:, :], compare_op=ALU.is_ge, fill=1.0,
                                    base=0, pattern=[[-1, P]], channel_multiplier=1))
            link(pool.iota(iota_f, pattern=[[1, CAP]], base=0, channel_multiplier=0,
                           allow_small_or_imprecise_dtypes=True))
            link(pool.tensor_copy(iota[:, :], iota_f))
            link(pool.tensor_copy(identb[:, :], ident[:, :]))
            link(pool.memset(onesb[:, :], 1.0))
            link(pool.iota(lane[:, :], pattern=[[0, 1]], base=0, channel_multiplier=1,
                           allow_small_or_imprecise_dtypes=True))
            pool.memset(mhalf[:, :], -0.5).then_inc(s_id, 1)
            for tile in (V[:, :, :, :], Vx[:, :, :], Vr[:, :, :]):
                link(pool.memset(tile, 0.0))
            link(pool.memset(V[:, :, :, HD:HD + 1], 1.0))
            link(pool.memset(Vx[:, :, HD:HD + 1], 1.0))
            link(pool.memset(Vr[:, :, HD:HD + 1], 1.0))
            link(pool.memset(kxst[:, :, :], 1.0))
            link(pool.memset(kxst[0:KQ, :, SK:160], 0.0))
            pool.memset(maskb[:, :, SK:160], MASKED).then_inc(s_ms, 1)

            def split(b, i0, i1):
                for i in range(i0, i1 + 1):
                    if i < i1:
                        p, r, cols = i % 2, i % RING, C * SK if i == 8 else N
                        if i >= 2:
                            wait_apart(pool, s_p4, b * PIECES + i - 1)
                        pool.wait_ge(s_p1, b * PIECES + i + 1)
                        pool.tensor_tensor(rest[:, p, 0:cols], full[:, p, 0:cols], part[:, r, 0, 0:cols],
                                           ALU.subtract).then_inc(s_p2, 1)
                    if i > i0:
                        i -= 1
                        p, r, cols = i % 2, i % RING, C * SK if i == 8 else N
                        pool.wait_ge(s_p3, b * PIECES + i + 1)
                        pool.tensor_tensor(part[:, r, 2, 0:cols], rest[:, p, 0:cols], part[:, r, 1, 0:cols],
                                           ALU.subtract).then_inc(s_p4, 1)

            def rsqrt(b, n):
                pool.wait_ge(s_z, b * 2 + n + 1)
                pool.tensor_tensor(rstd[:, :], ve[:, :], mhalf[:, :], ALU.pow).then_inc(s_rs, 1)

            def residual(b):
                wait_apart(pool, s_xl, b * 16 + 16)
                pool.tensor_tensor(xb[:, :, :], xb[:, :, :], brow[:, 1:2, :].to_broadcast([P, T, D]),
                                   ALU.add).then_inc(s_xb, 1)

            def mask_bias(b):
                wait_apart(pool, s_mi, b * 16 + 16)
                pool.tensor_scalar(maskb[:, :, 0:SK], mask_i[:, :, :], 0.0, MASKED, ALU.is_equal,
                                   ALU.mult).then_inc(s_mask, 1)

            def batch(b, more):
                rsqrt(b, 0)
                pool.wait_ge(s_ln, b * 2 * T + T)
                pool.tensor_tensor(xb[:, :, :], z[:, :, :], brow[:, 3:4, :].to_broadcast([P, T, D]),
                                   ALU.add).then_inc(s_xb, 1)
                split(b, 9, 13)
                if more:
                    split(b + 1, 0, 8)
                rsqrt(b, 1)
                if more:
                    split(b + 1, 8, 9)
                    mask_bias(b + 1)
                    residual(b + 1)

            pool.wait_ge(s_wb, 160)
            split(0, 0, 9)
            mask_bias(0)
            residual(0)
            with pool.Fori(0, B - 1) as b:
                batch(b, True)
            batch(B - 1, False)

            pool.wait_ge(s_x2, B * 16 + START)

            for b in range(B):
                rows = slice(b * S, (b + 1) * S)
                pool.dma_start(acc_rows[rows, :], x2_rows[rows, :]).then_inc(s_sc[b], COPIED)
            for b in range(B):
                pool.wait_ge(s_sc[b], COPIED)

            def gather(b, half):
                for j in range(2):
                    pool.indirect_dma_start(xg[b][:, j, :], None, x2_rows,
                                            bass.IndirectOffsetOnAxis(tok_g[half][:, b, j:j + 1], 0)
                                            ).then_inc(s_g[b], 16)

            def scatter(b, half):
                for j in range(2):
                    pool.indirect_dma_start(acc_rows, bass.IndirectOffsetOnAxis(tok_s[half][:, b, j:j + 1], 0),
                                            yg[b][:, j, :], None, compute_op=ALU.add).then_inc(s_sc[b], 16)

            def experts(i, last):
                for u in range(UNITS):
                    half, b = divmod(u, B)
                    more = not (last and half == 1)
                    if b == 0:
                        wait_apart(pool, s_tk, i * 4 + half * 2 + (3 if more else 2))
                    if more:
                        wait_apart(pool, s_gt, i * UNITS + u + 1 + START)
                        gather(b, 1 - half)
                    wait_apart(pool, s_ye, i * UNITS + u + 1 + START, s_sc[b], (i * 2 + half) * 32 + COPIED)
                    scatter(b, half)

            pool.wait_ge(s_tk, 1)
            for b in range(B):
                gather(b, 0)
            with pool.Fori(0, E // 2 - 1) as i:
                experts(i, False)
            experts(E // 2 - 1, True)
            for b in range(B):
                pool.wait_ge(s_fz, b + 1)
                pool.tensor_tensor(frstd[:, b, :], frstd[:, b, :], mhalf[:, :], ALU.pow).then_inc(s_fr, 1)

        @blk.scalar
        def _(act):
            def taken_before(at, idx):
                act.wait_ge(s_item, at.made(idx + 1))

            def copy_item(at, idx, dst, cols=N):
                taken_before(at, idx)
                act.activation(dst, PS[:, at.bank(idx), 0:cols], ACT.Copy).then_inc(s_eva, 1)

            def part1(at, b, i, cols):
                p, r = i % 2, i % RING
                act.wait_ge(s_evd, at.taken("D", at.piece(i) + 1))
                act.wait_ge(s_pw[r], 48 * (b * PIECES_OF[r] + (i // RING)) + START)
                act.activation(part[:, r, 0, 0:cols], full[:, p, 0:cols], ACT.Copy).then_inc(s_p1, 1)

            def part2(b, i, cols):
                p = i % 2
                act.wait_ge(s_p2, b * PIECES + i + 1 + START)
                act.activation(part[:, i % RING, 1, 0:cols], rest[:, p, 0:cols], ACT.Copy).then_inc(s_p3, 1)

            def attention(b, n0, units, scale):
                per = units // NG
                banks = BANKS_CROSS if n0 else BANKS_SELF
                for n in range(units + LAG + 1):
                    if n < units:
                        act.wait_ge(s_st, b * ST_ALL + n0 + n + 1)
                        if n0 + n >= 4:
                            act.wait_ge(s_pu, b * ST_ALL + n0 + n - 3)
                        act.activation(pT[:, n % 4, :], PS[:, banks[n], :], ACT.Exp,
                                       scale=scale).then_inc(s_ex, 1)
                    m = n - LAG - 1
                    if m >= 0 and m % per == per - 1:
                        k = m // per
                        act.wait_ge(s_pu, b * ST_ALL + n0 + m + 1)
                        if n0 == 0 and k == 0:
                            act.wait_ge(s_mask, b + 1 + START)
                        act.activation(oT[:, k, :], PS[:, 5 + k % 2, :],
                                       ACT.Copy).then_inc(s_ave, 1)

            def parts(at, b, i0, i1):
                for i in range(i0, i1 + 1):
                    if i < i1:
                        part1(at, b, i, C * SK if i == 8 else N)
                    if i > i0:
                        part2(b, i - 1, C * SK if i == 9 else N)

            def turned_half(at, name):
                for n in (1, 3):
                    copy_item(at, at.nth(name, n), xT[:, n // 2, (n % 2) * N:(n % 2 + 1) * N])

            def logits_exp(b):
                act.wait_ge(s_ls, b + 1)
                act.activation(lge[:, :, :], lg[:, :, :], ACT.Exp).then_inc(s_le, 1)

            def rest_of_batch(b, more):
                at = Place(EACH if more else LAST, b)
                turned_half(at, "oT")
                turned_half(at, "x1T")
                parts(at, b, 9, 13)
                attention(b, ST_SELF, ST_CROSS, SCALE_CROSS)
                if more:
                    parts(at, b + 1, 0, 8)
                if more:
                    parts(at, b + 1, 8, 9)
                logits_exp(b)
                if more:
                    attention(b + 1, 0, ST_SELF, SCALE_SELF)

            parts(Place(FIRST), 0, 0, 9)
            attention(0, 0, ST_SELF, SCALE_SELF)
            with act.Fori(0, B - 1) as b:
                rest_of_batch(b, True)
            rest_of_batch(B - 1, False)
            with act.Fori(0, E // 2) as i:
                for u in range(UNITS):
                    k = u % 2
                    act.wait_ge(s_y, i * UNITS + u - 1 + START)
                    for fh in range(2):
                        act.wait_ge(s_h, i * UNITS * 2 + 2 * u + fh + 1)
                        act.activation(hT[k][:, 2 * fh:2 * fh + 2, :].rearrange("p f j -> p (f j)"),
                                       PS[:, 2 + 2 * k + fh, :], ACT.Silu).then_inc(s_si, 1)
            for b in range(B):
                act.wait_ge(s_fb, b + 1)
                for t in range(T):
                    ins = act.activation(fin[b][:, t, :], fin[b][:, t, :], ACT.Identity,
                                         bias=fshift[:, b, t:t + 1], scale=frstd[:, b, t:t + 1])
                ins.then_inc(s_fl, 1)

        FIRST_STEPS = 4 + NG * 4
        DVE_STEPS = FIRST_STEPS + NG * 3 + 2 * (T + 2) + 4

        @blk.vector
        def _(dve):
            chain = {"before": 0, "steps": 0}

            def link(ins, how=wait):
                chain["steps"] += 1
                ins.then_inc(s_dve, 1)
                how(dve, s_dve, chain["before"] + chain["steps"])

            def ready(at, idx):
                dve.wait_ge(s_item, at.made(idx + 1))

            def copy_item(at, idx, dst, cols=N):
                ready(at, idx)
                dve.tensor_copy(dst, PS[:, at.bank(idx), 0:cols]).then_inc(s_evd, 1)

            def full_free(b, i):
                dve.wait_ge(s_p2, b * PIECES + max(0, i - 1) + START)

            def roped(at, b, i):
                half, name, c0 = i % 4 // 2, "qk"[i // 4], (2, 6)[i // 4]
                idx = at.nth(name, 4 * half)
                cols = slice(half * N, (half + 1) * N)
                dve.wait_ge(s_evd, at.taken("D", idx))
                for c in range(C):
                    ready(at, idx + c)
                    dve.scalar_tensor_tensor(out=by_cos[:, c, :], in0=PS[:, at.bank(idx + c), :],
                                             scalar=bcol[:, c0 + 2 + c:c0 + 3 + c], in1=cosT[:, cols],
                                             op0=ALU.add, op1=ALU.mult)
                    dve.scalar_tensor_tensor(out=by_sin[:, c, :], in0=PS[:, at.bank(idx + c), :],
                                             scalar=bcol[:, c0 + 2 + c:c0 + 3 + c], in1=sinT[:, cols],
                                             op0=ALU.add, op1=ALU.mult).then_inc(s_evd, 1)
                dve.wait_ge(s_evd, at.taken("D", idx + 2))
                dve.tensor_tensor(by_cos[:, 0, :], by_cos[:, 0, :], by_sin[:, 1, :], ALU.subtract)
                link(dve.tensor_tensor(by_cos[:, 1, :], by_cos[:, 1, :], by_sin[:, 0, :], ALU.add))
                for c in range(C):
                    full_free(b, i + c)
                    ready(at, idx + 2 + c)
                    dve.scalar_tensor_tensor(out=full[:, c, :], in0=PS[:, at.bank(idx + 2 + c), :],
                                             scalar=bcol[:, c0 + c:c0 + c + 1], in1=by_cos[:, c, :],
                                             op0=ALU.add, op1=ALU.add).then_inc(s_evd, 1)

            def attention(b, n0, g0, order, cross):
                sm_group = (SM_CROSS if cross else SM_SELF) // NG
                for what, n in order:
                    if what == "logits" and n == T - 1:
                        shift_logits(b - 1)
                    if what == "smax":
                        if order is ORDER_NEXT and n == sm_group - 1:
                            softmax_experts(b - 1)
                        dve.wait_ge(s_sm, b * SM_ALL + n0 + n + 1)
                        g, k = divmod(n, sm_group)
                        if cross:
                            j, t0, nt = k // 3, 3 * (k % 3), min(3, T - 3 * (k % 3))
                            dve.tensor_reduce(nmf[:, t0:t0 + nt, j:j + 1],
                                              PS[:, n % 3, 0:nt * SK].rearrange("p (t k) -> p t k", k=SK),
                                              AX.X, ALU.max, negate=True).then_inc(s_smu, 1)
                        else:
                            j, t, half = k // (T * HALVES), k // HALVES % T, k % HALVES
                            dve.tensor_reduce(mh[:, 0, t, j, half:half + 1], PS[:, n % 3, :],
                                              AX.X, ALU.max).then_inc(s_smu, 1)
                        if k == sm_group - 1:
                            p = (g0 + g) % 2
                            dve.wait_ge(s_smu, b * SM_ALL + n0 + n + 1)
                            if not cross:
                                link(dve.tensor_reduce(nmf[:, :, :], mh[:, 0, :, :, :], AX.X, ALU.max,
                                                          negate=True))
                            dve.wait_ge(s_nt, b * 2 * NG + max(0, g0 + g - 1) + START)
                            link(dve.tensor_copy(nmp[:, p, :, 0:G], nmf[:, :, :]))
                            link(dve.tensor_tensor(nmr[:, :, :], nmf[:, :, :], nmp[:, p, :, 0:G],
                                                      ALU.subtract))
                            link(dve.tensor_copy(nmp[:, p, :, G:2 * G], nmr[:, :, :]))
                            dve.tensor_tensor(nmp[:, p, :, 2 * G:3 * G], nmr[:, :, :], nmp[:, p, :, G:2 * G],
                                              ALU.subtract).then_inc(s_nm, 1)
                    elif what == "turn":
                        dve.wait_ge(s_nt, b * 2 * NG + g0 + n + 1 + START)
                        m = g0 + n
                        dve.wait_ge(s_nl[m % 2], 48 * (b * NG + m // 2) + START)
                        dve.tensor_copy(nmT[:, m % 2, :], PS[0:3 * G, 7, :].bitcast(BF16)).then_inc(s_ne, 1)

            def heads_out(at, b, name, n0, n1):
                if n0 == 0:
                    if name == "ox":
                        dve.wait_ge(s_xb, b * 2 + 2 + START)
                    else:
                        dve.wait_ge(s_x2, b * 16 + START)
                        dve.wait_ge(s_xb, b * 2 + 1 + START)
                for n in range(n0, n1):
                    idx, (chunk, c) = at.nth(name, n), divmod(n, 4)
                    ready(at, idx)
                    heads = PS[:, at.bank(idx), :].rearrange("p (h a k) -> p a h k", a=HALVES, k=V32)
                    sums = rz[:, n % 2, :].rearrange("p (a h) -> p a h", a=HALVES)
                    link(dve.reciprocal(sums, heads[:, :, :, HD]))
                    for a in range(HALVES):
                        ins = dve.tensor_tensor(
                            z[:, a * 4 + c, chunk * P:(chunk + 1) * P].rearrange("p (h k) -> p h k", k=HD),
                            heads[:, a, :, 0:HD],
                            sums[:, a, :].rearrange("p (h k) -> p h k", k=1).to_broadcast([P, H // 2, HD]), ALU.mult)
                    ins.then_inc(s_evd, 1)

            def residual_sum(at, name):
                for k in range(4):
                    idx = at.nth(name, k)
                    ready(at, idx)
                    dve.tensor_tensor(z[:, 2 * k:2 * k + 2, :],
                                      PS[:, at.bank(idx), :].rearrange("p (t d) -> p t d", t=2),
                                      xb[:, 2 * k:2 * k + 2, :], ALU.add).then_inc(s_evd, 1)
                    dve.wait_ge(s_evd, at.taken("D", idx + 1))
                    for t in (2 * k, 2 * k + 1):
                        ins = dve.bn_stats(st6[:, t, :], z[:, t, :])
                link(ins, wait_apart)
                for t in range(T):
                    ins = dve.bn_aggr(mv[:, t, :], st6[:, t, :])
                link(ins)
                dve.tensor_scalar(ve[:, :], mv[:, :, 1], EPS, None, ALU.add).then_inc(s_z, 1)

            def normalise(b, n):
                dve.wait_ge(s_rs, b * 2 + n + 1)
                for t in range(T):
                    dve.tensor_scalar(z[:, t, :], z[:, t, :], mv[:, t, 0:1], rstd[:, t:t + 1],
                                      ALU.subtract, ALU.mult).then_inc(s_ln, 1)

            def turn_in(at):
                for n in range(4):
                    copy_item(at, at.nth("xT", n), xTf[:, n // 2, (n % 2) * N:(n % 2 + 1) * N])

            def latents(at):
                for name, dst, col in (("ctq", ctq, 0), ("ctkv", ctkv, 1)):
                    for half in range(HALVES):
                        idx = at.nth(name, half)
                        ready(at, idx)
                        dve.tensor_scalar(dst[:, half * N:(half + 1) * N], PS[:, at.bank(idx), :],
                                          bcol[:, col:col + 1], None, ALU.add).then_inc(s_evd, 1)

            def turned_half(at, name):
                for n in (0, 2):
                    copy_item(at, at.nth(name, n), xT[:, n // 2, (n % 2) * N:(n % 2 + 1) * N])

            def turn_ctx(at):
                copy_item(at, at.nth("ctxT"), cxT[:, :, :].rearrange("p c n -> p (c n)"), C * SK)

            def values(at, b):
                for k in range(4):
                    idx = at.nth("v", k)
                    ready(at, idx)
                    for t in range(2):
                        ins = dve.tensor_tensor(
                            V[:, 2 * k + t, :, 0:HD],
                            PS[:, at.bank(idx), t * D:(t + 1) * D].rearrange("p (h d) -> p h d", d=HD),
                            brow[:, 0, :].rearrange("p (h d) -> p h d", d=HD), ALU.add)
                    ins.then_inc(s_evd, 1)
                idx = at.nth("kx")
                ready(at, idx)
                full_free(b, 8)
                for c in range(C):
                    ins = dve.tensor_scalar(full[:, 0, c * SK:(c + 1) * SK],
                                            PS[:, at.bank(idx), c * SK:(c + 1) * SK],
                                            bcol[:, 10 + c:11 + c], None, ALU.add)
                ins.then_inc(s_evd, 1)
                idx = at.nth("vx")
                ready(at, idx)
                dve.tensor_tensor(Vx[:, :, 0:HD], PS[:, at.bank(idx), 0:D].rearrange("p (h d) -> p h d", d=HD),
                                  brow[:, 2, :].rearrange("p (h d) -> p h d", d=HD), ALU.add).then_inc(s_evd, 1)
                idx = at.nth("vxr")
                ready(at, idx)
                for j in range(TILES):
                    rows = slice(V32 * j, V32 * j + SKR)
                    ins = dve.tensor_tensor(
                        Vr[rows, :, 0:HD],
                        PS[rows, at.bank(idx), 0:D].rearrange("p (g j d) -> p g j d", j=G, d=HD)[:, :, j // HALVES, :],
                        brow[rows, 2, :].rearrange("p (g j d) -> p g j d", j=G, d=HD)[:, :, j // HALVES, :], ALU.add)
                ins.then_inc(s_evd, 1)

            def shift_logits(b):
                wait_apart(dve, s_lo, b + 1)
                lgp = PS[:, 6, 0:T * E].rearrange("p (t e) -> p t e", e=E)
                link(dve.tensor_reduce(lgm[:, :], lgp, AX.X, ALU.max))
                dve.tensor_tensor(lg[:, :, :], lgp,
                                  lgm[:, :].rearrange("p (t e) -> p t e", e=1).to_broadcast([P, T, E]),
                                  ALU.subtract).then_inc(s_ls, 1)

            def softmax_experts(b):
                wait_apart(dve, s_le, b + 1)
                link(dve.tensor_reduce(lgs[:, :], lge[:, :, :], AX.X, ALU.add))
                link(dve.reciprocal(lgm[:, :], lgs[:, :]))
                link(dve.tensor_tensor(prob[:, :, bass.ds(b * E, E)], lge[:, :, :],
                                       lgm[:, :].rearrange("p (t e) -> p t e", e=1).to_broadcast([P, T, E]),
                                       ALU.mult))

            def rest_of_batch(b, more):
                at = Place(EACH if more else LAST, b)
                chain["before"], chain["steps"] = b * DVE_STEPS + FIRST_STEPS, 0
                heads_out(at, b, "o", 0, T)
                turned_half(at, "oT")
                residual_sum(at, "y")
                normalise(b, 0)
                turned_half(at, "x1T")
                for i in range(9, 13):
                    idx = at.piece(i)
                    ready(at, idx)
                    full_free(b, i)
                    c = (i - 9) // 2
                    dve.tensor_scalar(full[:, i % 2, :], PS[:, at.bank(idx), :], bcol[:, 12 + c:13 + c], None,
                                      ALU.add).then_inc(s_evd, 1)
                if more:
                    turn_in(at)
                    turn_ctx(at)
                    latents(at)
                attention(b, SM_SELF, NG, ORDER_CROSS, True)
                if more:
                    for i in (0, 2, 4):
                        roped(at, b + 1, i)
                heads_out(at, b, "ox", 0, T)
                if more:
                    roped(at, b + 1, 6)
                for n in range(4):
                    copy_item(at, at.nth("oxT", n), xT[:, n // 2, (n % 2) * N:(n % 2 + 1) * N])
                residual_sum(at, "yx")
                if more:
                    values(at, b + 1)
                normalise(b, 1)
                for n in range(4):
                    copy_item(at, at.nth("x2T", n), xT[:, n // 2, (n % 2) * N:(n % 2 + 1) * N])
                if more:
                    attention(b + 1, 0, 0, ORDER_NEXT, False)
                else:
                    shift_logits(b)
                    softmax_experts(b)
                assert chain["steps"] == DVE_STEPS - (0 if more else FIRST_STEPS)

            dve.wait_ge(s_id, 1)
            at = Place(FIRST)
            turn_in(at)
            turn_ctx(at)
            dve.wait_ge(s_wa, 48)
            latents(at)
            dve.wait_ge(s_wb, 160)
            for i in range(0, 8, 2):
                roped(at, 0, i)
            dve.wait_ge(s_ms, 1)
            values(at, 0)
            attention(0, 0, 0, ORDER_SELF, False)
            assert chain["steps"] == FIRST_STEPS
            with dve.Fori(0, B - 1) as b:
                rest_of_batch(b, True)
            rest_of_batch(B - 1, False)

            made = [0]

            def link_r(ins):
                made[0] += 1
                ins.then_inc(s_r, 1)
                dve.wait_ge(s_r, made[0])

            def over_tiles(ap):
                return ap.rearrange("p (t n) -> p t n", t=1).to_broadcast([P, T, BE])

            def per_expert(ap):
                return PS[:, ap, 0:BE]

            dve.wait_ge(s_pu, B * ST_ALL)
            link_r(dve.memset(thr.bitcast(I32), 0))
            link_r(dve.memset(bit.bitcast(I32), 1 << (BITS - 1)))
            before = made[0]
            with dve.Fori(0, BITS) as n:
                dve.tensor_tensor(cand.bitcast(I32), thr.bitcast(I32), bit.bitcast(I32),
                                  ALU.bitwise_or).then_inc(s_r, 1)
                dve.wait_ge(s_r, n * 3 + before + 1)
                dve.tensor_tensor(above[:, :, :], prob[:, :, :], over_tiles(cand), ALU.is_ge).then_inc(s_in, 1)
                dve.tensor_scalar(bit.bitcast(I32), bit.bitcast(I32), 1, None,
                                  ALU.logical_shift_right)
                dve.wait_ge(s_cn, n + 1)
                dve.scalar_tensor_tensor(out=hit, in0=PS[:, 0, 0:BE], scalar=float(CAP), in1=cand,
                                         op0=ALU.is_ge, op1=ALU.mult).then_inc(s_r, 1)
                dve.wait_ge(s_r, n * 3 + before + 2)
                dve.tensor_tensor(thr, thr, hit, ALU.max).then_inc(s_r, 1)
                dve.wait_ge(s_r, n * 3 + before + 3)
            made[0] = before + 3 * BITS
            link_r(dve.tensor_tensor(above[:, :, :], prob[:, :, :], over_tiles(thr), ALU.is_gt))
            dve.tensor_tensor(equal[:, :, :], prob[:, :, :], over_tiles(thr), ALU.is_equal).then_inc(s_in, 1)
            dve.wait_ge(s_cn, BITS + 1)
            link_r(dve.tensor_scalar(hit, PS[:, 0, 0:BE], -1.0, float(CAP), ALU.mult, ALU.add))
            ranks = PS[:, 1, 0:T * BE].rearrange("p (t n) -> p t n", n=BE)
            link_r(dve.tensor_tensor(pos[:, :, :], ranks, over_tiles(hit), ALU.is_lt))
            link_r(dve.tensor_tensor(pos[:, :, :], pos[:, :, :], equal[:, :, :], ALU.mult))
            dve.tensor_tensor(chosen[:, :, :], pos[:, :, :], above[:, :, :], ALU.add).then_inc(s_in, 1)
            dve.wait_ge(s_in, BITS + 2)
            for t in range(T):
                for b in range(B):
                    dve.memset(picks[:, t, b * E:(b + 1) * E, 1], float(b * T + t))
            dve.tensor_scalar(picks[:, :, :, 0], prob[:, :, :], 0.0, lane[:, 0:1], ALU.mult, ALU.add)
            link_r(dve.tensor_copy(picks[:, :, :, 2], prob[:, :, :]))
            link_r(dve.tensor_tensor(pos[:, :, :], prob[:, :, :], picks[:, :, :, 2], ALU.subtract))
            link_r(dve.tensor_copy(picks[:, :, :, 3], pos[:, :, :]))
            link_r(dve.tensor_tensor(picks[:, :, :, 4], pos[:, :, :], picks[:, :, :, 3], ALU.subtract))
            dve.wait_ge(s_cn, BITS + 2)
            link_r(dve.scalar_tensor_tensor(out=pos[:, :, :], in0=ranks, scalar=1.0, in1=chosen[:, :, :],
                                            op0=ALU.add, op1=ALU.mult))
            link_r(dve.tensor_scalar(pos[:, :, :], pos[:, :, :], 1.0, None, ALU.subtract))

            def choose(n, e, b):
                wait_apart(dve, s_pk, n - 1 + START)
                for t in range(T):
                    ins = dve.tensor_scalar(onehot[b % 2][:, t, :], iota[:, :], pos[:, t, bass.ds(e + b * E, 1)],
                                            None, ALU.is_equal)
                ins.then_inc(s_oh, 1)

            def take_choice(e, half, link):
                wait_apart(dve, s_pk, (e + 1) * B + START)
                dve.tensor_copy(picked[:, :, :, :].rearrange("p b j c -> p (b j c)"),
                                PS[:, 1, 0:B * 2 * COLS]).then_inc(s_pe2, 1)
                dve.wait_ge(s_pe2, e + 1 + START)
                col = lambda c: picked[:, :, :, c]
                tokf3 = tokf.rearrange("p (b j) -> p b j", j=2)
                link(dve.scalar_tensor_tensor(out=tokf3, in0=col(1), scalar=float(P), in1=col(0),
                                              op0=ALU.mult, op1=ALU.add))
                dve.tensor_scalar(tok_g[half][:, :, :], tokf3, 0.0, None, ALU.add).then_inc(s_tk, 1)
                link(dve.tensor_tensor(gate[half][:, :, :], col(2), col(3), ALU.add))
                link(dve.tensor_tensor(gate[half][:, :, :], gate[half][:, :, :], col(4), ALU.add))

            def scatter_tokens(half):
                dve.tensor_copy(tok_s[half][:, :, :], tok_g[half][:, :, :]).then_inc(s_tk, 1)

            def turned(n, k):
                dve.wait_ge(s_gt, n + 1 + START)
                dve.tensor_copy(xgT[k].rearrange("p c j -> p (c j)"), PS[:, 0, :]).then_inc(s_te, 1)

            def gated(n, e, b, half):
                wait_apart(dve, s_y, n + 1 + START, s_sc[b], e * 32 + COPIED)
                for j in range(2):
                    ins = dve.tensor_scalar(yg[b][:, j, :], PS[:, 6 + b % 2, j * D:(j + 1) * D],
                                            gate[half][:, b, j:j + 1], None, ALU.mult)
                ins.then_inc(s_ye, 1)

            for e in range(2):
                for b in range(B):
                    choose(e * B + b, e, b)
                take_choice(e, e, link_r)
                if e == 0:
                    dve.wait_ge(s_tk, 1)
                    scatter_tokens(0)
            turned(0, 0)
            turned(1, 1)
            STEPS = 2 * 3
            before = made[0]

            def experts(i, last):
                linked = [0]

                def link_e(ins):
                    linked[0] += 1
                    ins.then_inc(s_r, 1)
                    dve.wait_ge(s_r, i * STEPS + before + linked[0])

                for u in range(UNITS):
                    half, b = divmod(u, B)
                    n, e = i * UNITS + u, i * 2 + half
                    if not (last and u + 2 >= UNITS):
                        turned(n + 2, u % 2)
                    if not last:
                        choose(n + 2 * B, e + 2, b)
                    gated(n, e, b, half)
                    if b == B - 1 and not (last and half == 1):
                        dve.wait_ge(s_tk, i * 4 + half * 2 + 3)
                        scatter_tokens(1 - half)
                        if not last:
                            take_choice(e + 2, half, link_e)

            with dve.Fori(0, E // 2 - 1) as i:
                experts(i, False)
            experts(E // 2 - 1, True)

            base = before + (E // 2 - 1) * STEPS
            made[0] = base
            for b in range(B):
                dve.wait_ge(s_al[b], 16)
                for t in range(T):
                    ins = dve.bn_stats(st6[:, t, :], fin[b][:, t, :])
                link_r(ins)
                for t in range(T):
                    ins = dve.bn_aggr(fmv[:, b, t, :], st6[:, t, :])
                link_r(ins)
                dve.tensor_scalar(frstd[:, b, :], fmv[:, b, :, 1], EPS, None, ALU.add).then_inc(s_fz, 1)
                dve.wait_ge(s_fr, b + 1)
                dve.scalar_tensor_tensor(out=fshift[:, b, :], in0=fmv[:, b, :, 0], scalar=-1.0,
                                         in1=frstd[:, b, :], op0=ALU.mult, op1=ALU.mult).then_inc(s_fb, 1)

        @blk.tensor
        def _(pe):
            def wait_taken(at, engine, upto):
                count = at.plan.taken(engine, upto)
                if count > at.waited.get(engine, -1):
                    at.waited[engine] = count
                    pe.wait_ge({"A": s_eva, "D": s_evd}[engine], at.taken(engine, upto))

            def item(at, idx):
                old = idx - 8
                if old >= at.plan.start[idx]:
                    wait_taken(at, at.plan.items[old][1], old + 1)
                return PS[:, at.bank(idx), :]

            def taken_upto(at, idx):
                wait_taken(at, "A", idx)
                wait_taken(at, "D", idx)

            def turn_tokens(at, name, src, per_tile=None):
                for n in range(4):
                    idx = at.nth(name, n)
                    for k in range(4):
                        t = 4 * (n % 2) + k
                        if per_tile is not None and n % 2 == 0:
                            per_tile(n // 2, t)
                        if k == 0:
                            ps = item(at, idx)
                        ins = pe.transpose(ps[:, k * P:(k + 1) * P], src[:, t, (n // 2) * P:(n // 2 + 1) * P],
                                           ident[:, :])
                    ins.then_inc(s_item, 1)

            def project(at, idx, w, rhs, half, m, cols=N):
                ps = item(at, idx)
                for c in range(C):
                    ins = pe.matmul(ps[:, 0:cols], w[:, c, m * P:(m + 1) * P], rhs[:, c, half * N:half * N + cols],
                                    start=(c == 0), stop=(c == C - 1))
                ins.then_inc(s_item, 1)

            def attention(b, n0, u0, g0, order, cross):
                sm_group = (SM_CROSS if cross else SM_SELF) // NG
                per = (ST_CROSS if cross else ST_SELF) // NG
                banks, before = (BANKS_CROSS, BEFORE_CROSS) if cross else (BANKS_SELF, BEFORE_SELF)
                for what, n in order:
                    if what == "logits":
                        logits(n, b - 1)
                    elif what == "smax":
                        g, k = divmod(n, sm_group)
                        if k == 0 and g * G % 8 == 0:
                            if cross:
                                pe.wait_ge(s_mask, b + 1 + START)
                                pe.wait_ge(s_ql[g * G // 8], b * 192 + 192)
                                pe.wait_ge(s_kx, b * 192 + 192)
                            else:
                                pe.wait_ge(s_ql[g * G // 8], b * 192 + 96)
                                pe.wait_ge(s_kl[g * G // 8], b * 96 + 96)
                        if n >= 3:
                            pe.wait_ge(s_smu, b * SM_ALL + n0 + n - 2)
                        ps = PS[:, n % 3, :]
                        if cross:
                            h, t0 = g * G + k // 3, 3 * (k % 3)
                            nt = min(3, T - t0)
                            pe.matmul(ps[:, 0:nt * SK], identb[:, :], maskb[:, t0:t0 + nt, 0:SK],
                                      start=True, stop=False, skip_group_check=True)
                            for t in range(t0, t0 + nt):
                                ins = pe.matmul(ps[:, (t - t0) * SK:(t - t0 + 1) * SK],
                                                qst[0:KQ, h, t * P:(t + 1) * P], kxst[0:KQ, h, 0:SK],
                                                start=False, stop=(t == t0 + nt - 1), skip_group_check=True)
                        else:
                            h, t, half = g * G + k // (T * HALVES), k // HALVES % T, k % HALVES
                            ins = pe.matmul(ps, qst[0:KQ, h, t * P:(t + 1) * P],
                                            kst[0:KQ, h, half * N:(half + 1) * N], start=True, stop=True)
                        ins.then_inc(s_sm, 1)
                    elif what == "turn":
                        m = g0 + n
                        pe.wait_ge(s_nm, b * 2 * NG + m + 1)
                        pe.wait_ge(s_ne, b * 2 * NG + m + START)
                        rows = PS[0:3 * G, 7, :].bitcast(BF16)
                        for t in range(T):
                            ins = pe.transpose(rows[:, t * P:(t + 1) * P], nmp[:, m % 2, t, :], identb[:, :])
                        ins.then_inc(s_nt, 1)
                    elif what == "st":
                        g, k = divmod(n, per)
                        head, half = g * G + k % TILES // HALVES, k % HALVES
                        cols = slice(half * N, (half + 1) * N)
                        if k == 0:
                            if not cross and g == 0:
                                pe.wait_ge(s_on, b * 16 + 16)
                            m = g0 + g
                            pe.wait_ge(s_nl[m % 2], 48 * (b * NG + m // 2 + 1) + START)
                        if before[n] is not None:
                            pe.wait_ge(s_ex, b * ST_ALL + u0 + before[n] + 1)
                        elif banks[n] < 3:
                            pe.wait_ge(s_smu, b * SM_ALL + n0 + (SM_CROSS if cross else SM_SELF))
                        ps = PS[:, banks[n], :]
                        if not cross:
                            kc = k // TILES
                            ins = pe.matmul(ps, kst[0:KM, head, kc * P:(kc + 1) * P],
                                            qst[0:KM, head, cols], start=True, stop=True)
                        elif k < TILES:
                            for t in range(4):
                                pe.matmul(ps[:, t * P:(t + 1) * P], maskb[:, 4 * half + t, 0:P], identb[:, :],
                                          start=(t == 0), stop=False, skip_group_check=True)
                            ins = pe.matmul(ps, kxst[0:KM, head, 0:P], qst[0:KM, head, cols],
                                            start=False, stop=True, skip_group_check=True)
                        else:
                            for j in range(TILES):
                                head, half = g * G + j // HALVES, j % HALVES
                                cols = slice(half * N, (half + 1) * N)
                                rows = PS[V32 * j:V32 * (j + 1), banks[n], :]
                                for t in range(4):
                                    pe.matmul(rows[:, t * P:(t + 1) * P], maskb[:, 4 * half + t, P:P + V32],
                                              identb[:, :], start=(t == 0), stop=False, skip_group_check=True,
                                              tile_position=(0, V32 * j))
                                ins = pe.matmul(rows, kxst[0:KM, head, P:P + V32], qst[0:KM, head, cols],
                                                start=False, stop=True, skip_group_check=True,
                                                tile_position=(0, V32 * j))
                        ins.then_inc(s_st, 1)
                    else:
                        g, k = divmod(n, per)
                        (wait_apart if cross and k == TILES else wait)(pe, s_ex, b * ST_ALL + u0 + n + 1)
                        if k == 0 and g >= 2:
                            pe.wait_ge(s_ave, b * 2 * NG + (NG if cross else 0) + g - 1)
                        av = PS[:, 5 + g % 2, :]
                        if not cross:
                            kc, j = divmod(k, TILES)
                            ins = pe.matmul(av[V32 * j:V32 * (j + 1), :], V[:, kc, g * G + j // HALVES, :], pT[:, n % 4, :],
                                            start=(kc == 0), stop=(kc == T - 1), tile_position=(0, V32 * j),
                                            skip_group_check=True)
                        elif k < TILES:
                            ins = pe.matmul(av[V32 * k:V32 * (k + 1), :], Vx[:, g * G + k // HALVES, :], pT[:, n % 4, :],
                                            start=True, stop=False, tile_position=(0, V32 * k),
                                            skip_group_check=True)
                        else:
                            for j in range(TILES):
                                rows = slice(V32 * j, V32 * j + SKR)
                                ins = pe.matmul(av[V32 * j:V32 * (j + 1), :], Vr[rows, g, :], pT[rows, n % 4, :],
                                                start=False, stop=True, skip_group_check=True,
                                                tile_position=(V32 * j, V32 * j))
                        ins.then_inc(s_pu, 1)

            def close_stage(b, cross):
                pe.wait_ge(s_smu, b * SM_ALL + (SM_ALL if cross else SM_SELF))
                pe.wait_ge(s_ex, b * ST_ALL + (ST_ALL if cross else ST_SELF))
                pe.wait_ge(s_ave, b * 2 * NG + (2 if cross else 1) * NG)
                pe.wait_ge(s_ne, b * 2 * NG + (2 if cross else 1) * NG + START)

            def o_tiles(at, name, n0, n1):
                for n in range(n0, n1):
                    idx, (chunk, c) = at.nth(name, n), divmod(n, 4)
                    ps = item(at, idx)
                    for k in range(4):
                        ins = pe.transpose(ps[:, k * P:(k + 1) * P], oT[:, chunk * 4 + k, c * P:(c + 1) * P],
                                           ident[:, :])
                    ins.then_inc(s_item, 1)

            def turn_heads(at, o_name, t_name):
                turn_tokens(at, t_name, z, lambda chunk, t: wait_taken(
                    at, "D", at.nth(o_name, chunk * 4 + t % 4) + 1))

            def output(at, t_name, y_name, w):
                taken_upto(at, at.nth(t_name, 3) + 1)
                for k in range(4):
                    idx = at.nth(y_name, k)
                    ps = item(at, idx)
                    for t in (2 * k, 2 * k + 1):
                        for c in range(C):
                            ins = pe.matmul(ps[:, (t % 2) * D:(t % 2 + 1) * D], xT[:, c, t * P:(t + 1) * P],
                                            w[:, c, :], start=(c == 0), stop=(c == C - 1))
                    ins.then_inc(s_item, 1)

            def turn_in(at, b):
                pe.wait_ge(s_x, b * 48 + 48)
                turn_tokens(at, "xT", x)

            def turn_ctx(at):
                ps = item(at, at.nth("ctxT"))
                for c in range(C):
                    pe.transpose(ps[:, c * SK:c * SK + P], cx[:, 0, c * P:(c + 1) * P], ident[:, :])
                    ins = pe.transpose(ps[:, c * SK + P:(c + 1) * SK], cx[0:SKR, 1, c * P:(c + 1) * P],
                                       ident[0:SKR, 0:SKR])
                ins.then_inc(s_item, 1)

            def latents(at):
                taken_upto(at, at.nth("xT", 3) + 1)
                for name, w in (("ctq", wdq), ("ctkv", wdkv)):
                    for half in range(HALVES):
                        project(at, at.nth(name, half), w, xTf, half, 0)

            def operands(at, name, half):
                latent, up = (ctq, wuq) if name == "q" else (ctkv, wuk)
                taken_upto(at, at.nth("ctkv", 1) + 1)
                idx = at.nth(name, 4 * half)
                cols = slice(half * N, (half + 1) * N)
                for m in range(C):
                    if name == "k":
                        project(at, idx + m, wkr, xTf, half, m)
                    else:
                        pe.matmul(item(at, idx + m), wqr[:, m * P:(m + 1) * P], latent[:, cols],
                                  start=True, stop=True).then_inc(s_item, 1)
                for m in range(C):
                    pe.matmul(item(at, idx + 2 + m), up[:, m * P:(m + 1) * P], latent[:, cols],
                              start=True, stop=True).then_inc(s_item, 1)

            def values(at):
                for k in range(4):
                    ps = item(at, at.nth("v", k))
                    for t in (2 * k, 2 * k + 1):
                        ins = pe.matmul(ps[:, (t % 2) * D:(t % 2 + 1) * D], ctkv[:, t * P:(t + 1) * P], wuv[:, :],
                                        start=True, stop=True)
                    ins.then_inc(s_item, 1)
                ps = item(at, at.nth("kx"))
                taken_upto(at, at.nth("ctxT") + 1)
                for m in range(C):
                    for c in range(C):
                        ins = pe.matmul(ps[:, m * SK:(m + 1) * SK], w1x[:, c, m * P:(m + 1) * P], cxT[:, c, :],
                                        start=(c == 0), stop=(c == C - 1))
                ins.then_inc(s_item, 1)
                ps = item(at, at.nth("vx"))
                for c in range(C):
                    ins = pe.matmul(ps[:, 0:D], cxT[:, c, 0:P], w2x[:, c, :], start=(c == 0), stop=(c == C - 1))
                ins.then_inc(s_item, 1)
                ps = item(at, at.nth("vxr"))
                for j in range(TILES):
                    for c in range(C):
                        ins = pe.matmul(ps[V32 * j:V32 * j + SKR, 0:D], cxT[:, c, P:SK], w2x[:, c, :],
                                        start=(c == 0), stop=(c == C - 1), tile_position=(0, V32 * j),
                                        skip_group_check=True)
                ins.then_inc(s_item, 1)

            def logits(t, b):
                for c in range(C):
                    ins = pe.matmul(PS[:, 6, t * E:(t + 1) * E], xT[:, c, t * P:(t + 1) * P], wch[:, c, :],
                                    start=(c == 0), stop=(c == C - 1))
                if t == T - 1:
                    ins.then_inc(s_lo, 1)

            def self_attention(at, b, order):
                taken_upto(at, len(at.plan.items))
                attention(b, 0, 0, 0, order, False)
                close_stage(b, False)

            def rest_of_batch(b, more):
                at = Place(EACH if more else LAST, b)
                o_tiles(at, "o", 0, T)
                turn_heads(at, "o", "oT")
                output(at, "oT", "y", wo)
                pe.wait_ge(s_ln, b * 2 * T + T)
                turn_tokens(at, "x1T", z)
                taken_upto(at, at.nth("x1T", 3) + 1)
                for i in range(4):
                    project(at, at.nth("qx", i), w0, xT, i % 2, i // 2)
                if more:
                    turn_in(at, b + 1)
                    turn_ctx(at)
                    latents(at)
                taken_upto(at, at.nth("ctkv" if more else "qx", -1) + 1)
                attention(b, SM_SELF, ST_SELF, NG, ORDER_CROSS, True)
                close_stage(b, True)
                if more:
                    operands(at, "q", 0)
                    operands(at, "q", 1)
                    operands(at, "k", 0)
                o_tiles(at, "ox", 0, T)
                if more:
                    operands(at, "k", 1)
                turn_heads(at, "ox", "oxT")
                output(at, "oxT", "yx", w3)
                if more:
                    values(at)
                pe.wait_ge(s_ln, b * 2 * T + 2 * T)
                turn_tokens(at, "x2T", z)
                if more:
                    self_attention(at, b + 1, ORDER_NEXT)
                else:
                    taken_upto(at, at.nth("x2T", 3) + 1)
                    for t in range(T):
                        logits(t, b)

            pe.wait_ge(s_id, 1)
            at = Place(FIRST)
            turn_in(at, 0)
            turn_ctx(at)
            pe.wait_ge(s_wa, 48)
            latents(at)
            pe.wait_ge(s_wb, 160)
            for name in "qk":
                for half in range(HALVES):
                    operands(at, name, half)
            values(at)
            pe.wait_ge(s_w, 64)
            pe.wait_ge(s_ms, 1)
            self_attention(at, 0, ORDER_SELF)
            with pe.Fori(0, B - 1) as b:
                rest_of_batch(b, True)
            rest_of_batch(B - 1, False)
            def count(ps, src):
                for t in range(T):
                    ins = pe.matmul(ps, onesb[:, :], src[:, t, :], start=(t == 0), stop=(t == T - 1))
                return ins

            def prefix(src):
                for t in range(T):
                    ps = PS[:, 1, t * BE:(t + 1) * BE]
                    for k in range(t):
                        pe.matmul(ps, onesb[:, :], src[:, k, :], start=(k == 0), stop=False)
                    ins = pe.matmul(ps, tri[:, :], src[:, t, :], start=(t == 0), stop=True)
                return ins

            pe.wait_ge(s_ls, B)
            with pe.Fori(0, BITS) as n:
                pe.wait_ge(s_in, n + 1)
                count(PS[:, 0, 0:BE], above).then_inc(s_cn, 1)
            pe.wait_ge(s_in, BITS + 1)
            count(PS[:, 0, 0:BE], above)
            prefix(equal).then_inc(s_cn, 1)
            pe.wait_ge(s_in, BITS + 2)
            prefix(chosen).then_inc(s_cn, 1)

            def pick(n, e, b):
                wait_apart(pe, s_oh, n + 1)
                if b == 0:
                    pe.wait_ge(s_pe2, e + START)
                for j in range(2):
                    for t in range(T):
                        ins = pe.matmul(PS[:, 1, (b * 2 + j) * COLS:(b * 2 + j + 1) * COLS],
                                        onehot[b % 2][:, t, j * P:(j + 1) * P],
                                        picks[:, t, bass.ds(e + b * E, 1), 0:COLS].rearrange("p a c -> p (a c)"),
                                        start=(t == 0), stop=(t == T - 1))
                ins.then_inc(s_pk, 1)

            def turn_rows(n, e, b):
                pe.wait_ge(s_g[b], e * 32 + 32)
                pe.wait_ge(s_te, n + START)
                for c in range(C):
                    for j in range(2):
                        ins = pe.transpose(PS[:, 0, c * CAP + j * P:c * CAP + (j + 1) * P],
                                           xg[b][:, j, c * P:(c + 1) * P], ident[:, :])
                ins.then_inc(s_gt, 1)

            def hidden(n, turn, u, first_unit=False):
                k, half = u % 2, u // B
                if u % B == 0:
                    pe.wait_ge(s_we[half], turn * 32 + 32)
                pe.wait_ge(s_te, n + 1 + START)
                if not first_unit:
                    pe.wait_ge(s_si, (n - 1) * 2 + START)
                for f in range(F // P):
                    for c in range(C):
                        ins = pe.matmul(PS[:, 2 + 2 * k + f // 2, (f % 2) * CAP:(f % 2 + 1) * CAP],
                                        we1[half][:, c, f * P:(f + 1) * P], xgT[k][:, c, :],
                                        start=(c == 0), stop=(c == C - 1))
                    if f % 2:
                        ins.then_inc(s_h, 1)

            def expert_out(i, u):
                k, half = u % 2, u // B
                pe.wait_ge(s_si, i * UNITS * 2 + 2 * u + 2 + START)
                pe.wait_ge(s_ye, i * UNITS + u - 1 + START)
                for j in range(2):
                    for f in range(F // P):
                        ins = pe.matmul(PS[:, 6 + k, j * D:(j + 1) * D], hT[k][:, f, j * P:(j + 1) * P],
                                        we2[half][:, f, :], start=(f == 0), stop=(f == F // P - 1))
                ins.then_inc(s_y, 1)

            def experts(i, last):
                for u in range(UNITS):
                    n = i * UNITS + u
                    half, b = divmod(u, B)
                    if not (last and u + 2 >= UNITS):
                        turn_rows(n + 2, i * 2 + (u + 2) // B, (u + 2) % B)
                    if not (last and u + 1 >= UNITS):
                        hidden(n + 1, i + (u + 1) // UNITS, (u + 1) % UNITS)
                    if not last:
                        pick(n + 2 * B, i * 2 + half + 2, b)
                    expert_out(i, u)

            for e in range(2):
                for b in range(B):
                    pick(e * B + b, e, b)
            turn_rows(0, 0, 0)
            turn_rows(1, 0, 1)
            hidden(0, 0, 0, True)
            with pe.Fori(0, E // 2 - 1) as i:
                experts(i, False)
            experts(E // 2 - 1, True)


def host_arrays(i):
    pos = np.arange(S, dtype=np.float32)[:, None]
    theta = (np.float32(10000.0) ** (np.float32(-2.0) * np.arange(D // 2, dtype=np.float32))
             / np.float32(D // 2)).astype(np.float32)
    r = pos * theta[None, :]
    order = np.concatenate([np.arange(0, D, 2), np.arange(1, D, 2)])
    col = lambda v: np.asarray(v).reshape(-1, P).T
    g = {k: np.asarray(v) for k, v in i.items()}
    at = lambda n: g["L0_attn_" + n]
    xa = lambda n: g["L0_xattn_" + n]
    bias_columns = np.concatenate([col(at("Wd_q_b")), col(at("Wd_kv_b")),
                                   col(at("Wu_q_b")[order]), col(at("Wq_r_b")[order]),
                                   col(at("Wu_k_b")[order]), col(at("Wk_r_b")[order]),
                                   col(xa("b1")), col(xa("b0"))], axis=1)
    out = {
        "x": g["x"].reshape(B * S, D), "ctx": g["ctx_1024"].reshape(B * SK, D),
        "mask": g["mask_BxSxS2_if1"].reshape(B * S, SK),
        "bias_columns": bias_columns,
        "bias_rows": np.stack([at("Wu_v_b"), at("Wo_b"), xa("b2"), xa("b3")])[None],
        "cos": np.cos(r).T, "sin": np.sin(r).T,
        "Wd_q": at("Wd_q_w"), "Wd_kv": at("Wd_kv_w"), "Wu_q": at("Wu_q_w")[:, order],
        "Wq_r": at("Wq_r_w")[:, order], "Wu_k": at("Wu_k_w")[:, order], "Wu_v": at("Wu_v_w"),
        "Wk_r": at("Wk_r_w")[:, order], "Wo": at("Wo_w"),
        "W0T": xa("W0").T, "W1T": xa("W1").T, "W2T": xa("W2").T, "W3T": xa("W3").T,
        "choiceT": g["L0_ffn_choice_w"].T,
        "w1": g["L0_ffn_w1"], "w2": g["L0_ffn_w2"],
    }
    return {k: np.ascontiguousarray(v) for k, v in out.items()}


def kernel(**inputs):
    import concourse.bacc as _bacc
    from concourse.bass_utils import run_bass_kernel_spmd as _run

    arrays = host_arrays(inputs)
    nc = _bacc.Bacc("TRN2", target_bir_lowering=False, num_devices=1)
    args = {n: nc.dram_tensor(f"in_{n}", v.shape, mybir.dt.from_np(v.dtype), kind="ExternalInput").ap()
            for n, v in arrays.items()}
    out = nc.dram_tensor("out", (B * S, D), F32, kind="ExternalOutput").ap()
    decoder_block(nc, args, out)
    r = _run(nc, [{f"in_{n}": v for n, v in arrays.items()}], core_ids=[0])
    return r.results[0]["out"].reshape(B, S, D)
```
